# Optimizing a Trainium2 kernel written in Bass

```python
import numpy as np
import jax
import jax.numpy as jnp

def _softmax(x, axis=-1):
    return jax.nn.softmax(x, axis=axis)

def _gelu(x):
    return jax.nn.gelu(x, approximate=True)

def _silu(x):
    return jax.nn.silu(x)

def _sigmoid(x):
    return jax.nn.sigmoid(x)

def _layernorm(x, axis=-1, eps=1e-05):
    m = jnp.mean(x, axis=axis, keepdims=True)
    v = jnp.var(x, axis=axis, keepdims=True)
    return (x - m) / jnp.sqrt(v + eps)

def _scatter_add(tgt, idx, src, axis=0):
    return tgt.at[idx].add(src)

def _segment_sum(src, seg, n):
    return jax.ops.segment_sum(src, seg, n)
kernel_name = 'mk_seq_postln_d2_jaxref_r8_9ca7a5'

def setup_inputs(seed: int=0):
    np.random.seed(seed)
    _w = jnp.asarray

    def _L0_attn_setup():
        import jax, jax.numpy as jnp
        import numpy as np
        NUM_HEADS = 16
        WINDOW = 32
        LN_EPS = 1e-05
        key = jax.random.key(seed)
        k1, k2, k3 = jax.random.split(key, 3)
        B, L, D = (2, 256, 128)
        x = jax.random.normal(k1, (B, L, D), dtype=jnp.float32)
        w_qkv = jax.random.normal(k2, (3 * D, D), dtype=jnp.float32) * 0.02
        w_out = jax.random.normal(k3, (D, D), dtype=jnp.float32) * 0.02
        gamma = jnp.ones((D,), dtype=jnp.float32)
        beta = jnp.zeros((D,), dtype=jnp.float32)
        return {'x': x, 'w_qkv': w_qkv, 'w_out': w_out, 'gamma': gamma, 'beta': beta}
    _L0_attn_in = _L0_attn_setup()

    def _L0_ffn_setup():
        import jax, jax.numpy as jnp
        import numpy as np
        B, L, D = (4, 64, 128)
        E, TOP_K = (16, 4)
        F = 4 * D
        key = jax.random.key(seed)
        ks = jax.random.split(key, 6)
        scale = 0.02
        return {'x': jax.random.normal(ks[0], (B, L, D), jnp.float32), 'keys': jax.random.normal(ks[1], (E, D), jnp.float32), 'w1': jax.random.normal(ks[2], (E, F, D), jnp.float32) * scale, 'b1': jnp.zeros((E, F), jnp.float32), 'w2': jax.random.normal(ks[3], (E, D, F), jnp.float32) * scale, 'b2': jnp.zeros((E, D), jnp.float32), 'rw': jax.random.normal(ks[4], (E, D), jnp.float32) * scale, 'rb': jnp.zeros((E,), jnp.float32)}
    _L0_ffn_in = _L0_ffn_setup()

    def _L1_attn_setup():
        import jax, jax.numpy as jnp
        import numpy as np
        B, T, D, C = (4, 1024, 128, 64)
        key = jax.random.key(seed)
        k1, k2, k3 = jax.random.split(key, 3)
        out = jax.random.normal(k1, (B, T, D), jnp.float32)
        W_write = jax.random.normal(k2, (D, D), jnp.float32) / np.float32(np.sqrt(D))
        W_read = jax.random.normal(k3, (D, D), jnp.float32) / np.float32(np.sqrt(D))
        decay = jnp.float32(4.6)
        log_alpha = jnp.log(jnp.float32(0.03))
        return {'out': out, 'W_write': W_write, 'W_read': W_read, 'decay': decay, 'log_alpha': log_alpha}
    _L1_attn_in = _L1_attn_setup()

    def _L1_ffn_setup():
        import jax, jax.numpy as jnp
        import numpy as np
        D_MODEL = 128
        HIDDEN = 512
        NUM_EXPERTS = 8
        TOP_K = 2
        DEPTH = 12
        DEPTH_SCALE = 1.0 / np.sqrt(DEPTH)
        key = jax.random.key(seed)
        k_x, k_r, k_g, k_u, k_d = jax.random.split(key, 5)
        s_in = 1.0 / np.sqrt(D_MODEL)
        s_hid = 1.0 / np.sqrt(HIDDEN)
        return {'x': jax.random.normal(k_x, (2, 256, D_MODEL), dtype=jnp.float32), 'Wr': jax.random.normal(k_r, (D_MODEL, NUM_EXPERTS), dtype=jnp.float32) * s_in, 'Wg': jax.random.normal(k_g, (NUM_EXPERTS, D_MODEL, HIDDEN), dtype=jnp.float32) * s_in, 'Wu': jax.random.normal(k_u, (NUM_EXPERTS, D_MODEL, HIDDEN), dtype=jnp.float32) * s_in, 'Wd': jax.random.normal(k_d, (NUM_EXPERTS, HIDDEN, D_MODEL), dtype=jnp.float32) * s_hid}
    _L1_ffn_in = _L1_ffn_setup()
    _d = {'L0_attn_x': _L0_attn_in['x'], 'L0_attn_w_qkv': _L0_attn_in['w_qkv'], 'L0_attn_w_out': _L0_attn_in['w_out'], 'L0_attn_gamma': _L0_attn_in['gamma'], 'L0_attn_beta': _L0_attn_in['beta'], 'L0_ffn_keys': _L0_ffn_in['keys'], 'L0_ffn_w1': _L0_ffn_in['w1'], 'L0_ffn_b1': _L0_ffn_in['b1'], 'L0_ffn_w2': _L0_ffn_in['w2'], 'L0_ffn_b2': _L0_ffn_in['b2'], 'L0_ffn_rw': _L0_ffn_in['rw'], 'L0_ffn_rb': _L0_ffn_in['rb'], 'L1_attn_W_write': _L1_attn_in['W_write'], 'L1_attn_W_read': _L1_attn_in['W_read'], 'L1_attn_decay': _L1_attn_in['decay'], 'L1_attn_log_alpha': _L1_attn_in['log_alpha'], 'L1_ffn_Wr': _L1_ffn_in['Wr'], 'L1_ffn_Wg': _L1_ffn_in['Wg'], 'L1_ffn_Wu': _L1_ffn_in['Wu'], 'L1_ffn_Wd': _L1_ffn_in['Wd']}
    _x0 = _d['L0_attn_x']
    _d['L0_attn_x'] = jax.random.normal(jax.random.fold_in(jax.random.key(seed), 1), (8, 512, 128), dtype=_x0.dtype)
    del _x0
    return _d

def reference(L0_attn_x, L0_attn_w_qkv, L0_attn_w_out, L0_attn_gamma, L0_attn_beta, L0_ffn_keys, L0_ffn_w1, L0_ffn_b1, L0_ffn_w2, L0_ffn_b2, L0_ffn_rw, L0_ffn_rb, L1_attn_W_write, L1_attn_W_read, L1_attn_decay, L1_attn_log_alpha, L1_ffn_Wr, L1_ffn_Wg, L1_ffn_Wu, L1_ffn_Wd):

    def _L0_attn_ref(x, w_qkv, w_out, gamma, beta):
        import jax, jax.numpy as jnp
        import numpy as np
        NUM_HEADS = 16
        WINDOW = 32
        LN_EPS = 1e-05
        B, L, D = x.shape
        H = NUM_HEADS
        HD = D // H
        residual = x
        mu = jnp.mean(x, axis=-1, keepdims=True)
        var = jnp.mean(jnp.square(x - mu), axis=-1, keepdims=True)
        xn = (x - mu) * jax.lax.rsqrt(var + LN_EPS) * gamma + beta
        qkv = jnp.einsum('bld,ed->ble', xn, w_qkv).reshape(B, L, 3, H, HD)
        qkv = jnp.transpose(qkv, (2, 0, 3, 1, 4))
        q, k, v = (qkv[0], qkv[1], qkv[2])
        scores = jnp.einsum('bhqd,bhkd->bhqk', q, k) / jnp.sqrt(jnp.float32(HD))
        idx = jnp.arange(L)
        band = jnp.abs(idx[:, None] - idx[None, :]) <= WINDOW // 2
        scores = jnp.where(band[None, None], scores, -jnp.inf)
        attn = jax.nn.softmax(scores, axis=-1)
        out = jnp.einsum('bhqk,bhkd->bhqd', attn, v)
        out = jnp.transpose(out, (0, 2, 1, 3)).reshape(B, L, D)
        return residual + jnp.einsum('bld,ed->ble', out, w_out)

    def _L0_ffn_ref(x, keys, w1, b1, w2, b2, rw, rb):
        import jax, jax.numpy as jnp
        import numpy as np
        B, L, D = (4, 64, 128)
        E, TOP_K = (16, 4)
        F = 4 * D
        diff = x[:, :, None, :] - keys
        dist2 = jnp.sum(diff * diff, axis=-1)
        logits = -dist2 + jnp.einsum('bld,ed->ble', x, rw) + rb
        topv, topi = jax.lax.top_k(logits, TOP_K)
        w = jax.nn.softmax(topv, axis=-1)
        hidden = jax.nn.gelu(jnp.einsum('bld,efd->blef', x, w1) + b1, approximate=False)
        exp_out = jnp.einsum('blef,edf->bled', hidden, w2) + b2
        sel = jnp.take_along_axis(exp_out, topi[..., None], axis=2)
        fused = jnp.sum(w[..., None] * sel, axis=2)
        return fused

    def _L1_attn_ref(out, W_write, W_read, decay, log_alpha):
        import jax, jax.numpy as jnp
        import numpy as np
        B, T, D, C = (4, 1024, 128, 64)
        Bd, Td, Dd = out.shape
        nC = Td // C
        out32 = out.astype(jnp.float32)
        gamma = jax.nn.sigmoid(decay)
        log_gamma = jnp.log(gamma)
        v = out32 @ W_write.T
        wk = jnp.pad(out32[:, :-1], ((0, 0), (1, 0), (0, 0)))
        rk = out32
        p = jnp.arange(C)
        diffs = jnp.maximum(p[:, None] - 1 - p[None, :], 0)
        causal = (p[:, None] > p[None, :]).astype(jnp.float32)
        M = jnp.exp(diffs * log_gamma) * causal
        dec_inter = gamma ** p
        gw = gamma ** (C - 1 - p)
        gC = gamma ** C

        def chunk(x):
            return x.reshape(Bd, nC, C, Dd).transpose(1, 0, 2, 3)
        rk_c, wk_c, v_c = (chunk(rk), chunk(wk), chunk(v))

        def body(W, xs):
            r, w, vv = xs
            inter = jnp.einsum('bde,bce->bcd', W, r) * dec_inter[None, :, None]
            S = jnp.einsum('bcd,bed->bce', r, w)
            intra = jnp.einsum('bce,bed->bcd', S * M, vv)
            W_new = gC * W + jnp.einsum('bcd,bce->bde', vv * gw[None, :, None], w)
            return (W_new, inter + intra)
        W0 = jnp.zeros((Bd, Dd, Dd), jnp.float32)
        _, reads = jax.lax.scan(body, W0, (rk_c, wk_c, v_c))
        reads = reads.transpose(1, 0, 2, 3).reshape(Bd, Td, Dd)
        alpha = jnp.exp(log_alpha)
        return out + alpha * (reads @ W_read.T).astype(out.dtype)

    def _L1_ffn_ref(x, Wr, Wg, Wu, Wd):
        import jax, jax.numpy as jnp
        import numpy as np
        D_MODEL = 128
        HIDDEN = 512
        NUM_EXPERTS = 8
        TOP_K = 2
        DEPTH = 12
        DEPTH_SCALE = 1.0 / np.sqrt(DEPTH)
        B, T, C = x.shape
        flat_x = x.reshape(-1, C)
        logits = flat_x @ Wr
        top_vals, top_idx = jax.lax.top_k(logits, TOP_K)
        rw = jax.nn.softmax(top_vals.astype(jnp.float32), axis=-1).astype(x.dtype)
        combine = jnp.sum(rw[..., None] * jax.nn.one_hot(top_idx, NUM_EXPERTS, dtype=x.dtype), axis=1)
        g = jnp.einsum('nc,ech->neh', flat_x, Wg)
        u = jnp.einsum('nc,ech->neh', flat_x, Wu)
        h = jax.nn.silu(g) * u
        eo = jnp.einsum('neh,ehc->nec', h, Wd) * DEPTH_SCALE
        out = jnp.einsum('ne,nec->nc', combine, eo)
        return out.reshape(B, T, C)
    x = L0_attn_x
    x = _layernorm(x + _L0_attn_ref(x, L0_attn_w_qkv, L0_attn_w_out, L0_attn_gamma, L0_attn_beta), axis=-1)
    x = _layernorm(x + _L0_ffn_ref(x, L0_ffn_keys, L0_ffn_w1, L0_ffn_b1, L0_ffn_w2, L0_ffn_b2, L0_ffn_rw, L0_ffn_rb), axis=-1)
    x = _layernorm(x + _L1_attn_ref(x, L1_attn_W_write, L1_attn_W_read, L1_attn_decay, L1_attn_log_alpha), axis=-1)
    x = _layernorm(x + _L1_ffn_ref(x, L1_ffn_Wr, L1_ffn_Wg, L1_ffn_Wu, L1_ffn_Wd), axis=-1)
    return x

_drawn_inputs = setup_inputs


def setup_inputs(seed=0):
    import zlib

    import numpy as np

    out = dict(_drawn_inputs(seed))
    spreads = {'L0_attn_gamma': (1.0, 0.6),
     'L0_attn_beta': (0.0, 0.8),
     'L0_ffn_b1': (0.0, 0.271),
     'L0_ffn_b2': (0.0, 0.1),
     'L0_ffn_rb': (0.0, 2.0)}
    factors = {'L0_attn_w_qkv': 5.028, 'L0_attn_w_out': 4.802, 'L0_ffn_rw': 36.12}
    for name, (base, spread) in spreads.items():
        noise = np.random.default_rng([zlib.crc32(name.encode()), seed]).standard_normal(out[name].shape)
        drawn = base * np.exp(spread * noise) if base else spread * noise
        out[name] = jnp.asarray(drawn.astype(out[name].dtype))
    for name, factor in factors.items():
        out[name] = (out[name] * factor).astype(out[name].dtype)
    return out
```

```python
from contextlib import ExitStack

import concourse.bass as bass
from concourse import mybir

F32 = mybir.dt.float32
BF16 = mybir.dt.bfloat16
U32 = mybir.dt.uint32
I32 = mybir.dt.int32
ALU = mybir.AluOpType
ACT = mybir.ActivationFunctionType
AX = mybir.AxisListType.X

P = 128
D = 128
B, L = 8, 512
T = L // P
NT = B * T
H, HD = 16, 8
HALF = 16
G = 4
WIN = [0, 96, 192, 288, 384]
QLO = [0, 112, 208, 304, 400, 512]
NW = len(WIN)
V1 = HD + 1
EPS = 1e-5
NEG = -1.0e30
TILE = 256
S2 = TILE // P
HID = 512
NC_H = HID // P
CH = 512
E0, K0 = 16, 4
E1, K1 = 8, 2
REGION = B * L + TILE
W_COLS = 2 * E0 * HID + 3 * E1 * HID
CHUNKS = W_COLS // CH
CPB = CHUNKS // B
W1_AT, W2_AT = 0, E0 * HID
WG_AT = 2 * E0 * HID
WU_AT = WG_AT + E1 * HID
WD_AT = WU_AT + E1 * HID
SCALE = float(HD) ** -0.5
DEPTH_SCALE = 12.0 ** -0.5
DVE_STEPS = 26
DVE_STEPS_1 = 21
DVE_STEPS_2 = 4


C_IDENT, C_NEG, C_IOTA, C_BASE, C_NHALF, C_ROW, C_STEP = 0, 128, 130, 146, 162, 166, 167
C_NMAT, C_CAUSAL = 183, 183 + L
C_EVEN = C_CAUSAL + L
C_COLS = C_EVEN + 1
CB_IDENT, CB_TRI, CB_ONES, CB_BAND, CB_SEL = 0, 128, 256, 384, 896
CB_COLS = CB_SEL + H * P


def max_tiles(experts, k):
    n = (B * L * k + experts * (TILE - 1)) // TILE
    return n + n % 2


class Chain:

    def __init__(self, eng, sem, base=0):
        self.eng, self.sem, self.base, self.n = eng, sem, base, 0

    def link(self, ins):
        ins.then_inc(self.sem, 1)
        self.n += 1
        self.eng.wait_ge(self.sem, self.base + self.n)
        return ins

    def mark(self, ins):
        ins.then_inc(self.sem, 1)
        self.n += 1
        return self.n

    def wait(self, n):
        self.eng.wait_ge(self.sem, self.base + n)


def bc(ap, axis, n):
    ap = ap.unsqueeze(axis)
    shape = list(ap.shape)
    shape[axis] = n
    return ap.to_broadcast(shape)



def program(nc, x_in, w_all, wq_s, wk_s, wv_t, wo_t, gamma, beta, keys_t, rw_t, rb, b1, b2,
            w_write, w_read_t, decay, log_alpha, wr, const, const_b, out):
    ctx = ExitStack()
    with ctx:
        scope = ctx

        def sb(name, shape, dt=F32):
            return scope.enter_context(nc.sbuf_tensor(name, shape, dt))

        def pb(name):
            return ctx.enter_context(nc.psum_tensor(name, [P, 512], F32))

        def sem(name):
            return ctx.enter_context(nc.semaphore(name))

        cf = sb("cf", [P, C_COLS])
        cb = sb("cb", [P, CB_COLS], BF16)
        ident = cf[:, C_IDENT:C_IDENT + P]
        neg_low = cf[:, C_NEG:C_NEG + 2]
        iota_e = cf[:, C_IOTA:C_IOTA + E0]
        base_e = cf[:, C_BASE:C_BASE + E0]
        nhalf = cf[:, C_NHALF:C_NHALF + T]
        ident_b = cb[:, CB_IDENT:CB_IDENT + P]
        tri = cb[:, CB_TRI:CB_TRI + P]
        ones_b = cb[:, CB_ONES:CB_ONES + P]
        band4 = cb[:, CB_BAND:CB_BAND + 4 * P]
        sel = cb[0:48, CB_SEL:CB_SEL + H * P].rearrange("p (c k) -> p c k", c=H)
        row_no = cf[:, C_ROW:C_ROW + 1]
        steps = cf[:, C_STEP:C_STEP + E0]
        nmat = cf[:, C_NMAT:C_NMAT + L]
        even = cf[:, C_EVEN:C_EVEN + 1]
        causal = cf[:, C_CAUSAL:C_CAUSAL + L]
        w_hi = sb("w_hi", [P, W_COLS], BF16)
        w_lo = sb("w_lo", [P, W_COLS], BF16)
        w_raw = sb("w_raw", [P, 2, CH])
        wqs = sb("wqs", [P, 512])
        wks = sb("wks", [P, 512])
        wv = sb("wv", [P, P])
        wo = sb("wo", [P, P])
        gb = sb("gb", [P, 2])
        keys_sb = sb("keys_sb", [P, 2, E0])
        keys2 = sb("keys2", [P, E0])
        ones_f = sb("ones_f", [P, P])
        g_route = sb("g_route", [P, E0])
        rb_sb = sb("rb_sb", [P, E0])
        c_route = sb("c_route", [P, E0])

        b1_sb = sb("b1_sb", [P, E0 * NC_H])
        wr_sb = sb("wr_sb", [P, E1])
        ww_sb = sb("ww_sb", [P, 2, D])
        dec = sb("dec", [P, 2])
        dexp = sb("dexp", [P, 1])
        dlog = sb("dlog", [P, 1])
        alpha = sb("alpha", [P, 1])
        wc = sb("wc", [P, D])
        zeros = sb("zeros", [P, S2 * D])

        xres = sb("xres", [P, NT, D])
        sres = [sb("sres0", [P, NT, K0]), sb("sres1", [P, NT, K1])]
        eres = [sb("eres0", [P, NT, K0]), sb("eres1", [P, NT, K1])]
        gres = [sb("gres0", [P, NT, K0], U32), sb("gres1", [P, NT, K1], U32)]
        wres = sb("wres", [P, NT, K0])
        carry = [sb("carry0", [P, E0]), sb("carry1", [P, E1])]
        carry_b = [sb("carry0_b", [P, E0], BF16), sb("carry1_b", [P, E1], BF16)]
        y = sb("y", [P, T, D])
        stat2 = sb("stat2", [P, T, 6])
        mv2 = sb("mv2", [P, T, 2])
        ve2 = sb("ve2", [P, T])
        rstd2 = sb("rstd2", [P, T])
        x1w = sb("x1w", [P, 2, T, D])
        x1_t = sb("x1_t", [P, L])
        lg = sb("lg", [P, T, E0])
        mx8 = sb("mx8", [P, T, 8])
        ix8 = sb("ix8", [P, T, 8], U32)
        dtop = sb("dtop", [P, T, K0])
        etop = sb("etop", [P, T, K0])
        ssum = sb("ssum", [P, T])
        rsum = sb("rsum", [P, T])
        idf = sb("idf", [P, T, K0])
        oneh = sb("oneh", [P, T, K0, E0])
        mask = sb("mask", [P, T, E0], BF16)
        msum = sb("msum", [P, E0])
        r2 = sb("r2", [P, T, E0])
        pr = sb("pr", [P, T, K0, E0])
        slf = sb("slf", [P, T * K0])
        sidx = sb("sidx", [P, 2, T * K0], U32)
        cnt = sb("cnt", [P, E0])
        over = sb("over", [P, E0, E0])
        ntile = sb("ntile", [P, E0])
        ntile_sum = sb("ntile_sum", [P, E0])
        past = sb("past", [P, E0])
        past_n = sb("past_n", [P, E0])
        tile_e = sb("tile_e", [P, 8])
        shift = sb("shift", [P, E0])
        table = sb("table", [1, 2 * P + 1], I32)
        tails = sb("tails", [1, E0], I32)

        scope = ExitStack()
        stat = sb("stat", [P, T, 6])
        mv = sb("mv", [P, T, 2])
        ve = sb("ve", [P, T])
        rstd = sb("rstd", [P, T])
        xh = sb("xh", [P, T, D])
        xn_t = sb("xn_t", [P, L])
        hi16 = sb("hi16", [P, 2, L], BF16)
        qst = sb("qst", [P, 2, G, L], BF16)
        kst = sb("kst", [P, 2, G, L], BF16)
        v1 = sb("v1", [P, 2, NW, H, V1])
        nm = sb("nm", [P, H])
        nm_t = sb("nm_t", [48, P], BF16)
        prob = sb("prob", [P, G, 4 * P])
        rden = sb("rden", [P, G, 4])
        ao = sb("ao", [P, D])
        ao_t = sb("ao_t", [P, L])
        scope.close()

        scope = ExitStack()
        choice = sb("choice", [P, NT * K0, E0])
        xg = sb("xg", [P, 2, S2, D])
        xt_hi = sb("xt_hi", [P, 2, TILE], BF16)
        xt_lo = sb("xt_lo", [P, 2, TILE], BF16)
        act_out = sb("act_out", [P, NC_H, TILE])
        hid = sb("hid", [P, NC_H, TILE])
        h_hi = sb("h_hi", [P, 2, NC_H, TILE], BF16)
        h_lo = sb("h_lo", [P, 2, NC_H, TILE], BF16)
        ysb = sb("ysb", [P, 2, S2, D])
        b2_sb = sb("b2_sb", [P, E0, D])
        scope.close()

        scope = ExitStack()
        gat = sb("gat", [P, 2, T, K0, D])
        gidx = sb("gidx", [P, 2, T * K0], U32)
        wsel = sb("wsel", [P, T, K0])
        x2w = sb("x2w", [P, T, D])
        x2_t = sb("x2_t", [P, L + 1])
        vv = sb("vv", [P, T, D])
        pm = sb("pm", [P, T, L])
        decay_m = sb("decay_m", [P, L])
        ow = sb("ow", [P, 2, T, D])
        scope.close()

        s_bank = [pb("s0"), pb("s1")]
        t_bank = [pb("t0"), pb("t1")]
        avbank = pb("avbank")
        proj = [pb("proj0"), pb("proj1")]
        xbank = pb("xbank")
        av = avbank[:, 0:H * V1].rearrange("p (i t v) -> p i t v", i=G, t=4)
        rt_lg = xbank[:, 64:64 + T * E0].rearrange("p (t e) -> p t e", t=T)
        nm_ps = xbank[0:H, 256:384]
        ao_ps = xbank[:, 384:512]
        rank_ps = xbank[:, 0:T * E0].rearrange("p (t e) -> p t e", t=T)

        xt_bank, h_bank, y_bank = xbank, s_bank + t_bank, [avbank, proj[0]]
        v_bank, ws_bank, r_bank = avbank, t_bank, proj[0]

        tiles = [max_tiles(E0, K0), max_tiles(E1, K1)]
        experts = [E0, E1]
        top = [K0, K1]
        xs = [nc.dram_tensor(f"xs{n}", [experts[n] * REGION, D], F32).ap() for n in range(2)]
        ys = [nc.dram_tensor(f"ys{n}", [(tiles[n] + 2) * TILE, D], F32).ap() for n in range(2)]

        (loaded, hi_done, lo_done, pool_step, dve_step, routes_ready, init_done, var_ready, rstd_ready,
         xhat_ready, xhat_turned, xn_ready, proj_ready, half_ready, stack_ready, v_ready, v_copied,
         s_ready, max_done, nm_ready, nm_split, st_ready, exp_done, av_ready, ao_ready, ao_turned,
         ao_copied, o_ready, y_ready, var2_ready, rstd2_ready, x1_ready, x1_turned, x1_copied, x1_kept,
         stored, keys_ready, wc_ready, gamma_ready, decay_ready, expd_ready,
         y2_ready, var3_ready, rstd3_ready, x2_ready, x2_turned, x2_copied, vv_ready, vv_copied,
         ws_ready, decayed, reads_ready, y3_ready, comb_done, out_ready, yf_ready, dlog_ready) = [
            sem(n) for n in (
                "loaded hi_done lo_done pool_step dve_step routes_ready init_done var_ready rstd_ready "
                "xhat_ready xhat_turned xn_ready proj_ready half_ready stack_ready v_ready v_copied "
                "s_ready max_done nm_ready nm_split st_ready exp_done av_ready ao_ready ao_turned "
                "ao_copied o_ready y_ready var2_ready rstd2_ready x1_ready x1_turned x1_copied x1_kept "
                "stored keys_ready wc_ready gamma_ready decay_ready expd_ready "
                "y2_ready var3_ready rstd3_ready x2_ready x2_turned x2_copied vv_ready vv_copied "
                "ws_ready decayed reads_ready y3_ready comb_done out_ready yf_ready dlog_ready").split()]

        def pair_of(name):
            return [sem(name + "0"), sem(name + "1")]

        (lg_ready, d_ready, e_ready, mask_ready, rank_ready, rank_used, slots_ready, carry_ready, cnt_ready,
         table_ready, table_turned, table_kept, tails_ready, tails_stored, g_turned, xhi_done, xlo_done,
         h_ready, act_done, split_done, yp_ready, y_done, tile_step, rows_ready) = [
            pair_of(n) for n in (
                "lg_ready d_ready e_ready mask_ready rank_ready rank_used slots_ready carry_ready cnt_ready "
                "table_ready table_turned table_kept tails_ready tails_stored g_turned xhi_done xlo_done "
                "h_ready act_done split_done yp_ready y_done tile_step rows_ready").split()]
        xg_loaded = [pair_of("xg_loaded0_"), pair_of("xg_loaded1_")]
        y_stored = [pair_of("y_stored0_"), pair_of("y_stored1_")]
        gathered = [pair_of("gathered0_"), pair_of("gathered1_")]
        scattered1 = pair_of("scattered1_")
        o_stored = pair_of("o_stored")
        raw_in = [sem("raw_in0"), sem("raw_in1")]
        scattered = [sem("scattered0"), sem("scattered1")]

        x_tiles = x_in.rearrange("b (t p) d -> p (b t) d", p=P)

        def tile_rounds(j, par):
            return 8 * (j - par)

        def more_pairs(eng, n):
            return eng.value_load(table[0:1, 2 * P:2 * P + 1], min_val=B * L * top[n] // (2 * TILE) - 1,
                                  max_val=tiles[n] // 2 - 1)

        def over_tiles(eng, n, tile, ch=None, steps=0):
            more = more_pairs(eng, n)
            last_tile = 2 * more + 1

            def one(j, par, first, last):
                if ch:
                    ch.base, ch.n = steps * j, 0
                tile(j, par, first, last)
                assert not ch or ch.n == steps, ch.n
            one(0, 0, True, False)
            with eng.Fori(0, more) as p:
                one(2 * p + 1, 1, False, False)
                one(2 * p + 2, 0, False, False)
            one(last_tile, 1, False, True)
            return last_tile

        def over_batches(eng, body):
            with eng.Fori(0, B // 2 - 1) as i:
                body(2 * i, i, 0, True, True)
                body(2 * i + 1, i, 1, True, True)
            body(B - 2, B // 2 - 1, 0, True, False)
            body(B - 1, B // 2 - 1, 1, False, False)

        LOADS = 18

        def apart(eng):
            eng.nop(nofuse=True)

        block = ctx.enter_context(nc.Block())

        @block.sync
        def _(sp):
            for dst, src in [(xres[:, :, :], x_tiles), (cf[:, :], const), (cb[:, :], const_b), (wqs[:, :], wq_s),
                             (wks[:, :], wk_s), (gb[:, 0:1], gamma), (wv[:, :], wv_t), (wo[:, :], wo_t),
                             (keys_sb[:, 0, :], keys_t), (keys_sb[:, 1, :], rw_t),
                             (rb_sb[:, :], rb.to_broadcast([P, E0])), (gb[:, 1:2], beta),
                             (b1_sb[:, :], b1), (wr_sb[:, :], wr), (ww_sb[:, 0, :], w_write),
                             (ww_sb[:, 1, :], w_read_t), (dec[:, 0:1], decay.to_broadcast([P, 1])),
                             (dec[:, 1:2], log_alpha.to_broadcast([P, 1]))]:
                sp.dma_start(dst, src).then_inc(loaded, 16)

            with sp.Fori(0, CHUNKS // 2) as c:
                sp.wait_ge(lo_done, 2 * c)
                for k in range(2):
                    sp.dma_start(w_raw[:, k, :], w_all[:, bass.ds((2 * c + k) * CH, CH)]).then_inc(raw_in[k], 16)
            def fill_tails(n):
                sp.wait_ge(tails_ready[n], 1)
                for e in range(experts[n]):
                    row = sp.value_load(tails[0:1, e:e + 1], min_val=e * REGION, max_val=e * REGION + B * L)
                    sp.dma_start(xs[n][bass.ds(row, TILE), :].rearrange("(p s) d -> p (s d)", s=S2),
                                 zeros[:, :]).then_inc(tails_stored[n], 16)
                sp.wait_ge(tails_stored[n], 16 * experts[n])
                for par in range(2):
                    sp.wait_ge((scattered, scattered1)[n][par], 8 * B * T * top[n])

            def expert_tiles(n):
                def load(j, par):
                    row = sp.value_load(table[0:1, bass.ds(P + j, 1)], min_val=0, max_val=experts[n] * REGION - TILE)
                    sp.dma_start(xg[:, par, :, :].rearrange("p s d -> p (s d)"),
                                 xs[n][bass.ds(row, TILE), :].rearrange("(p s) d -> p (s d)", s=S2)
                                 ).then_inc(xg_loaded[n][par], 16)

                def store(j, par):
                    sp.wait_ge(y_done[n], j + 1)
                    sp.dma_start(ys[n][bass.ds(j * TILE, TILE), :].rearrange("(p s) d -> p (s d)", s=S2),
                                 ysb[:, par, :, :].rearrange("p s d -> p (s d)")).then_inc(y_stored[n][par], 16)

                def tile(j, par, first, last):
                    if not last:
                        sp.wait_ge(g_turned[n], j + 1)
                        load(j + 2, par)
                    if not first:
                        store(j - 1, 1 - par)

                sp.wait_ge(table_kept[n], 1)
                load(0, 0)
                load(1, 1)
                store(over_tiles(sp, n, tile), 1)
                with sp.Fori(more_pairs(sp, n) + 1, tiles[n] // 2 + 1) as p:
                    for par in range(2):
                        sp.dma_start(ys[n][bass.ds((2 * p + par) * TILE, TILE), :].rearrange("(p s) d -> p (s d)", s=S2),
                                     zeros[:, :]).then_inc(y_stored[n][par], 16)

            sp.wait_ge(x1_kept, B)
            sp.wait_ge(table_kept[0], 1)
            sp.dma_start(b2_sb[:, :, :].rearrange("p e d -> p (e d)"), b2.to_broadcast([P, E0 * D])).then_inc(loaded, 16)
            fill_tails(0)
            expert_tiles(0)
            fill_tails(1)
            expert_tiles(1)
            for b in range(B):
                sp.wait_ge(out_ready, b + 1)
                sp.dma_start(out[b].rearrange("(t p) d -> p t d", p=P), ow[:, b % 2, :, :]).then_inc(o_stored[b % 2], 16)
            for par in range(2):
                sp.wait_ge(o_stored[par], 8 * B)

        @block.gpsimd
        def _(pool):
            pool.memset(nm_t[:, :], 0.0)
            for n in range(2):
                pool.memset(carry[n][:, :], 0.0)
                pool.memset(carry_b[n][:, :], 0.0)
            pool.memset(zeros[:, :], 0.0)
            pool.memset(ones_f[:, :], 1.0)
            pool.memset(v1[:, :, :, :, HD:V1], 1.0).then_inc(init_done, 1)
            pool.wait_ge(loaded, 16 * LOADS)

            def rstd_of(b):
                pool.wait_ge(var_ready, b + 1)
                pool.tensor_tensor(rstd[:, :], ve[:, :], nhalf, ALU.pow).then_inc(rstd_ready, 1)

            def body(b, i, par, nxt, nxt2):
                for k in range(CPB):
                    if k == 2 and nxt2:
                        rstd_of(b + 2)
                    pool.wait_ge(hi_done, CPB * b + k + 1)
                    at = (b * CPB + k) * CH
                    pool.tensor_tensor(w_lo[:, bass.ds(at, CH)], w_raw[:, (par * CPB + k) % 2, :],
                                       w_hi[:, bass.ds(at, CH)], ALU.subtract).then_inc(lo_done, 1)
                rstd_of_y(b + 1)
                send(0, b, par)

            def rstd_of_y(count):
                pool.wait_ge(var2_ready, count)
                pool.tensor_tensor(rstd2[:, :], ve2[:, :], nhalf, ALU.pow).then_inc(rstd2_ready, 1)

            def send(n, b, par):
                pool.wait_ge(x1_ready, B * n + b + 1)
                apart(pool)
                pool.tensor_copy(xres[:, bass.ds(b * T, T), :], x1w[:, par, :, :]).then_inc(x1_kept, 1)
                pool.wait_ge(x1_kept, B * n + b + 1)
                pool.wait_ge(slots_ready[n], b + 1)
                apart(pool)
                for t in range(T):
                    for k in range(top[n]):
                        at = t * top[n] + k
                        pool.indirect_dma_start(
                            out=xs[n][:, :], out_offset=bass.IndirectOffsetOnAxis(sidx[:, par, at:at + 1], 0),
                            in_=x1w[:, par, t, :], in_offset=None).then_inc((scattered, scattered1)[n][par], 16)

            def gather(n, b, par):
                k_n = top[n]
                apart(pool)
                pool.tensor_copy(gidx[:, par, 0:T * k_n].rearrange("p (t k) -> p t k", t=T),
                                 gres[n][:, bass.ds(b * T, T), :]).then_inc(pool_step, 1)
                pool.wait_ge(pool_step, B * n + b + 1)
                apart(pool)
                for t in range(T):
                    for k in range(k_n):
                        at = t * k_n + k
                        pool.indirect_dma_start(
                            out=gat[:, par, t, k, :], out_offset=None, in_=ys[n][:, :],
                            in_offset=bass.IndirectOffsetOnAxis(gidx[:, par, at:at + 1], 0)).then_inc(gathered[n][par], 16)

            def linear_body(b, i, par, nxt, nxt2):
                if nxt:
                    pool.wait_ge(comb_done, b)
                    gather(0, b + 1, 1 - par)
                rstd_of_y(B + 2 * b + 1)
                rstd_of_y(B + 2 * b + 2)
                send(1, b, par)

            def final_body(b, i, par, nxt, nxt2):
                if nxt:
                    pool.wait_ge(comb_done, B + b)
                    gather(1, b + 1, 1 - par)
                rstd_of_y(3 * B + b + 1)

            def outputs_stored(n):
                pool.wait_ge(table_kept[n], 1)
                more = more_pairs(pool, n)
                for par in range(2):
                    pool.wait_ge(y_stored[n][par], 8 * tiles[n] + 16)
                pool.wait_ge(xg_loaded[n][0], 16 * more + 32)
                pool.wait_ge(rows_ready[n], 1)

            rstd_of(0)
            rstd_of(1)
            over_batches(pool, body)
            outputs_stored(0)
            apart(pool)
            pool.memset(x2_t[:, 0:1], 0.0).then_inc(init_done, 1)
            gather(0, 0, 0)
            over_batches(pool, linear_body)
            outputs_stored(1)
            gather(1, 0, 0)
            over_batches(pool, final_body)

        @block.vector
        def _(dve):
            ch = Chain(dve, dve_step)
            dve.wait_ge(loaded, 16 * LOADS)
            dve.wait_ge(init_done, 1)
            dve.tensor_tensor(keys2[:, :], keys_sb[:, 0, :], keys_sb[:, 0, :], ALU.mult).then_inc(keys_ready, 1)
            dve.scalar_tensor_tensor(out=g_route[:, :], in0=keys_sb[:, 0, :], scalar=2.0, in1=keys_sb[:, 1, :],
                                     op0=ALU.mult, op1=ALU.add)
            dve.wait_ge(routes_ready, 1)
            ch.link(dve.tensor_tensor(c_route[:, :], rb_sb[:, :], rt_lg[:, 0, :], ALU.subtract))

            def stats(src, st, m, v, ready):
                for t in range(T):
                    ins = dve.bn_stats(st[:, t, :], src(t))
                ch.link(ins)
                apart(dve)
                for t in range(T):
                    ins = dve.bn_aggr(m[:, t, :], st[:, t, :])
                ch.link(ins)
                dve.tensor_scalar(v[:, :], m[:, :, 1], EPS, None, ALU.add).then_inc(ready, 1)

            def prep_norm(b):
                stats(lambda t: xres[:, b * T + t, :], stat, mv, ve, var_ready)
                dve.wait_ge(rstd_ready, b + 1)
                dve.wait_ge(xhat_turned, b)
                for t in range(T):
                    ins = dve.tensor_scalar(xh[:, t, :], xres[:, b * T + t, :], mv[:, t, 0:1], rstd[:, t:t + 1],
                                            ALU.subtract, ALU.mult)
                ins.then_inc(xhat_ready, 1)

            def prep_stacks(b, par):
                for j in range(2 * G):
                    dve.wait_ge(half_ready, 2 * G * b + j + 1)
                    dst = (qst if j < G else kst)[:, par, j % G, :]
                    dve.scalar_tensor_tensor(out=dst, in0=hi16[:, j % 2, :], scalar=neg_low[:, j // G:j // G + 1],
                                             in1=proj[(j + 1) % 2][:, :], op0=ALU.mult,
                                             op1=ALU.add).then_inc(stack_ready, 1)

            def maxima(win):
                for i in range(G):
                    dve.wait_ge(s_ready, G * win + i + 1)
                    dve.tensor_reduce(nm[:, 4 * i:4 * i + 4], s_bank[i % 2][:, :].rearrange("p (t k) -> p t k", t=4),
                                      AX.X, ALU.max, negate=True).then_inc(max_done, 1)

            def split_max(win):
                dve.wait_ge(nm_ready, win + 1)
                ch.link(dve.tensor_copy(nm_t[0:H, :], nm_ps))
                dve.tensor_tensor(nm_t[32:32 + H, :], nm_ps, nm_t[0:H, :], ALU.subtract).then_inc(nm_split, 1)

            def divide(win):
                dve.wait_ge(av_ready, win + 1)
                ch.link(dve.reciprocal(rden[:, :, :], av[:, :, :, HD]))
                dve.wait_ge(ao_turned, win)
                dve.tensor_tensor(ao[:, :].rearrange("p (t i d) -> p i t d", t=4, i=G), av[:, :, :, 0:HD],
                                  bc(rden[:, :, :], 3, HD), ALU.mult).then_inc(ao_ready, 1)

            def route(n, b, par):
                e_n, k_n = experts[n], top[n]
                lgv, mk, oh = lg[:, :, 0:e_n], mask[:, :, 0:e_n], oneh[:, :, 0:k_n, 0:e_n]
                dve.wait_ge(lg_ready[n], b + 1)
                if n == 0:
                    ch.link(dve.tensor_tensor(lgv, rt_lg, bc(c_route[:, :], 1, T), ALU.add))
                else:
                    ch.link(dve.tensor_copy(lgv, rt_lg[:, :, 0:e_n]))
                apart(dve)
                for t in range(T):
                    ins = dve.max(mx8[:, t, :], lgv[:, t, :])
                ch.link(ins)
                apart(dve)
                for t in range(T):
                    ins = dve.max_index(ix8[:, t, :], mx8[:, t, :], lgv[:, t, :])
                ch.link(ins)
                dve.tensor_tensor(dtop[:, :, 0:k_n], mx8[:, :, 0:k_n], mx8[:, :, 0:1].to_broadcast([P, T, k_n]),
                                  ALU.subtract).then_inc(d_ready[n], 1)
                ch.link(dve.tensor_copy(idf[:, :, 0:k_n], ix8[:, :, 0:k_n]))
                for k in range(k_n):
                    ins = dve.tensor_tensor(oh[:, :, k, :], bc(iota_e[:, 0:e_n], 1, T),
                                            idf[:, :, k:k + 1].to_broadcast([P, T, e_n]), ALU.is_equal)
                ch.link(ins)
                with nc.allow_low_precision(reason="the sums are 0 or 1"):
                    dve.tensor_reduce(mk, oh.rearrange("p t k e -> p t e k"), AX.X, ALU.add).then_inc(mask_ready[n], 1)
                dve.wait_ge(mask_ready[n], b + 1)
                ch.link(dve.tensor_reduce(msum[:, 0:e_n], mk.rearrange("p t e -> p e t"), AX.X, ALU.add))
                dve.wait_ge(e_ready[n], b + 1)
                ch.link(dve.tensor_reduce(ssum[:, :], etop[:, :, 0:k_n], AX.X, ALU.add))
                ch.link(dve.reciprocal(rsum[:, :], ssum[:, :]))
                if n == 1:
                    ch.link(dve.tensor_scalar(rsum[:, :], rsum[:, :], DEPTH_SCALE, None, ALU.mult))
                dve.tensor_tensor(wres[:, bass.ds(b * T, T), 0:k_n], etop[:, :, 0:k_n], bc(rsum[:, :], 2, k_n), ALU.mult)
                dve.wait_ge(rank_ready[n], b + 1)
                dve.tensor_tensor(r2[:, :, 0:e_n], rank_ps[:, :, 0:e_n], bc(base_e[:, 0:e_n], 1, T),
                                  ALU.add).then_inc(rank_used[n], 1)
                ch.link(dve.tensor_tensor(carry[n][:, :], carry[n][:, :], msum[:, 0:e_n], ALU.add))
                dve.tensor_copy(carry_b[n][:, :], carry[n][:, :]).then_inc(carry_ready[n], 1)
                dve.wait_ge(rank_used[n], b + 1)
                for k in range(k_n):
                    ins = dve.tensor_tensor(pr[:, :, k, 0:e_n], oh[:, :, k, :], r2[:, :, 0:e_n], ALU.mult)
                ch.link(ins)
                ch.link(dve.tensor_reduce(slf[:, 0:T * k_n].rearrange("p (t k) -> p t k", t=T),
                                          pr[:, :, 0:k_n, 0:e_n], AX.X, ALU.add))
                dve.tensor_copy(sidx[:, par, 0:T * k_n], slf[:, 0:T * k_n]).then_inc(slots_ready[n], 1)
                dve.tensor_copy(eres[n][:, bass.ds(b * T, T), :], idf[:, :, 0:k_n])
                ch.link(dve.tensor_copy(sres[n][:, bass.ds(b * T, T), :],
                                        slf[:, 0:T * k_n].rearrange("p (t k) -> p t k", t=T)))

            def tile_table(n):
                e_n = experts[n]
                dve.wait_ge(cnt_ready[n], 1)
                ch.link(dve.tensor_copy(cnt[:, 0:e_n], xbank[:, 0:e_n]))
                dve.tensor_tensor(tails[0:1, 0:e_n], cnt[0:1, 0:e_n], base_e[0:1, 0:e_n], ALU.add).then_inc(tails_ready[n], 1)
                ch.link(dve.tensor_tensor(over[:, 0:e_n, :], cnt[:, 0:e_n].unsqueeze(2).to_broadcast([P, e_n, E0]),
                                          bc(steps, 1, e_n), ALU.is_gt))
                ch.link(dve.tensor_reduce(ntile[:, 0:e_n], over[:, 0:e_n, :], AX.X, ALU.add))
                ch.link(dve.tensor_tensor_scan(ntile_sum[:, 0:e_n], ones_f[:, 0:e_n], ntile[:, 0:e_n], 0.0, ALU.mult, ALU.add))
                ch.link(dve.tensor_scalar(past[:, 0:e_n], ntile_sum[:, 0:e_n], row_no, None, ALU.is_le))
                ch.link(dve.tensor_tensor(past_n[:, 0:e_n], past[:, 0:e_n], ntile[:, 0:e_n], ALU.mult))
                dve.tensor_reduce(tile_e[:, 0:1], past[:, 0:e_n], AX.X, ALU.add)
                ch.link(dve.tensor_reduce(tile_e[:, 1:2], past_n[:, 0:e_n], AX.X, ALU.add))
                dve.tensor_tensor(tile_e[:, 2:3], row_no, tile_e[:, 1:2], ALU.subtract)
                ch.link(dve.tensor_scalar(tile_e[:, 3:4], tile_e[:, 0:1], e_n - 0.5, None, ALU.is_lt))
                ch.link(dve.tensor_scalar(tile_e[:, 2:3], tile_e[:, 2:3], float(TILE), None, ALU.mult))
                ch.link(dve.scalar_tensor_tensor(out=tile_e[:, 2:3], in0=tile_e[:, 0:1], scalar=float(REGION),
                                                 in1=tile_e[:, 2:3], op0=ALU.mult, op1=ALU.add))
                dve.tensor_tensor(tile_e[:, 4:5], tile_e[:, 0:1], tile_e[:, 3:4], ALU.mult)
                dve.tensor_tensor(tile_e[:, 5:6], tile_e[:, 2:3], tile_e[:, 3:4], ALU.mult).then_inc(table_ready[n], 1)
                ch.link(dve.tensor_tensor(shift[:, 0:e_n], ntile_sum[:, 0:e_n], ntile[:, 0:e_n], ALU.subtract))
                ch.link(dve.tensor_scalar(shift[:, 0:e_n], shift[:, 0:e_n], float(TILE), None, ALU.mult))
                ch.link(dve.tensor_tensor(shift[:, 0:e_n], shift[:, 0:e_n], base_e[:, 0:e_n], ALU.subtract))
                dve.wait_ge(table_turned[n], 1)
                dve.tensor_copy(table[0:1, :], xbank[0:1, 0:2 * P + 1]).then_inc(table_kept[n], 1)

            def expert_tiles(n):
                ch = Chain(dve, tile_step[n])

                def lo_of(j, par):
                    dve.wait_ge(xhi_done[n], j + 1)
                    dve.tensor_tensor(xt_lo[:, par, :], xt_bank[:, 0:TILE], xt_hi[:, par, :],
                                      ALU.subtract).then_inc(xlo_done[n], 1)

                def split(j, par, half, src):
                    c = slice(2 * half, 2 * half + 2)
                    ch.link(dve.tensor_copy(h_hi[:, par, c, :], src[:, c, :]))
                    dve.tensor_tensor(h_lo[:, par, c, :], src[:, c, :], h_hi[:, par, c, :],
                                      ALU.subtract).then_inc(split_done[n], 1)

                def take_out(j, par):
                    dve.wait_ge(yp_ready[n], j + 1)
                    dve.wait_ge(y_stored[n][par], tile_rounds(j, par))
                    src = y_bank[par][:, 0:S2 * D].rearrange("p (s d) -> p s d", s=S2)
                    if n == 0:
                        e = dve.value_load(table[0:1, bass.ds(j, 1)], min_val=0, max_val=E0 - 1)
                        ins = dve.tensor_tensor(ysb[:, par, :, :], src,
                                                b2_sb[:, bass.ds(e, 1), :].to_broadcast([P, S2, D]), ALU.add)
                    else:
                        ins = dve.tensor_copy(ysb[:, par, :, :], src)
                    ins.then_inc(y_done[n], 1)

                def tile(j, par, first, last):
                    if not last:
                        lo_of(j + 1, 1 - par)
                    for half in range(2):
                        if n == 0:
                            dve.wait_ge(act_done[n], 2 * j + half + 1)
                            split(j, par, half, act_out)
                        else:
                            for c in range(2 * half, 2 * half + 2):
                                dve.wait_ge(act_done[n], NC_H * j + c + 1)
                                ins = dve.tensor_tensor(hid[:, c, :], act_out[:, c, :], h_bank[c][:, TILE:2 * TILE], ALU.mult)
                                ch.link(ins)
                            split(j, par, half, hid)
                    if not first:
                        take_out(j - 1, 1 - par)

                dve.wait_ge(table_kept[n], 1)
                lo_of(0, 0)
                take_out(over_tiles(dve, n, tile, ch, 2 if n == 0 else 6), 1)

            def output_rows(n):
                e_n, m = experts[n], NT * top[n]
                sel_e = choice[:, 0:m, 0:e_n]
                ch.link(dve.tensor_tensor(sel_e, bc(iota_e[:, 0:e_n], 1, m),
                                          bc(eres[n][:, :, :].rearrange("p t k -> p (t k)"), 2, e_n), ALU.is_equal))
                ch.link(dve.tensor_tensor(sel_e, sel_e, bc(shift[:, 0:e_n], 1, m), ALU.mult))
                rows = eres[n][:, :, :].rearrange("p t k -> p (t k)")
                ch.link(dve.tensor_reduce(rows, sel_e, AX.X, ALU.add))
                ch.link(dve.tensor_tensor(rows, rows, sres[n][:, :, :].rearrange("p t k -> p (t k)"), ALU.add))
                dve.tensor_copy(gres[n][:, :, :].rearrange("p t k -> p (t k)"), rows).then_inc(rows_ready[n], 1)

            def combine(n, b, i, par):
                k_n = top[n]
                ch.link(dve.tensor_copy(wsel[:, :, 0:k_n], wres[:, bass.ds(b * T, T), 0:k_n]))
                dve.wait_ge(gathered[n][par], 16 * T * k_n * (i + 1))
                for k in range(k_n):
                    for t in range(T):
                        before = xres[:, b * T + t, :] if k == 0 else y[:, t, :]
                        ins = dve.scalar_tensor_tensor(out=y[:, t, :], in0=gat[:, par, t, k, :],
                                                       scalar=wsel[:, t, k:k + 1], in1=before,
                                                       op0=ALU.mult, op1=ALU.add)
                    if k < k_n - 1:
                        ch.link(ins)
                ins.then_inc(comb_done, 1)
                dve.wait_ge(comb_done, B * n + b + 1)

            def norm(count, dst, ready):
                stats(lambda t: y[:, t, :], stat2, mv2, ve2, var2_ready)
                dve.wait_ge(rstd2_ready, count)
                for t in range(T):
                    ins = dve.tensor_scalar(dst(t), y[:, t, :], mv2[:, t, 0:1], rstd2[:, t:t + 1],
                                            ALU.subtract, ALU.mult)
                ins.then_inc(ready, 1)

            def linear_body(b, i, par, nxt, nxt2):
                combine(0, b, i, par)
                norm(B + 2 * b + 1, lambda t: x2w[:, t, :], x2_ready)
                for e in range(T):
                    dve.wait_ge(ws_ready, T * b + e + 1)
                    dve.tensor_tensor(pm[:, e, 0:L - e * P], ws_bank[e % 2][:, 0:L - e * P],
                                      decay_m[:, 0:L - e * P], ALU.mult).then_inc(decayed, 1)
                dve.wait_ge(reads_ready, b + 1)
                dve.scalar_tensor_tensor(out=y[:, :, :].rearrange("p t d -> p (t d)"),
                                         in0=x2w[:, :, :].rearrange("p t d -> p (t d)"), scalar=2.0,
                                         in1=r_bank[:, :], op0=ALU.mult, op1=ALU.add).then_inc(y3_ready, 1)
                dve.wait_ge(y3_ready, b + 1)
                dve.wait_ge(scattered1[par], 16 * T * K1 * i)
                norm(B + 2 * b + 2, lambda t: x1w[:, par, t, :], x1_ready)
                route(1, b, par)

            def final_body(b, i, par, nxt, nxt2):
                combine(1, b, i, par)
                dve.wait_ge(o_stored[par], 16 * i)
                norm(3 * B + b + 1, lambda t: ow[:, par, t, :], out_ready)

            def body(b, i, par, nxt, nxt2):
                for w in range(NW):
                    split_max(b * NW + w)
                    if w < NW - 1 or nxt:
                        maxima(b * NW + w + 1)
                    if w == 1 and nxt2:
                        prep_norm(b + 2)
                    divide(b * NW + w)
                dve.wait_ge(o_ready, b + 1)
                dve.scalar_tensor_tensor(out=y[:, :, :].rearrange("p t d -> p (t d)"),
                                         in0=xres[:, bass.ds(b * T, T), :].rearrange("p t d -> p (t d)"), scalar=2.0,
                                         in1=proj[0][:, :], op0=ALU.mult, op1=ALU.add).then_inc(y_ready, 1)
                dve.wait_ge(y_ready, b + 1)
                dve.wait_ge(scattered[par], 16 * T * K0 * i)
                norm(b + 1, lambda t: x1w[:, par, t, :], x1_ready)
                if nxt2:
                    prep_stacks(b + 2, par)
                route(0, b, par)

            prep_norm(0)
            prep_stacks(0, 0)
            prep_norm(1)
            maxima(0)
            prep_stacks(1, 1)

            def counted(body, steps):
                start = ch.base + ch.n

                def one(b, i, par, nxt, nxt2):
                    if nxt:
                        ch.base, ch.n = start + steps * b, 0
                    body(b, i, par, nxt, nxt2)
                    assert not nxt2 or ch.n == steps, ch.n
                return one

            over_batches(dve, counted(body, DVE_STEPS))
            tile_table(0)
            expert_tiles(0)
            output_rows(0)
            dve.wait_ge(expd_ready, 1)
            dve.tensor_tensor(decay_m[:, :], decay_m[:, :], causal, ALU.mult).then_inc(decay_ready, 1)
            dve.wait_ge(decay_ready, 1)
            over_batches(dve, counted(linear_body, DVE_STEPS_1))
            tile_table(1)
            expert_tiles(1)
            output_rows(1)
            over_batches(dve, counted(final_body, DVE_STEPS_2))

        @block.scalar
        def _(act):
            act.wait_ge(loaded, 16 * LOADS)

            def prep(b, par):
                act.wait_ge(xhat_turned, b + 1)
                nc.scalar.activation(xn_t[:, :], xbank[:, :], ACT.Identity, bias=gb[:, 1:2],
                                     scale=gb[:, 0:1]).then_inc(xn_ready, 1)

            def halves(b):
                for j in range(2 * G):
                    act.wait_ge(proj_ready, 2 * G * b + j + 1)
                    nc.scalar.copy(hi16[:, j % 2, :], proj[(j + 1) % 2][:, :]).then_inc(half_ready, 1)

            def values(b, par):
                act.wait_ge(v_ready, 2 * b + 1)
                for w in range(4):
                    ins = nc.scalar.copy(v1[:, par, w, :, 0:HD],
                                         proj[1][:, w * P:w * P + P].rearrange("p (h d) -> p h d", h=H))
                ins.then_inc(v_copied, 1)
                act.wait_ge(v_ready, 2 * b + 2)
                nc.scalar.copy(v1[:, par, 4, :, 0:HD],
                               proj[0][:, 0:P].rearrange("p (h d) -> p h d", h=H)).then_inc(v_copied, 1)

            def keep_turned(win, w):
                lo, hi = QLO[w], QLO[w + 1]
                act.wait_ge(ao_turned, win + 1)
                nc.scalar.copy(ao_t[:, lo:hi], ao_ps[:, lo - WIN[w]:hi - WIN[w]]).then_inc(ao_copied, 1)

            def body(b, i, par, nxt, nxt2):
                done = 0
                for w in range(NW):
                    win = b * NW + w
                    for g in range(G):
                        act.wait_ge(st_ready, G * win + g + 1)
                        nc.scalar.activation(prob[:, g, :], t_bank[g % 2][:, :], ACT.Exp,
                                             scale=SCALE).then_inc(exp_done, 1)
                        if g == 0 and w > 0:
                            keep_turned(win - 1, w - 1)
                    for k in range(done, done + (2 if w < CPB - NW else 1)):
                        act.wait_ge(raw_in[(par * CPB + k) % 2], 16 * (CPB * i + (par * CPB + k) // 2 + 1))
                        nc.scalar.copy(w_hi[:, bass.ds((b * CPB + k) * CH, CH)],
                                       w_raw[:, (par * CPB + k) % 2, :]).then_inc(hi_done, 1)
                        done = k + 1
                if nxt2:
                    prep(b + 2, par)
                keep_turned(b * NW + NW - 1, NW - 1)
                if nxt2:
                    halves(b + 2)
                act.wait_ge(x1_turned, b + 1)
                nc.scalar.copy(x1_t[:, :], xbank[:, :]).then_inc(x1_copied, 1)
                if nxt2:
                    values(b + 2, par)
                route(0, b)

            def route(n, b):
                act.wait_ge(d_ready[n], b + 1)
                nc.scalar.activation(etop[:, :, 0:top[n]], dtop[:, :, 0:top[n]], ACT.Exp).then_inc(e_ready[n], 1)

            def expert_tiles(n):
                def hi_of(j, par):
                    act.wait_ge(g_turned[n], j + 1)
                    nc.scalar.copy(xt_hi[:, par, :], xt_bank[:, 0:TILE]).then_inc(xhi_done[n], 1)

                def tile(j, par, first, last):
                    if not last:
                        hi_of(j + 1, 1 - par)
                    if n == 0:
                        e = act.value_load(table[0:1, bass.ds(j, 1)], min_val=0, max_val=E0 - 1)
                    act.wait_ge(split_done[n], 2 * j)
                    for c in range(NC_H):
                        if n == 0:
                            if c % 2 == 0:
                                act.wait_ge(h_ready[n], 2 * j + c // 2 + 1)
                            ins = nc.scalar.activation(
                                act_out[:, c, :], h_bank[2 * par + c // 2][:, (c % 2) * TILE:(c % 2 + 1) * TILE],
                                ACT.Gelu, bias=b1_sb[:, bass.ds(e * NC_H + c, 1)])
                            if c % 2 == 1:
                                ins.then_inc(act_done[n], 1)
                        else:
                            act.wait_ge(h_ready[n], NC_H * j + c + 1)
                            nc.scalar.activation(act_out[:, c, :], h_bank[c][:, 0:TILE],
                                                 ACT.Silu).then_inc(act_done[n], 1)

                act.wait_ge(table_kept[n], 1)
                hi_of(0, 0)
                over_tiles(act, n, tile)

            def linear_body(b, i, par, nxt, nxt2):
                act.wait_ge(x2_turned, b + 1)
                nc.scalar.copy(x2_t[:, 1:L + 1], xbank[:, :]).then_inc(x2_copied, 1)
                act.wait_ge(vv_ready, b + 1)
                nc.scalar.copy(vv[:, :, :].rearrange("p t d -> p (t d)"), v_bank[:, :]).then_inc(vv_copied, 1)
                act.wait_ge(x1_turned, B + b + 1)
                nc.scalar.copy(x1_t[:, :], xbank[:, :]).then_inc(x1_copied, 1)
                route(1, b)

            nc.scalar.activation(dexp[:, :], dec[:, 0:1], ACT.Exp, scale=-1.0).then_inc(gamma_ready, 1)
            nc.scalar.activation(alpha[:, :], dec[:, 1:2], ACT.Exp).then_inc(gamma_ready, 1)
            act.wait_ge(gamma_ready, 2)
            nc.scalar.activation(dlog[:, :], dexp[:, :], ACT.Ln, bias=1.0).then_inc(dlog_ready, 1)
            act.wait_ge(wc_ready, 1)
            nc.scalar.activation(wc[:, :], avbank[:, 0:D], ACT.Identity, scale=alpha[:, 0:1])
            act.wait_ge(init_done, 1)
            for b in range(2):
                prep(b, b)
                halves(b)
                values(b, b)
            over_batches(act, body)
            expert_tiles(0)
            act.wait_ge(dlog_ready, 1)
            act.wait_ge(init_done, 2)
            nc.scalar.activation(decay_m[:, :], nmat, ACT.Exp, scale=dlog[:, 0:1]).then_inc(expd_ready, 1)
            over_batches(act, linear_body)
            expert_tiles(1)

        @block.tensor
        def _(pe):
            pe.wait_ge(loaded, 16 * LOADS)
            pe.wait_ge(keys_ready, 1)
            pe.wait_ge(init_done, 1)
            pe.matmul(rt_lg[:, 0, :], ones_f[:, :], keys2[:, :], start=True, stop=True).then_inc(routes_ready, 1)
            pe.matmul(avbank[:, 0:D], ww_sb[:, 0, :], ww_sb[:, 1, :], start=True, stop=True).then_inc(wc_ready, 1)

            def turn(b):
                pe.wait_ge(xhat_ready, b + 1)
                for t in range(T):
                    ins = pe.transpose(xbank[:, t * P:(t + 1) * P], xh[:, t, :], ident)
                ins.then_inc(xhat_turned, 1)

            def stacks(b, j):
                src = (wqs if j < G else wks)[:, (j % G) * P:(j % G + 1) * P]
                pe.matmul(proj[(j + 1) % 2][:, :], src, xn_t[:, :], start=True, stop=True).then_inc(proj_ready, 1)

            def values(b):
                pe.wait_ge(stack_ready, 2 * G * b + 7)
                for w in range(4):
                    ins = pe.matmul(proj[1][:, w * P:(w + 1) * P], xn_t[:, WIN[w]:WIN[w] + P], wv[:, :],
                                    start=True, stop=True)
                ins.then_inc(v_ready, 1)
                pe.wait_ge(stack_ready, 2 * G * b + 8)
                pe.matmul(proj[0][:, 0:P], xn_t[:, WIN[4]:WIN[4] + P], wv[:, :], start=True,
                          stop=True).then_inc(v_ready, 1)

            def scores(win, w, par, g, first=False):
                if not first or g >= 2:
                    pe.wait_ge(max_done, G * win + g - 1)
                bank, rows, at = s_bank[g % 2], slice(32 * g, 32 * g + 32), slice(WIN[w], WIN[w] + P)
                pe.matmul(bank[:, :], ident_b, band4, start=True, stop=True)
                for t in range(4):
                    ins = pe.matmul(bank[:, t * P:(t + 1) * P], qst[rows, par, t, at], kst[rows, par, t, at],
                                    start=False, stop=True, skip_group_check=True)
                ins.then_inc(s_ready, 1)

            def scores_t(win, w, par, g):
                if g >= 2:
                    pe.wait_ge(exp_done, G * win + g - 1)
                bank, rows, at = t_bank[g % 2], slice(32 * g, 32 * g + 32), slice(WIN[w], WIN[w] + P)
                pe.matmul(bank[:, :], ident_b, band4, start=True, stop=True)
                for t in range(4):
                    pe.matmul(bank[:, t * P:(t + 1) * P], kst[rows, par, t, at], qst[rows, par, t, at],
                              start=False, stop=False, skip_group_check=True)
                for t in range(4):
                    ins = pe.matmul(bank[:, t * P:(t + 1) * P], sel[:, 4 * g + t, :], nm_t[:, :],
                                    start=False, stop=True, skip_group_check=True)
                ins.then_inc(st_ready, 1)

            def weighted(win, w, par, g):
                pe.wait_ge(exp_done, G * win + g + 1)
                for t in range(4):
                    ins = pe.matmul(av[:, g, t, :], prob[:, g, t * P:(t + 1) * P], v1[:, par, w, 4 * t + g, :],
                                    start=True, stop=True)
                if g == G - 1:
                    ins.then_inc(av_ready, 1)

            def turn_out(win):
                pe.wait_ge(ao_ready, win + 1)
                pe.wait_ge(ao_copied, win)
                pe.transpose(ao_ps, ao[:, :], ident).then_inc(ao_turned, 1)

            def body(b, i, par, nxt, nxt2):
                for w in range(NW):
                    win = b * NW + w
                    pe.wait_ge(max_done, G * (win + 1))
                    if w == 0:
                        pe.wait_ge(rank_used[0], b)
                    else:
                        pe.wait_ge(ao_copied, win - 1)
                    pe.transpose(nm_ps, nm[:, :], ident).then_inc(nm_ready, 1)
                    after = None
                    if w < NW - 1:
                        after = lambda g: scores(win + 1, w + 1, par, g)
                    elif nxt:
                        pe.wait_ge(stack_ready, 2 * G * (b + 2))
                        after = lambda g: scores(win + 1, 0, 1 - par, g)
                    if after:
                        after(0)
                        after(1)
                    pe.wait_ge(nm_split, win + 1)
                    scores_t(win, w, par, 0)
                    if w > 0:
                        turn_out(win - 1)
                    if after:
                        after(2)
                    scores_t(win, w, par, 1)
                    if w == 0:
                        pe.wait_ge(v_copied, 2 * (b + 1))
                    pe.wait_ge(ao_ready, win)
                    weighted(win, w, par, 0)
                    if after:
                        after(3)
                    scores_t(win, w, par, 2)
                    weighted(win, w, par, 1)
                    scores_t(win, w, par, 3)
                    weighted(win, w, par, 2)
                    weighted(win, w, par, 3)
                if nxt2:
                    pe.wait_ge(ao_copied, NW * b + NW - 1)
                    turn(b + 2)
                    pe.wait_ge(xn_ready, b + 3)
                turn_out(b * NW + NW - 1)
                pe.wait_ge(v_copied, 2 * (b + 2) if nxt else 2 * B)
                pe.wait_ge(ao_copied, NW * (b + 1))
                for t in range(T):
                    ins = pe.matmul(proj[0][:, t * P:(t + 1) * P], ao_t[:, t * P:(t + 1) * P], wo[:, :],
                                    start=True, stop=True)
                ins.then_inc(o_ready, 1)
                if nxt2:
                    for j in range(2 * G):
                        if j == 1:
                            pe.wait_ge(y_ready, b + 1)
                        if j >= 2:
                            pe.wait_ge(stack_ready, 2 * G * (b + 2) + j - 1)
                        stacks(b + 2, j)
                turn_x1(b + 1, par)
                if nxt2:
                    values(b + 2)
                route(0, b)

            def turn_x1(count, par):
                pe.wait_ge(x1_ready, count)
                for t in range(T):
                    ins = pe.transpose(xbank[:, t * P:(t + 1) * P], x1w[:, par, t, :], ident)
                ins.then_inc(x1_turned, 1)

            def route(n, b):
                e_n = experts[n]
                pe.wait_ge(x1_copied, B * n + b + 1)
                for t in range(T):
                    ins = pe.matmul(rt_lg[:, t, 0:e_n], x1_t[:, t * P:(t + 1) * P], (g_route, wr_sb)[n][:, :],
                                    start=True, stop=True)
                ins.then_inc(lg_ready[n], 1)
                pe.wait_ge(mask_ready[n], b + 1)
                ranks, mk = rank_ps[:, :, 0:e_n], mask[:, :, 0:e_n]
                pe.matmul(ranks, tri, mk, start=True, stop=True)
                for t in range(T - 1):
                    pe.matmul(ranks[:, t + 1:T, :], ones_b, bc(mk[:, t, :], 1, T - 1 - t), start=False,
                              stop=True, skip_group_check=True)
                pe.matmul(ranks, ones_b, bc(carry_b[n][:, :], 1, T), start=False, stop=True,
                          skip_group_check=True).then_inc(rank_ready[n], 1)

            def tile_table(n):
                pe.wait_ge(carry_ready[n], B)
                pe.wait_ge(rank_used[n], B)
                pe.matmul(xbank[:, 0:experts[n]], ones_b, carry_b[n][:, :], start=True, stop=True).then_inc(cnt_ready[n], 1)
                pe.wait_ge(table_ready[n], 1)
                for c in range(2):
                    pe.transpose(xbank[0:1, c * P:(c + 1) * P], tile_e[:, 4 + c:5 + c], ident)
                ins = pe.matmul(xbank[0:1, 2 * P:2 * P + 1], tile_e[:, 3:4], even, start=True, stop=True)
                ins.then_inc(table_turned[n], 1)
                pe.wait_ge(table_kept[n], 1)

            def expert_tiles(n):
                def turn_rows(j, par):
                    pe.wait_ge(xg_loaded[n][par], 8 * (j - par) + 16)
                    pe.wait_ge(xlo_done[n], j)
                    for k in range(S2):
                        ins = pe.transpose(xt_bank[:, k * P:(k + 1) * P], xg[:, par, k, :], ident)
                    ins.then_inc(g_turned[n], 1)

                def hidden_chunk(dst, w_at, e, c, par):
                    at = e * HID + (w_at + c * P)
                    w_h, w_l = w_hi[:, bass.ds(at, P)], w_lo[:, bass.ds(at, P)]
                    pe.matmul(dst, w_h, xt_hi[:, par, :], start=True, stop=False)
                    pe.matmul(dst, w_h, xt_lo[:, par, :], start=False, stop=False)
                    return pe.matmul(dst, w_l, xt_hi[:, par, :], start=False, stop=True)

                def outputs(j, par, e):
                    pe.wait_ge(y_done[n], j)
                    for half in range(2):
                        pe.wait_ge(split_done[n], 2 * j + half + 1)
                        for k in range(S2):
                            dst, rows = y_bank[par][:, k * D:(k + 1) * D], slice(k * P, (k + 1) * P)
                            for c in (2 * half, 2 * half + 1):
                                at = e * HID + ((W2_AT, WD_AT)[n] + c * D)
                                w_h, w_l = w_hi[:, bass.ds(at, D)], w_lo[:, bass.ds(at, D)]
                                for m, (x, w) in enumerate(((h_hi, w_h), (h_hi, w_l), (h_lo, w_h))):
                                    ins = pe.matmul(dst, x[:, par, c, rows], w, start=(c == 0 and m == 0 and k == 0),
                                                    stop=True, skip_group_check=True)
                    ins.then_inc(yp_ready[n], 1)

                def expert_of(j):
                    return pe.value_load(table[0:1, bass.ds(j, 1)], min_val=0, max_val=experts[n] - 1)

                def tile(j, par, first, last):
                    if not last:
                        turn_rows(j + 1, 1 - par)
                    e = expert_of(j)
                    pe.wait_ge(xlo_done[n], j + 1)
                    for c in range(NC_H):
                        if n == 0:
                            ins = hidden_chunk(h_bank[2 * par + c // 2][:, (c % 2) * TILE:(c % 2 + 1) * TILE], W1_AT, e, c, par)
                            if c % 2 == 1:
                                ins.then_inc(h_ready[n], 1)
                        else:
                            pe.wait_ge(split_done[n], 2 * j)
                            hidden_chunk(h_bank[c][:, 0:TILE], WG_AT, e, c, par)
                            hidden_chunk(h_bank[c][:, TILE:2 * TILE], WU_AT, e, c, par).then_inc(h_ready[n], 1)
                    if not first:
                        outputs(j - 1, 1 - par, expert_of(j - 1))

                turn_rows(0, 0)
                last_tile = over_tiles(pe, n, tile)
                outputs(last_tile, 1, expert_of(last_tile))

            def linear_body(b, i, par, nxt, nxt2):
                pe.wait_ge(x2_ready, b + 1)
                pe.wait_ge(rank_used[1], b)
                for t in range(T):
                    ins = pe.transpose(xbank[:, t * P:(t + 1) * P], x2w[:, t, :], ident)
                ins.then_inc(x2_turned, 1)
                pe.wait_ge(x2_copied, b + 1)
                for e in range(T):
                    if e == 2:
                        for t in range(T):
                            ins = pe.matmul(v_bank[:, t * D:(t + 1) * D], x2_t[:, 1 + t * P:1 + (t + 1) * P], wc[:, :],
                                            start=True, stop=True)
                        ins.then_inc(vv_ready, 1)
                    if e >= 2:
                        pe.wait_ge(decayed, T * b + e - 1)
                    pe.matmul(ws_bank[e % 2][:, 0:L - e * P], x2_t[:, e * P:(e + 1) * P], x2_t[:, 1 + e * P:1 + L],
                              start=True, stop=True).then_inc(ws_ready, 1)
                pe.wait_ge(vv_copied, b + 1)
                for c in range(T):
                    pe.wait_ge(decayed, T * b + c + 1)
                    for e in range(c + 1):
                        ins = pe.matmul(r_bank[:, c * P:(c + 1) * P], pm[:, e, (c - e) * P:(c - e + 1) * P],
                                        vv[:, e, :], start=e == 0, stop=e == c)
                ins.then_inc(reads_ready, 1)
                turn_x1(B + b + 1, par)
                route(1, b)

            for b in range(2):
                if b:
                    pe.wait_ge(v_copied, 2)
                turn(b)
                pe.wait_ge(xn_ready, b + 1)
                for j in range(2 * G):
                    if j >= 2:
                        pe.wait_ge(stack_ready, 2 * G * b + j - 1)
                    stacks(b, j)
                values(b)
                if b == 0:
                    for g in range(G):
                        scores(0, 0, 0, g, first=True)
            over_batches(pe, body)
            tile_table(0)
            expert_tiles(0)
            over_batches(pe, linear_body)
            tile_table(1)
            expert_tiles(1)


def constants():
    import numpy as np

    row = np.arange(P)
    cf = np.zeros((P, C_COLS), np.float32)
    cf[:, C_IDENT:C_IDENT + P] = np.eye(P)
    part = row % 32 // HD
    cf[:, C_NEG] = -1.0 * (part >= 2)
    cf[:, C_NEG + 1] = -1.0 * (part % 2)
    cf[:, C_IOTA:C_IOTA + E0] = np.arange(E0)
    cf[:, C_BASE:C_BASE + E0] = REGION * np.arange(E0)
    cf[:, C_NHALF:C_NHALF + T] = -0.5
    cf[:, C_ROW] = row
    lag = np.arange(L)[None, :] - 1 - row[:, None]
    cf[:, C_NMAT:C_NMAT + L] = -np.maximum(lag, 0)
    cf[:, C_CAUSAL:C_CAUSAL + L] = lag >= 0
    cf[:, C_EVEN] = (row % 2 == 0) & (row > 0)
    cf[:, C_STEP:C_STEP + E0] = TILE * np.arange(E0)
    cb = np.zeros((P, CB_COLS), np.float32)
    cb[:, CB_IDENT:CB_IDENT + P] = np.eye(P)
    cb[:, CB_TRI:CB_TRI + P] = row[:, None] < row[None, :]
    cb[:, CB_ONES:CB_ONES + P] = 1
    cb[:, CB_BAND:CB_BAND + 4 * P] = np.tile(np.where(abs(row[:, None] - row[None, :]) <= HALF, 0, NEG), 4)
    s = np.zeros((P, H, P), np.float32)
    for c in range(H):
        s[c, c] = s[32 + c, c] = 1
    cb[:, CB_SEL:] = s.reshape(P, H * P)
    return cf, cb.astype(mybir.dt.np(BF16))


def kernel(**inputs):
    import numpy as np
    import concourse.bacc as bacc
    from concourse.bass_utils import run_bass_kernel_spmd

    a = {k: np.asarray(v) for k, v in inputs.items()}
    wqkv = a["L0_attn_w_qkv"]

    def stacked(w):
        w = w.reshape(4, G, 1, HD, D)
        return np.broadcast_to(w, (4, G, 4, HD, D)).reshape(512, D).T

    w1 = a["L0_ffn_w1"].transpose(2, 0, 1).reshape(D, E0 * HID)
    w2 = a["L0_ffn_w2"].reshape(E0, D, NC_H, P).transpose(3, 0, 2, 1).reshape(P, E0 * HID)
    wg = a["L1_ffn_Wg"].transpose(1, 0, 2).reshape(D, E1 * HID)
    wu = a["L1_ffn_Wu"].transpose(1, 0, 2).reshape(D, E1 * HID)
    wd = a["L1_ffn_Wd"].reshape(E1, NC_H, P, D).transpose(2, 0, 1, 3).reshape(P, E1 * HID)
    cf, cb = constants()
    arrays = {
        "x_in": a["L0_attn_x"],
        "w_all": np.concatenate([w1, w2, wg, wu, wd], 1),
        "wq_s": stacked(wqkv[:D]),
        "wk_s": stacked(wqkv[D:2 * D]),
        "wv_t": wqkv[2 * D:].T,
        "wo_t": a["L0_attn_w_out"].T,
        "gamma": a["L0_attn_gamma"].reshape(D, 1),
        "beta": a["L0_attn_beta"].reshape(D, 1),
        "keys_t": a["L0_ffn_keys"].T,
        "rw_t": a["L0_ffn_rw"].T,
        "rb": a["L0_ffn_rb"].reshape(1, E0),
        "b1": a["L0_ffn_b1"].reshape(E0, NC_H, P).transpose(2, 0, 1).reshape(P, E0 * NC_H),
        "b2": a["L0_ffn_b2"].reshape(1, E0 * D),
        "w_write": a["L1_attn_W_write"],
        "w_read_t": a["L1_attn_W_read"].T,
        "decay": a["L1_attn_decay"].reshape(1, 1),
        "log_alpha": a["L1_attn_log_alpha"].reshape(1, 1),
        "wr": a["L1_ffn_Wr"],
        "const": cf,
        "const_b": cb,
    }
    arrays = {k: np.ascontiguousarray(v) for k, v in arrays.items()}
    nc = bacc.Bacc("TRN2", target_bir_lowering=False, num_devices=1)
    args = [nc.dram_tensor(k, v.shape, mybir.dt.from_np(v.dtype), kind="ExternalInput").ap()
            for k, v in arrays.items()]
    out = nc.dram_tensor("out", (B, L, D), F32, kind="ExternalOutput").ap()
    program(nc, *args, out)
    return run_bass_kernel_spmd(nc, [arrays], core_ids=[0]).results[0]["out"]
```

```python
from contextlib import ExitStack

import concourse.bass as bass
from concourse import mybir

F32 = mybir.dt.float32
BF16 = mybir.dt.bfloat16
U32 = mybir.dt.uint32
I32 = mybir.dt.int32
ALU = mybir.AluOpType
ACT = mybir.ActivationFunctionType
AX = mybir.AxisListType.X

P = 128
D = 128
B, L = 8, 512
T = L // P
NT = B * T
H, HD = 16, 8
HALF = 16
G = 4
WIN = [0, 96, 192, 288, 384]
QLO = [0, 112, 208, 304, 400, 512]
NW = len(WIN)
NQ = [QLO[w + 1] - QLO[w] for w in range(NW)]
V1 = HD + 1
EPS = 1e-5
NEG = -1.0e30
TILE = 256
S2 = TILE // P
HID = 512
NC_H = HID // P
CH = 512
E0, K0 = 16, 4
E1, K1 = 8, 2
REGION = B * L + TILE
W_COLS = 2 * E0 * HID + 3 * E1 * HID
CHUNKS = W_COLS // CH
CPB = CHUNKS // B
W1_AT, W2_AT = 0, E0 * HID
WG_AT = 2 * E0 * HID
WU_AT = WG_AT + E1 * HID
WD_AT = WU_AT + E1 * HID
SCALE = float(HD) ** -0.5
DEPTH_SCALE = 12.0 ** -0.5
DVE_STEPS = 26
STACK_BANK = [1, 1, 0, 1, 1, 0, 1, 0]
DVE_STEPS_1 = 21
DVE_STEPS_2 = 4


C_IDENT, C_NEG, C_IOTA, C_BASE, C_NHALF, C_ROW, C_STEP = 0, 128, 130, 146, 162, 166, 167
C_NMAT, C_CAUSAL = 183, 183 + L
C_EVEN = C_CAUSAL + L
C_COLS = C_EVEN + 1
CB_IDENT, CB_TRI, CB_ONES, CB_BAND, CB_SEL = 0, 128, 256, 384, 896
CB_COLS = CB_SEL + H * P


def max_tiles(experts, k):
    n = (B * L * k + experts * (TILE - 1)) // TILE
    return n + n % 2


class Chain:

    def __init__(self, eng, sem, base=0):
        self.eng, self.sem, self.base, self.n = eng, sem, base, 0

    def link(self, ins):
        ins.then_inc(self.sem, 1)
        self.n += 1
        self.eng.wait_ge(self.sem, self.base + self.n)
        return ins

    def mark(self, ins):
        ins.then_inc(self.sem, 1)
        self.n += 1
        return self.n

    def wait(self, n):
        self.eng.wait_ge(self.sem, self.base + n)


def bc(ap, axis, n):
    ap = ap.unsqueeze(axis)
    shape = list(ap.shape)
    shape[axis] = n
    return ap.to_broadcast(shape)



def program(nc, x_in, w_all, wq_s, wk_s, wv_t, wo_t, gamma, beta, keys_t, rw_t, rb, b1, b2,
            w_write, w_read_t, decay, log_alpha, wr, const, const_b, out):
    ctx = ExitStack()
    with ctx:
        scope = ctx

        def sb(name, shape, dt=F32):
            return scope.enter_context(nc.sbuf_tensor(name, shape, dt))

        def pb(name):
            return ctx.enter_context(nc.psum_tensor(name, [P, 512], F32))

        def sem(name):
            return ctx.enter_context(nc.semaphore(name))

        cf = sb("cf", [P, C_COLS])
        cb = sb("cb", [P, CB_COLS], BF16)
        ident = cf[:, C_IDENT:C_IDENT + P]
        neg_low = cf[:, C_NEG:C_NEG + 2]
        iota_e = cf[:, C_IOTA:C_IOTA + E0]
        base_e = cf[:, C_BASE:C_BASE + E0]
        nhalf = cf[:, C_NHALF:C_NHALF + T]
        ident_b = cb[:, CB_IDENT:CB_IDENT + P]
        tri = cb[:, CB_TRI:CB_TRI + P]
        ones_b = cb[:, CB_ONES:CB_ONES + P]
        band4 = cb[:, CB_BAND:CB_BAND + 4 * P]
        sel = cb[:, CB_SEL:CB_SEL + H * P].rearrange("p (c k) -> p c k", c=H)
        row_no = cf[:, C_ROW:C_ROW + 1]
        steps = cf[:, C_STEP:C_STEP + E0]
        nmat = cf[:, C_NMAT:C_NMAT + L]
        even = cf[:, C_EVEN:C_EVEN + 1]
        causal = cf[:, C_CAUSAL:C_CAUSAL + L]
        w_hi = sb("w_hi", [P, W_COLS], BF16)
        w_lo = sb("w_lo", [P, W_COLS], BF16)
        w_raw = sb("w_raw", [P, 2, CH])
        wqs = sb("wqs", [P, 512])
        wks = sb("wks", [P, 512])
        wv = sb("wv", [P, P])
        wo = sb("wo", [P, P])
        gb = sb("gb", [P, 2])
        keys_sb = sb("keys_sb", [P, 2, E0])
        keys2 = sb("keys2", [P, E0])
        ones_f = sb("ones_f", [P, P])
        g_route = sb("g_route", [P, E0])
        rb_sb = sb("rb_sb", [P, E0])
        c_route = sb("c_route", [P, E0])

        b1_sb = sb("b1_sb", [P, E0 * NC_H])
        wr_sb = sb("wr_sb", [P, E1])
        ww_sb = sb("ww_sb", [P, 2, D])
        dec = sb("dec", [P, 2])
        dexp = sb("dexp", [P, 1])
        dlog = sb("dlog", [P, 1])
        alpha = sb("alpha", [P, 1])
        wc = sb("wc", [P, D])
        zeros = sb("zeros", [P, S2 * D])

        xres = sb("xres", [P, NT, D])
        sres = [sb("sres0", [P, NT, K0]), sb("sres1", [P, NT, K1])]
        eres = [sb("eres0", [P, NT, K0]), sb("eres1", [P, NT, K1])]
        gres = [sb("gres0", [P, NT, K0], U32), sb("gres1", [P, NT, K1], U32)]
        wres = sb("wres", [P, NT, K0])
        carry = [sb("carry0", [P, E0]), sb("carry1", [P, E1])]
        carry_b = [sb("carry0_b", [P, E0], BF16), sb("carry1_b", [P, E1], BF16)]
        y = sb("y", [P, T, D])
        stat2 = sb("stat2", [P, T, 6])
        mv2 = sb("mv2", [P, T, 2])
        ve2 = sb("ve2", [P, T])
        rstd2 = sb("rstd2", [P, T])
        x1w = sb("x1w", [P, 2, T, D])
        x1_t = y[:, :, :].rearrange("p t d -> p (t d)")
        lg = sb("lg", [P, T, E0])
        mx8 = sb("mx8", [P, T, 8])
        ix8 = sb("ix8", [P, T, 8], U32)
        dtop = sb("dtop", [P, T, K0])
        etop = sb("etop", [P, T, K0])
        ssum = sb("ssum", [P, T])
        rsum = sb("rsum", [P, T])
        idf = sb("idf", [P, T, K0])
        oneh = sb("oneh", [P, T, K0, E0])
        mask = sb("mask", [P, T, E0], BF16)
        msum = sb("msum", [P, E0])
        r2 = sb("r2", [P, T, E0])
        pr = sb("pr", [P, T, K0, E0])
        slf = sb("slf", [P, T * K0])
        sidx = sb("sidx", [P, 2, T * K0], U32)
        cnt = sb("cnt", [P, E0])
        over = pr[:, :, :, :].rearrange("p t k e -> p (t k) e")
        ntile = sb("ntile", [P, E0])
        ntile_sum = sb("ntile_sum", [P, E0])
        past = sb("past", [P, E0])
        past_n = sb("past_n", [P, E0])
        tile_e = sb("tile_e", [P, 8])
        shift = sb("shift", [P, E0])
        table = sb("table", [1, 2 * P + 1], I32)
        tails = sb("tails", [1, E0], I32)

        scope = ExitStack()
        stat = sb("stat", [P, T, 6])
        mv = sb("mv", [P, T, 2])
        ve = sb("ve", [P, T])
        rstd = sb("rstd", [P, T])
        xh = sb("xh", [P, T, D])
        xn_t = sb("xn_t", [P, L])
        hi16 = sb("hi16", [P, 2, L], BF16)
        qst = sb("qst", [P, 2, G, L], BF16)
        kst = sb("kst", [P, 2, G, L], BF16)
        v2 = sb("v2", [P, 2, NW, H, V1 + HD], BF16)
        nm = sb("nm", [P, H])
        nm_t = sb("nm_t", [P, P], BF16)
        prob = sb("prob", [P, 2, 4 * P])
        prob_hi = sb("prob_hi", [P, G, 4 * P], BF16)
        prob_lo = sb("prob_lo", [P, G, 4 * P], BF16)
        rden = sb("rden", [P, G, 4])
        ao = sb("ao", [P, D])
        ao_t = sb("ao_t", [P, L])
        scope.close()

        scope = ExitStack()
        choice = sb("choice", [P, NT * K0, E0])
        xg = sb("xg", [P, 2, S2, D])
        xt_hi = sb("xt_hi", [P, 2, TILE], BF16)
        xt_lo = sb("xt_lo", [P, 2, TILE], BF16)
        act_out = sb("act_out", [P, NC_H, TILE])
        hid = sb("hid", [P, NC_H, TILE])
        h_hi = sb("h_hi", [P, 2, NC_H, TILE], BF16)
        h_lo = sb("h_lo", [P, 2, NC_H, TILE], BF16)
        ysb = sb("ysb", [P, 2, S2, D])
        b2_sb = sb("b2_sb", [P, E0, D])
        scope.close()

        scope = ExitStack()
        gat = sb("gat", [P, 2, T, K0, D])
        gidx = sb("gidx", [P, 2, T * K0], U32)
        wsel = sb("wsel", [P, T, K0])
        x2w = sb("x2w", [P, T, D])
        x2_t = sb("x2_t", [P, L + 1])
        vv = sb("vv", [P, T, D])
        pm = sb("pm", [P, T, L])
        decay_m = sb("decay_m", [P, L])
        ow = sb("ow", [P, 2, T, D])
        scope.close()

        s_bank = [pb("s0"), pb("s1")]
        t_bank = [pb("t0"), pb("t1")]
        avbank = pb("avbank")
        proj = [pb("proj0"), pb("proj1")]
        xbank = pb("xbank")
        av = avbank[:, 0:H * V1].rearrange("p (i t v) -> p i t v", i=G, t=4)
        lg_ps = avbank[:, 192:192 + T * E0].rearrange("p (t e) -> p t e", t=T)
        rk_ps = proj[1][:, 0:T * E0].rearrange("p (t e) -> p t e", t=T)
        rt_lg = xbank[:, 64:64 + T * E0].rearrange("p (t e) -> p t e", t=T)
        nm_ps = xbank[0:H, 256:384]
        ao_ps = xbank[:, 384:512]
        rank_ps = xbank[:, 0:T * E0].rearrange("p (t e) -> p t e", t=T)

        xt_bank, h_bank, y_bank = xbank, s_bank + t_bank, [avbank, proj[0]]
        v_bank, ws_bank, r_bank = avbank, t_bank, proj[0]

        tiles = [max_tiles(E0, K0), max_tiles(E1, K1)]
        experts = [E0, E1]
        top = [K0, K1]
        xs = [nc.dram_tensor(f"xs{n}", [experts[n] * REGION, D], F32).ap() for n in range(2)]
        ys = [nc.dram_tensor(f"ys{n}", [(tiles[n] + 2) * TILE, D], F32).ap() for n in range(2)]

        (loaded, hi_done, lo_done, pool_step, dve_step, routes_ready, init_done, var_ready, rstd_ready, v_high, low_even, low_odd,
         xhat_ready, xhat_turned, xn_ready, proj_ready, half_ready, stack_ready, v_ready, v_copied,
         s_ready, max_done, nm_ready, nm_split, st_ready, exp_done, av_ready, ao_ready, ao_turned,
         ao_copied, o_ready, y_ready, var2_ready, rstd2_ready, x1_ready, x1_turned, x1_copied, x1_kept,
         stored, keys_ready, wc_ready, gamma_ready, decay_ready, expd_ready,
         y2_ready, var3_ready, rstd3_ready, x2_ready, x2_turned, x2_copied, vv_ready, vv_copied,
         ws_ready, decayed, reads_ready, y3_ready, comb_done, out_ready, yf_ready, dlog_ready) = [
            sem(n) for n in (
                "loaded hi_done lo_done pool_step dve_step routes_ready init_done var_ready rstd_ready v_high low_even low_odd "
                "xhat_ready xhat_turned xn_ready proj_ready half_ready stack_ready v_ready v_copied "
                "s_ready max_done nm_ready nm_split st_ready exp_done av_ready ao_ready ao_turned "
                "ao_copied o_ready y_ready var2_ready rstd2_ready x1_ready x1_turned x1_copied x1_kept "
                "stored keys_ready wc_ready gamma_ready decay_ready expd_ready "
                "y2_ready var3_ready rstd3_ready x2_ready x2_turned x2_copied vv_ready vv_copied "
                "ws_ready decayed reads_ready y3_ready comb_done out_ready yf_ready dlog_ready").split()]

        def pair_of(name):
            return [sem(name + "0"), sem(name + "1")]

        (lg_ready, d_ready, e_ready, mask_ready, rank_ready, rank_used, slots_ready, carry_ready, cnt_ready,
         table_ready, table_turned, table_kept, tails_ready, tails_stored, g_turned, xhi_done, xlo_done,
         h_ready, act_done, split_done, yp_ready, y_done, tile_step, rows_ready) = [
            pair_of(n) for n in (
                "lg_ready d_ready e_ready mask_ready rank_ready rank_used slots_ready carry_ready cnt_ready "
                "table_ready table_turned table_kept tails_ready tails_stored g_turned xhi_done xlo_done "
                "h_ready act_done split_done yp_ready y_done tile_step rows_ready").split()]
        xg_loaded = [pair_of("xg_loaded0_"), pair_of("xg_loaded1_")]
        y_stored = [pair_of("y_stored0_"), pair_of("y_stored1_")]
        gathered = [pair_of("gathered0_"), pair_of("gathered1_")]
        scattered1 = pair_of("scattered1_")
        o_stored = pair_of("o_stored")
        raw_in = [sem("raw_in0"), sem("raw_in1")]
        scattered = [sem("scattered0"), sem("scattered1")]

        x_tiles = x_in.rearrange("b (t p) d -> p (b t) d", p=P)

        def tile_rounds(j, par):
            return 8 * (j - par)

        def more_pairs(eng, n):
            return eng.value_load(table[0:1, 2 * P:2 * P + 1], min_val=B * L * top[n] // (2 * TILE) - 1,
                                  max_val=tiles[n] // 2 - 1)

        def over_tiles(eng, n, tile, ch=None, steps=0):
            more = more_pairs(eng, n)
            last_tile = 2 * more + 1

            def one(j, par, first, last):
                if ch:
                    ch.base, ch.n = steps * j, 0
                tile(j, par, first, last)
                assert not ch or ch.n == steps, ch.n
            one(0, 0, True, False)
            with eng.Fori(0, more) as p:
                one(2 * p + 1, 1, False, False)
                one(2 * p + 2, 0, False, False)
            one(last_tile, 1, False, True)
            return last_tile

        def over_batches(eng, body):
            with eng.Fori(0, B // 2 - 1) as i:
                body(2 * i, i, 0, True, True)
                body(2 * i + 1, i, 1, True, True)
            body(B - 2, B // 2 - 1, 0, True, False)
            body(B - 1, B // 2 - 1, 1, False, False)

        def over_attention(eng, body, ch=None, steps=0):
            body(0, 0, 0, 0, True, True)
            body(1, 0, 1, 1, True, True)
            start = ch.base + ch.n if ch else 0

            def one(b, i, par):
                if ch:
                    ch.base, ch.n = start + steps * (b - 2), 0
                body(b, i, par, 2, True, True)
                assert not ch or ch.n == steps, ch.n
            with eng.Fori(0, B // 2 - 2) as j:
                one(2 * j + 2, j + 1, 0)
                one(2 * j + 3, j + 1, 1)
            body(B - 2, B // 2 - 1, 0, 2, True, False)
            body(B - 1, B // 2 - 1, 1, 2, False, False)

        LOADS = 18

        def apart(eng):
            eng.nop(nofuse=True)

        block = ctx.enter_context(nc.Block())

        @block.sync
        def _(sp):
            for dst, src in [(xres[:, :, :], x_tiles), (cf[:, :], const), (cb[:, :], const_b), (wqs[:, :], wq_s),
                             (wks[:, :], wk_s), (gb[:, 0:1], gamma), (wv[:, :], wv_t), (wo[:, :], wo_t),
                             (keys_sb[:, 0, :], keys_t), (keys_sb[:, 1, :], rw_t),
                             (rb_sb[:, :], rb.to_broadcast([P, E0])), (gb[:, 1:2], beta),
                             (b1_sb[:, :], b1), (wr_sb[:, :], wr), (ww_sb[:, 0, :], w_write),
                             (ww_sb[:, 1, :], w_read_t), (dec[:, 0:1], decay.to_broadcast([P, 1])),
                             (dec[:, 1:2], log_alpha.to_broadcast([P, 1]))]:
                sp.dma_start(dst, src).then_inc(loaded, 16)

            for k in range(2):
                sp.dma_start(w_raw[:, k, :], w_all[:, k * CH:(k + 1) * CH]).then_inc(raw_in[k], 16)
            with sp.Fori(1, CHUNKS // 2) as c:
                for k in range(2):
                    sp.wait_ge(lo_done, 2 * c + k - 1)
                    sp.dma_start(w_raw[:, k, :], w_all[:, bass.ds((2 * c + k) * CH, CH)]).then_inc(raw_in[k], 16)
            def fill_tails(n):
                sp.wait_ge(tails_ready[n], 1)
                for e in range(experts[n]):
                    row = sp.value_load(tails[0:1, e:e + 1], min_val=e * REGION, max_val=e * REGION + B * L)
                    sp.dma_start(xs[n][bass.ds(row, TILE), :].rearrange("(p s) d -> p (s d)", s=S2),
                                 zeros[:, :]).then_inc(tails_stored[n], 16)
                sp.wait_ge(tails_stored[n], 16 * experts[n])
                for par in range(2):
                    sp.wait_ge((scattered, scattered1)[n][par], 8 * B * T * top[n])

            def expert_tiles(n):
                def load(j, par):
                    row = sp.value_load(table[0:1, bass.ds(P + j, 1)], min_val=0, max_val=experts[n] * REGION - TILE)
                    sp.dma_start(xg[:, par, :, :].rearrange("p s d -> p (s d)"),
                                 xs[n][bass.ds(row, TILE), :].rearrange("(p s) d -> p (s d)", s=S2)
                                 ).then_inc(xg_loaded[n][par], 16)

                def store(j, par):
                    sp.wait_ge(y_done[n], j + 1)
                    sp.dma_start(ys[n][bass.ds(j * TILE, TILE), :].rearrange("(p s) d -> p (s d)", s=S2),
                                 ysb[:, par, :, :].rearrange("p s d -> p (s d)")).then_inc(y_stored[n][par], 16)

                def tile(j, par, first, last):
                    if not last:
                        sp.wait_ge(g_turned[n], j + 1)
                        load(j + 2, par)
                    if not first:
                        store(j - 1, 1 - par)

                sp.wait_ge(table_kept[n], 1)
                load(0, 0)
                load(1, 1)
                store(over_tiles(sp, n, tile), 1)
                with sp.Fori(more_pairs(sp, n) + 1, tiles[n] // 2 + 1) as p:
                    for par in range(2):
                        sp.dma_start(ys[n][bass.ds((2 * p + par) * TILE, TILE), :].rearrange("(p s) d -> p (s d)", s=S2),
                                     zeros[:, :]).then_inc(y_stored[n][par], 16)

            sp.wait_ge(x1_kept, B)
            sp.wait_ge(table_kept[0], 1)
            sp.dma_start(b2_sb[:, :, :].rearrange("p e d -> p (e d)"), b2.to_broadcast([P, E0 * D])).then_inc(loaded, 16)
            fill_tails(0)
            expert_tiles(0)
            fill_tails(1)
            expert_tiles(1)
            for b in range(B):
                sp.wait_ge(out_ready, b + 1)
                sp.dma_start(out[b].rearrange("(t p) d -> p t d", p=P), ow[:, b % 2, :, :]).then_inc(o_stored[b % 2], 16)
            for par in range(2):
                sp.wait_ge(o_stored[par], 8 * B)

        @block.gpsimd
        def _(pool):
            pool.memset(nm_t[:, :], 0.0)
            pool.memset(prob_hi[:, :, :], 1.0)
            pool.memset(prob_lo[:, :, :], 0.0)
            for n in range(2):
                pool.memset(carry[n][:, :], 0.0)
                pool.memset(carry_b[n][:, :], 0.0)
            pool.memset(zeros[:, :], 0.0)
            pool.memset(ones_f[:, :], 1.0)
            pool.memset(v2[:, :, :, :, HD:V1], 1.0).then_inc(init_done, 1)
            pool.wait_ge(loaded, 16 * LOADS)

            def rstd_of(b):
                pool.wait_ge(var_ready, b + 1)
                pool.tensor_tensor(rstd[:, :], ve[:, :], nhalf, ALU.pow).then_inc(rstd_ready, 1)

            def low_of(win, w, g):
                pool.wait_ge(exp_done, G * win + g + 1)
                width = 4 * NQ[w]
                pool.tensor_tensor(prob_lo[:, g, 0:width], prob[:, g % 2, 0:width], prob_hi[:, g, 0:width],
                                   ALU.subtract).then_inc(low_odd, 1)

            def body(b, i, par, prev, nxt, nxt2):
                done = 0
                for w in range(NW):
                    low_of(b * NW + w, w, 1)
                    if prev == 2 and w < T:
                        if w == 0:
                            pool.wait_ge(slots_ready[0], b - 1)
                            apart(pool)
                        scatter(0, par, w, range(0, K0 // 2))
                    if w == 3 and nxt2:
                        rstd_of(b + 2)
                    low_of(b * NW + w, w, 3)
                    if prev == 2 and w < T:
                        scatter(0, par, w, range(K0 // 2, K0))
                    if w == 1 and prev:
                        rstd_of_y(b)
                    for k in range(done, done + (2 if w >= 2 * NW - CPB else 1)):
                        pool.wait_ge(hi_done, CPB * b + k + 1)
                        at = (b * CPB + k) * CH
                        pool.tensor_tensor(w_lo[:, bass.ds(at, CH)], w_raw[:, (par * CPB + k) % 2, :],
                                           w_hi[:, bass.ds(at, CH)], ALU.subtract).then_inc(lo_done, 1)
                        done = k + 1
                if prev:
                    keep(0, b - 1, 1 - par)

            def rstd_of_y(count):
                pool.wait_ge(var2_ready, count)
                pool.tensor_tensor(rstd2[:, :], ve2[:, :], nhalf, ALU.pow).then_inc(rstd2_ready, 1)

            def keep(n, b, par):
                pool.wait_ge(x1_ready, B * n + b + 1)
                apart(pool)
                pool.tensor_copy(xres[:, bass.ds(b * T, T), :], x1w[:, par, :, :]).then_inc(x1_kept, 1)

            def scatter(n, par, t, ks):
                for k in ks:
                    at = t * top[n] + k
                    pool.indirect_dma_start(
                        out=xs[n][:, :], out_offset=bass.IndirectOffsetOnAxis(sidx[:, par, at:at + 1], 0),
                        in_=x1w[:, par, t, :], in_offset=None).then_inc((scattered, scattered1)[n][par], 16)

            def send(n, b, par):
                pool.wait_ge(slots_ready[n], b + 1)
                apart(pool)
                for t in range(T):
                    scatter(n, par, t, range(top[n]))

            def gather(n, b, par):
                k_n = top[n]
                apart(pool)
                pool.tensor_copy(gidx[:, par, 0:T * k_n].rearrange("p (t k) -> p t k", t=T),
                                 gres[n][:, bass.ds(b * T, T), :]).then_inc(pool_step, 1)
                pool.wait_ge(pool_step, B * n + b + 1)
                apart(pool)
                for t in range(T):
                    for k in range(k_n):
                        at = t * k_n + k
                        pool.indirect_dma_start(
                            out=gat[:, par, t, k, :], out_offset=None, in_=ys[n][:, :],
                            in_offset=bass.IndirectOffsetOnAxis(gidx[:, par, at:at + 1], 0)).then_inc(gathered[n][par], 16)

            def linear_body(b, i, par, nxt, nxt2):
                if nxt:
                    pool.wait_ge(comb_done, b)
                    gather(0, b + 1, 1 - par)
                rstd_of_y(B + 2 * b + 1)
                rstd_of_y(B + 2 * b + 2)
                keep(1, b, par)
                send(1, b, par)

            def final_body(b, i, par, nxt, nxt2):
                if nxt:
                    pool.wait_ge(comb_done, B + b)
                    gather(1, b + 1, 1 - par)
                rstd_of_y(3 * B + b + 1)

            def outputs_stored(n):
                pool.wait_ge(table_kept[n], 1)
                more = more_pairs(pool, n)
                for par in range(2):
                    pool.wait_ge(y_stored[n][par], 8 * tiles[n] + 16)
                pool.wait_ge(xg_loaded[n][0], 16 * more + 32)
                pool.wait_ge(rows_ready[n], 1)

            rstd_of(0)
            rstd_of(1)
            over_attention(pool, body)
            rstd_of_y(B)
            send(0, B - 2, 0)
            send(0, B - 1, 1)
            keep(0, B - 1, 1)
            outputs_stored(0)
            apart(pool)
            pool.memset(x2_t[:, 0:1], 0.0).then_inc(init_done, 1)
            gather(0, 0, 0)
            over_batches(pool, linear_body)
            outputs_stored(1)
            gather(1, 0, 0)
            over_batches(pool, final_body)

        @block.vector
        def _(dve):
            ch = Chain(dve, dve_step)
            dve.wait_ge(loaded, 16 * LOADS)
            dve.wait_ge(init_done, 1)
            dve.tensor_tensor(keys2[:, :], keys_sb[:, 0, :], keys_sb[:, 0, :], ALU.mult).then_inc(keys_ready, 1)
            dve.scalar_tensor_tensor(out=g_route[:, :], in0=keys_sb[:, 0, :], scalar=2.0, in1=keys_sb[:, 1, :],
                                     op0=ALU.mult, op1=ALU.add)
            dve.wait_ge(routes_ready, 1)
            ch.link(dve.tensor_tensor(c_route[:, :], rb_sb[:, :], rt_lg[:, 0, :], ALU.subtract))

            def stats(src, st, m, v, ready):
                for t in range(T):
                    ins = dve.bn_stats(st[:, t, :], src(t))
                ch.link(ins)
                apart(dve)
                for t in range(T):
                    ins = dve.bn_aggr(m[:, t, :], st[:, t, :])
                ch.link(ins)
                dve.tensor_scalar(v[:, :], m[:, :, 1], EPS, None, ALU.add).then_inc(ready, 1)

            def prep_stats(b):
                stats(lambda t: xres[:, b * T + t, :], stat, mv, ve, var_ready)

            def prep_xhat(b):
                dve.wait_ge(rstd_ready, b + 1)
                dve.wait_ge(xhat_turned, b)
                for t in range(T):
                    ins = dve.tensor_scalar(xh[:, t, :], xres[:, b * T + t, :], mv[:, t, 0:1], rstd[:, t:t + 1],
                                            ALU.subtract, ALU.mult)
                ins.then_inc(xhat_ready, 1)

            def prep_stack(b, par, j):
                dve.wait_ge(half_ready, 2 * G * b + j + 1)
                dst = (qst if j < G else kst)[:, par, j % G, :]
                dve.scalar_tensor_tensor(out=dst, in0=hi16[:, j % 2, :], scalar=neg_low[:, j // G:j // G + 1],
                                         in1=proj[STACK_BANK[j]][:, :], op0=ALU.mult,
                                         op1=ALU.add).then_inc(stack_ready, 1)

            def value_low(b, par):
                for part, (bank, ws) in enumerate(((proj[1], range(0, 4)), (proj[0], range(4, 5)))):
                    dve.wait_ge(v_high, 2 * b + part + 1)
                    for w in ws:
                        at = (w % 4) * P
                        ins = dve.tensor_tensor(v2[:, par, w, :, V1:V1 + HD],
                                                bank[:, at:at + P].rearrange("p (h d) -> p h d", h=H),
                                                v2[:, par, w, :, 0:HD], ALU.subtract)
                    ins.then_inc(v_copied, 1)

            def max_of(win, i):
                dve.wait_ge(s_ready, G * win + i + 1)
                dve.tensor_reduce(nm[:, 4 * i:4 * i + 4], s_bank[i % 2][:, :].rearrange("p (t k) -> p t k", t=4),
                                  AX.X, ALU.max, negate=True).then_inc(max_done, 1)

            def prob_low(win, w, g):
                dve.wait_ge(exp_done, G * win + g + 1)
                width = 4 * NQ[w]
                dve.tensor_tensor(prob_lo[:, g, 0:width], prob[:, g % 2, 0:width], prob_hi[:, g, 0:width],
                                  ALU.subtract).then_inc(low_even, 1)

            def split_max(win):
                dve.wait_ge(nm_ready, win + 1)
                ch.link(dve.tensor_copy(nm_t[0:H, :], nm_ps))
                dve.tensor_tensor(nm_t[32:32 + H, :], nm_ps, nm_t[0:H, :], ALU.subtract).then_inc(nm_split, 1)

            def divide(win, beside=None):
                dve.wait_ge(av_ready, win + 1)
                if beside:
                    beside()
                ch.link(dve.reciprocal(rden[:, :, :], av[:, :, :, HD]))
                dve.wait_ge(ao_turned, win)
                dve.tensor_tensor(ao[:, :].rearrange("p (t i d) -> p i t d", t=4, i=G), av[:, :, :, 0:HD],
                                  bc(rden[:, :, :], 3, HD), ALU.mult).then_inc(ao_ready, 1)

            def take_logits(n, b):
                dve.wait_ge(lg_ready[n], b + 1)
                if n == 0:
                    ch.link(dve.tensor_tensor(lg[:, :, :], lg_ps, bc(c_route[:, :], 1, T), ALU.add))
                else:
                    ch.link(dve.tensor_copy(lg[:, :, 0:E1], rt_lg[:, :, 0:E1]))

            def choose(n):
                k_n = top[n]
                lgv = lg[:, :, 0:experts[n]]
                apart(dve)
                for t in range(T):
                    ins = dve.max(mx8[:, t, :], lgv[:, t, :])
                ch.link(ins)
                apart(dve)
                for t in range(T):
                    ins = dve.max_index(ix8[:, t, :], mx8[:, t, :], lgv[:, t, :])
                ch.link(ins)
                dve.tensor_tensor(dtop[:, :, 0:k_n], mx8[:, :, 0:k_n], mx8[:, :, 0:1].to_broadcast([P, T, k_n]),
                                  ALU.subtract).then_inc(d_ready[n], 1)
                ch.link(dve.tensor_copy(idf[:, :, 0:k_n], ix8[:, :, 0:k_n]))

            def mark(n):
                e_n, k_n = experts[n], top[n]
                mk, oh = mask[:, :, 0:e_n], oneh[:, :, 0:k_n, 0:e_n]
                for k in range(k_n):
                    ins = dve.tensor_tensor(oh[:, :, k, :], bc(iota_e[:, 0:e_n], 1, T),
                                            idf[:, :, k:k + 1].to_broadcast([P, T, e_n]), ALU.is_equal)
                ch.link(ins)
                with nc.allow_low_precision(reason="the sums are 0 or 1"):
                    dve.tensor_reduce(mk, oh.rearrange("p t k e -> p t e k"), AX.X, ALU.add).then_inc(mask_ready[n], 1)

            def take_ranks(n, b, ranks):
                e_n = experts[n]
                dve.wait_ge(rank_ready[n], b + 1)
                dve.tensor_tensor(r2[:, :, 0:e_n], ranks[:, :, 0:e_n], bc(base_e[:, 0:e_n], 1, T),
                                  ALU.add).then_inc(rank_used[n], 1)

            def weigh(n, b):
                e_n, k_n = experts[n], top[n]
                dve.wait_ge(mask_ready[n], b + 1)
                ch.link(dve.tensor_reduce(msum[:, 0:e_n], mask[:, :, 0:e_n].rearrange("p t e -> p e t"), AX.X, ALU.add))
                dve.wait_ge(e_ready[n], b + 1)
                ch.link(dve.tensor_reduce(ssum[:, :], etop[:, :, 0:k_n], AX.X, ALU.add))
                ch.link(dve.reciprocal(rsum[:, :], ssum[:, :]))
                if n == 1:
                    ch.link(dve.tensor_scalar(rsum[:, :], rsum[:, :], DEPTH_SCALE, None, ALU.mult))
                dve.tensor_tensor(wres[:, bass.ds(b * T, T), 0:k_n], etop[:, :, 0:k_n], bc(rsum[:, :], 2, k_n), ALU.mult)

            def place(n, b, par):
                e_n, k_n = experts[n], top[n]
                oh = oneh[:, :, 0:k_n, 0:e_n]
                dve.wait_ge(rank_used[n], b + 1)
                ch.link(dve.tensor_tensor(carry[n][:, :], carry[n][:, :], msum[:, 0:e_n], ALU.add))
                dve.tensor_copy(carry_b[n][:, :], carry[n][:, :]).then_inc(carry_ready[n], 1)
                for k in range(k_n):
                    ins = dve.tensor_tensor(pr[:, :, k, 0:e_n], oh[:, :, k, :], r2[:, :, 0:e_n], ALU.mult)
                ch.link(ins)
                ch.link(dve.tensor_reduce(slf[:, 0:T * k_n].rearrange("p (t k) -> p t k", t=T),
                                          pr[:, :, 0:k_n, 0:e_n], AX.X, ALU.add))
                dve.tensor_copy(sidx[:, par, 0:T * k_n], slf[:, 0:T * k_n]).then_inc(slots_ready[n], 1)
                dve.tensor_copy(eres[n][:, bass.ds(b * T, T), :], idf[:, :, 0:k_n])
                ch.link(dve.tensor_copy(sres[n][:, bass.ds(b * T, T), :],
                                        slf[:, 0:T * k_n].rearrange("p (t k) -> p t k", t=T)))

            def tile_table(n):
                e_n = experts[n]
                dve.wait_ge(cnt_ready[n], 1)
                ch.link(dve.tensor_copy(cnt[:, 0:e_n], xbank[:, 0:e_n]))
                dve.tensor_tensor(tails[0:1, 0:e_n], cnt[0:1, 0:e_n], base_e[0:1, 0:e_n], ALU.add).then_inc(tails_ready[n], 1)
                ch.link(dve.tensor_tensor(over[:, 0:e_n, :], cnt[:, 0:e_n].unsqueeze(2).to_broadcast([P, e_n, E0]),
                                          bc(steps, 1, e_n), ALU.is_gt))
                ch.link(dve.tensor_reduce(ntile[:, 0:e_n], over[:, 0:e_n, :], AX.X, ALU.add))
                ch.link(dve.tensor_tensor_scan(ntile_sum[:, 0:e_n], ones_f[:, 0:e_n], ntile[:, 0:e_n], 0.0, ALU.mult, ALU.add))
                ch.link(dve.tensor_scalar(past[:, 0:e_n], ntile_sum[:, 0:e_n], row_no, None, ALU.is_le))
                ch.link(dve.tensor_tensor(past_n[:, 0:e_n], past[:, 0:e_n], ntile[:, 0:e_n], ALU.mult))
                dve.tensor_reduce(tile_e[:, 0:1], past[:, 0:e_n], AX.X, ALU.add)
                ch.link(dve.tensor_reduce(tile_e[:, 1:2], past_n[:, 0:e_n], AX.X, ALU.add))
                dve.tensor_tensor(tile_e[:, 2:3], row_no, tile_e[:, 1:2], ALU.subtract)
                ch.link(dve.tensor_scalar(tile_e[:, 3:4], tile_e[:, 0:1], e_n - 0.5, None, ALU.is_lt))
                ch.link(dve.tensor_scalar(tile_e[:, 2:3], tile_e[:, 2:3], float(TILE), None, ALU.mult))
                ch.link(dve.scalar_tensor_tensor(out=tile_e[:, 2:3], in0=tile_e[:, 0:1], scalar=float(REGION),
                                                 in1=tile_e[:, 2:3], op0=ALU.mult, op1=ALU.add))
                dve.tensor_tensor(tile_e[:, 4:5], tile_e[:, 0:1], tile_e[:, 3:4], ALU.mult)
                dve.tensor_tensor(tile_e[:, 5:6], tile_e[:, 2:3], tile_e[:, 3:4], ALU.mult).then_inc(table_ready[n], 1)
                ch.link(dve.tensor_tensor(shift[:, 0:e_n], ntile_sum[:, 0:e_n], ntile[:, 0:e_n], ALU.subtract))
                ch.link(dve.tensor_scalar(shift[:, 0:e_n], shift[:, 0:e_n], float(TILE), None, ALU.mult))
                ch.link(dve.tensor_tensor(shift[:, 0:e_n], shift[:, 0:e_n], base_e[:, 0:e_n], ALU.subtract))
                dve.wait_ge(table_turned[n], 1)
                dve.tensor_copy(table[0:1, :], xbank[0:1, 0:2 * P + 1]).then_inc(table_kept[n], 1)

            def expert_tiles(n):
                ch = Chain(dve, tile_step[n])

                def lo_of(j, par):
                    dve.wait_ge(xhi_done[n], j + 1)
                    dve.tensor_tensor(xt_lo[:, par, :], xt_bank[:, 0:TILE], xt_hi[:, par, :],
                                      ALU.subtract).then_inc(xlo_done[n], 1)

                def split(j, par, half, src):
                    c = slice(2 * half, 2 * half + 2)
                    ch.link(dve.tensor_copy(h_hi[:, par, c, :], src[:, c, :]))
                    dve.tensor_tensor(h_lo[:, par, c, :], src[:, c, :], h_hi[:, par, c, :],
                                      ALU.subtract).then_inc(split_done[n], 1)

                def take_out(j, par):
                    dve.wait_ge(yp_ready[n], j + 1)
                    dve.wait_ge(y_stored[n][par], tile_rounds(j, par))
                    src = y_bank[par][:, 0:S2 * D].rearrange("p (s d) -> p s d", s=S2)
                    if n == 0:
                        e = dve.value_load(table[0:1, bass.ds(j, 1)], min_val=0, max_val=E0 - 1)
                        ins = dve.tensor_tensor(ysb[:, par, :, :], src,
                                                b2_sb[:, bass.ds(e, 1), :].to_broadcast([P, S2, D]), ALU.add)
                    else:
                        ins = dve.tensor_copy(ysb[:, par, :, :], src)
                    ins.then_inc(y_done[n], 1)

                def tile(j, par, first, last):
                    if not last:
                        lo_of(j + 1, 1 - par)
                    for half in range(2):
                        if n == 0:
                            dve.wait_ge(act_done[n], 2 * j + half + 1)
                            split(j, par, half, act_out)
                        else:
                            for c in range(2 * half, 2 * half + 2):
                                dve.wait_ge(act_done[n], NC_H * j + c + 1)
                                ins = dve.tensor_tensor(hid[:, c, :], act_out[:, c, :], h_bank[c][:, TILE:2 * TILE], ALU.mult)
                                ch.link(ins)
                            split(j, par, half, hid)
                    if not first:
                        take_out(j - 1, 1 - par)

                dve.wait_ge(table_kept[n], 1)
                lo_of(0, 0)
                take_out(over_tiles(dve, n, tile, ch, 2 if n == 0 else 6), 1)

            def output_rows(n):
                e_n, m = experts[n], NT * top[n]
                sel_e = choice[:, 0:m, 0:e_n]
                ch.link(dve.tensor_tensor(sel_e, bc(iota_e[:, 0:e_n], 1, m),
                                          bc(eres[n][:, :, :].rearrange("p t k -> p (t k)"), 2, e_n), ALU.is_equal))
                ch.link(dve.tensor_tensor(sel_e, sel_e, bc(shift[:, 0:e_n], 1, m), ALU.mult))
                rows = eres[n][:, :, :].rearrange("p t k -> p (t k)")
                ch.link(dve.tensor_reduce(rows, sel_e, AX.X, ALU.add))
                ch.link(dve.tensor_tensor(rows, rows, sres[n][:, :, :].rearrange("p t k -> p (t k)"), ALU.add))
                dve.tensor_copy(gres[n][:, :, :].rearrange("p t k -> p (t k)"), rows).then_inc(rows_ready[n], 1)

            def combine(n, b, i, par):
                k_n = top[n]
                ch.link(dve.tensor_copy(wsel[:, :, 0:k_n], wres[:, bass.ds(b * T, T), 0:k_n]))
                dve.wait_ge(gathered[n][par], 16 * T * k_n * (i + 1))
                for k in range(k_n):
                    for t in range(T):
                        before = xres[:, b * T + t, :] if k == 0 else y[:, t, :]
                        ins = dve.scalar_tensor_tensor(out=y[:, t, :], in0=gat[:, par, t, k, :],
                                                       scalar=wsel[:, t, k:k + 1], in1=before,
                                                       op0=ALU.mult, op1=ALU.add)
                    if k < k_n - 1:
                        ch.link(ins)
                ins.then_inc(comb_done, 1)
                dve.wait_ge(comb_done, B * n + b + 1)

            def y_stats():
                stats(lambda t: y[:, t, :], stat2, mv2, ve2, var2_ready)

            def norm_apply(count, dst, ready):
                dve.wait_ge(rstd2_ready, count)
                for t in range(T):
                    ins = dve.tensor_scalar(dst(t), y[:, t, :], mv2[:, t, 0:1], rstd2[:, t:t + 1],
                                            ALU.subtract, ALU.mult)
                ins.then_inc(ready, 1)

            def norm(count, dst, ready):
                y_stats()
                norm_apply(count, dst, ready)

            def linear_body(b, i, par, nxt, nxt2):
                combine(0, b, i, par)
                norm(B + 2 * b + 1, lambda t: x2w[:, t, :], x2_ready)
                for e in range(T):
                    dve.wait_ge(ws_ready, T * b + e + 1)
                    dve.tensor_tensor(pm[:, e, 0:L - e * P], ws_bank[e % 2][:, 0:L - e * P],
                                      decay_m[:, 0:L - e * P], ALU.mult).then_inc(decayed, 1)
                dve.wait_ge(reads_ready, b + 1)
                dve.scalar_tensor_tensor(out=y[:, :, :].rearrange("p t d -> p (t d)"),
                                         in0=x2w[:, :, :].rearrange("p t d -> p (t d)"), scalar=2.0,
                                         in1=r_bank[:, :], op0=ALU.mult, op1=ALU.add).then_inc(y3_ready, 1)
                dve.wait_ge(y3_ready, b + 1)
                dve.wait_ge(scattered1[par], 16 * T * K1 * i)
                norm(B + 2 * b + 2, lambda t: x1w[:, par, t, :], x1_ready)
                take_logits(1, b)
                choose(1)
                mark(1)
                weigh(1, b)
                take_ranks(1, b, rank_ps)
                place(1, b, par)

            def final_body(b, i, par, nxt, nxt2):
                combine(1, b, i, par)
                dve.wait_ge(o_stored[par], 16 * i)
                norm(3 * B + b + 1, lambda t: ow[:, par, t, :], out_ready)

            def residual(b):
                dve.wait_ge(o_ready, b + 1)
                dve.scalar_tensor_tensor(out=y[:, :, :].rearrange("p t d -> p (t d)"),
                                         in0=xres[:, bass.ds(b * T, T), :].rearrange("p t d -> p (t d)"), scalar=2.0,
                                         in1=proj[0][:, :], op0=ALU.mult, op1=ALU.add).then_inc(y_ready, 1)

            def residual_stats(b):
                dve.wait_ge(y_ready, b + 1)
                y_stats()

            def normalise(b, i, par):
                dve.wait_ge(scattered[par], 16 * T * K0 * i)
                norm_apply(b + 1, lambda t: x1w[:, par, t, :], x1_ready)

            def body(b, i, par, prev, nxt, nxt2):
                for w in range(NW):
                    win = b * NW + w
                    before, after = w > 0 or prev, w < NW - 1 or nxt
                    split_max(win)
                    if after:
                        max_of(win + 1, 0)
                    if after:
                        max_of(win + 1, 1)
                    if w in (2, 3) and nxt:
                        prep_stack(b + 1, 1 - par, 3 * w - 3)
                    if before:
                        beside = None
                        if w == 3 and prev:
                            beside = lambda: take_logits(0, b - 1)
                        divide(win - 1, beside)
                    if w == 2 and prev:
                        normalise(b - 1, i - 1 + par, 1 - par)
                    if w == 1 and prev:
                        residual(b - 1)
                    if w == 4 and prev:
                        mark(0)
                    if after:
                        max_of(win + 1, 2)
                    prob_low(win, w, 0)
                    if after:
                        max_of(win + 1, 3)
                    if w in (0, 1, 3) and nxt:
                        prep_stack(b + 1, 1 - par, (0, 1, None, 7)[w])
                    prob_low(win, w, 2)
                    if w == 1 and prev:
                        residual_stats(b - 1)
                    if w == 1 and nxt:
                        prep_stack(b + 1, 1 - par, 2)
                    if w == 2:
                        if nxt:
                            prep_stack(b + 1, 1 - par, 4)
                            prep_stack(b + 1, 1 - par, 5)
                        if nxt2:
                            prep_stats(b + 2)
                    if w == 3:
                        if nxt:
                            value_low(b + 1, 1 - par)
                        if prev:
                            choose(0)
                    if w == 4:
                        if nxt2:
                            prep_xhat(b + 2)
                        if prev:
                            weigh(0, b - 1)
                            take_ranks(0, b - 1, rk_ps)
                            place(0, b - 1, 1 - par)

            prep_stats(0)
            prep_xhat(0)
            prep_stats(1)
            for j in range(2 * G):
                prep_stack(0, 0, j)
            value_low(0, 0)
            prep_xhat(1)
            for g in range(G):
                max_of(0, g)

            def counted(body, steps):
                start = ch.base + ch.n

                def one(b, i, par, nxt, nxt2):
                    if nxt:
                        ch.base, ch.n = start + steps * b, 0
                    body(b, i, par, nxt, nxt2)
                    assert not nxt2 or ch.n == steps, ch.n
                return one

            over_attention(dve, body, ch, DVE_STEPS)
            divide(B * NW - 1)
            residual(B - 1)
            residual_stats(B - 1)
            normalise(B - 1, B // 2 - 1, 1)
            take_logits(0, B - 1)
            choose(0)
            mark(0)
            weigh(0, B - 1)
            take_ranks(0, B - 1, rk_ps)
            place(0, B - 1, 1)
            tile_table(0)
            expert_tiles(0)
            output_rows(0)
            dve.wait_ge(expd_ready, 1)
            dve.tensor_tensor(decay_m[:, :], decay_m[:, :], causal, ALU.mult).then_inc(decay_ready, 1)
            dve.wait_ge(decay_ready, 1)
            over_batches(dve, counted(linear_body, DVE_STEPS_1))
            tile_table(1)
            expert_tiles(1)
            output_rows(1)
            over_batches(dve, counted(final_body, DVE_STEPS_2))

        @block.scalar
        def _(act):
            act.wait_ge(loaded, 16 * LOADS)

            def prep(b):
                act.wait_ge(xhat_turned, b + 1)
                nc.scalar.activation(xn_t[:, :], proj[0][:, :], ACT.Identity, bias=gb[:, 1:2],
                                     scale=gb[:, 0:1]).then_inc(xn_ready, 1)

            def half(b, j):
                act.wait_ge(proj_ready, 2 * G * b + j + 1)
                nc.scalar.copy(hi16[:, j % 2, :], proj[STACK_BANK[j]][:, :]).then_inc(half_ready, 1)

            def values(b, par):
                act.wait_ge(v_ready, 2 * b + 1)
                for w in range(4):
                    ins = nc.scalar.copy(v2[:, par, w, :, 0:HD],
                                         proj[1][:, w * P:w * P + P].rearrange("p (h d) -> p h d", h=H))
                ins.then_inc(v_high, 1)
                act.wait_ge(v_ready, 2 * b + 2)
                nc.scalar.copy(v2[:, par, 4, :, 0:HD],
                               proj[0][:, 0:P].rearrange("p (h d) -> p h d", h=H)).then_inc(v_high, 1)

            def keep_turned(win, w):
                lo, hi = QLO[w], QLO[w + 1]
                act.wait_ge(ao_turned, win + 1)
                nc.scalar.copy(ao_t[:, lo:hi], ao_ps[:, 0:NQ[w]]).then_inc(ao_copied, 1)

            def probs(win, w, g):
                act.wait_ge(st_ready, G * win + g + 1)
                if g >= 2:
                    act.wait_ge((low_even, low_odd)[g % 2], 2 * win + 1)
                width = 4 * NQ[w]
                nc.scalar.activation(prob[:, g % 2, 0:width], t_bank[g % 2][:, 0:width], ACT.Exp, scale=SCALE)
                nc.scalar.activation(prob_hi[:, g, 0:width], t_bank[g % 2][:, 0:width], ACT.Exp,
                                     scale=SCALE).then_inc(exp_done, 1)

            def copy_x1(b):
                act.wait_ge(x1_turned, b + 1)
                nc.scalar.copy(x1_t, proj[0][:, :]).then_inc(x1_copied, 1)

            def body(b, i, par, prev, nxt, nxt2):
                done = 0
                for w in range(NW):
                    win = b * NW + w
                    if w == 0 and nxt:
                        prep(b + 1)
                    if w in (2, 3) and nxt:
                        half(b + 1, 3 * w - 3)
                    if w == 4 and prev:
                        route(0, b - 1)
                    probs(win, w, 0)
                    probs(win, w, 1)
                    if w > 0 or prev:
                        keep_turned(win - 1, (w - 1) % NW)
                    if w in (0, 1, 3) and nxt:
                        half(b + 1, (0, 1, None, 7)[w])
                    if w == 2 and prev:
                        copy_x1(b - 1)
                    probs(win, w, 2)
                    probs(win, w, 3)
                    if w == 1 and nxt:
                        half(b + 1, 2)
                    if w == 2 and nxt:
                        half(b + 1, 4)
                        half(b + 1, 5)
                    if w == 3 and nxt:
                        values(b + 1, 1 - par)
                    for k in range(done, done + (2 if w >= 2 * NW - CPB else 1)):
                        act.wait_ge(raw_in[(par * CPB + k) % 2], 16 * (CPB * i + (par * CPB + k) // 2 + 1))
                        nc.scalar.copy(w_hi[:, bass.ds((b * CPB + k) * CH, CH)],
                                       w_raw[:, (par * CPB + k) % 2, :]).then_inc(hi_done, 1)
                        done = k + 1

            def route(n, b):
                act.wait_ge(d_ready[n], b + 1)
                nc.scalar.activation(etop[:, :, 0:top[n]], dtop[:, :, 0:top[n]], ACT.Exp).then_inc(e_ready[n], 1)

            def expert_tiles(n):
                def hi_of(j, par):
                    act.wait_ge(g_turned[n], j + 1)
                    nc.scalar.copy(xt_hi[:, par, :], xt_bank[:, 0:TILE]).then_inc(xhi_done[n], 1)

                def tile(j, par, first, last):
                    if not last:
                        hi_of(j + 1, 1 - par)
                    if n == 0:
                        e = act.value_load(table[0:1, bass.ds(j, 1)], min_val=0, max_val=E0 - 1)
                    act.wait_ge(split_done[n], 2 * j)
                    for c in range(NC_H):
                        if n == 0:
                            if c % 2 == 0:
                                act.wait_ge(h_ready[n], 2 * j + c // 2 + 1)
                            ins = nc.scalar.activation(
                                act_out[:, c, :], h_bank[2 * par + c // 2][:, (c % 2) * TILE:(c % 2 + 1) * TILE],
                                ACT.Gelu, bias=b1_sb[:, bass.ds(e * NC_H + c, 1)])
                            if c % 2 == 1:
                                ins.then_inc(act_done[n], 1)
                        else:
                            act.wait_ge(h_ready[n], NC_H * j + c + 1)
                            nc.scalar.activation(act_out[:, c, :], h_bank[c][:, 0:TILE],
                                                 ACT.Silu).then_inc(act_done[n], 1)

                act.wait_ge(table_kept[n], 1)
                hi_of(0, 0)
                over_tiles(act, n, tile)

            def linear_body(b, i, par, nxt, nxt2):
                act.wait_ge(x2_turned, b + 1)
                nc.scalar.copy(x2_t[:, 1:L + 1], xbank[:, :]).then_inc(x2_copied, 1)
                act.wait_ge(vv_ready, b + 1)
                nc.scalar.copy(vv[:, :, :].rearrange("p t d -> p (t d)"), v_bank[:, :]).then_inc(vv_copied, 1)
                act.wait_ge(x1_turned, B + b + 1)
                nc.scalar.copy(x1_t, xbank[:, :]).then_inc(x1_copied, 1)
                route(1, b)

            nc.scalar.activation(dexp[:, :], dec[:, 0:1], ACT.Exp, scale=-1.0).then_inc(gamma_ready, 1)
            nc.scalar.activation(alpha[:, :], dec[:, 1:2], ACT.Exp).then_inc(gamma_ready, 1)
            act.wait_ge(gamma_ready, 2)
            nc.scalar.activation(dlog[:, :], dexp[:, :], ACT.Ln, bias=1.0).then_inc(dlog_ready, 1)
            act.wait_ge(wc_ready, 1)
            nc.scalar.activation(wc[:, :], avbank[:, 0:D], ACT.Identity, scale=alpha[:, 0:1])
            act.wait_ge(init_done, 1)
            prep(0)
            for j in range(2 * G):
                half(0, j)
            values(0, 0)
            over_attention(act, body)
            keep_turned(B * NW - 1, NW - 1)
            copy_x1(B - 1)
            route(0, B - 1)
            expert_tiles(0)
            act.wait_ge(dlog_ready, 1)
            act.wait_ge(init_done, 2)
            nc.scalar.activation(decay_m[:, :], nmat, ACT.Exp, scale=dlog[:, 0:1]).then_inc(expd_ready, 1)
            over_batches(act, linear_body)
            expert_tiles(1)

        @block.tensor
        def _(pe):
            pe.wait_ge(loaded, 16 * LOADS)
            pe.wait_ge(keys_ready, 1)
            pe.wait_ge(init_done, 1)
            pe.matmul(rt_lg[:, 0, :], ones_f[:, :], keys2[:, :], start=True, stop=True).then_inc(routes_ready, 1)
            pe.matmul(avbank[:, 0:D], ww_sb[:, 0, :], ww_sb[:, 1, :], start=True, stop=True).then_inc(wc_ready, 1)

            def turn(b):
                pe.wait_ge(xhat_ready, b + 1)
                for t in range(T):
                    ins = pe.transpose(proj[0][:, t * P:(t + 1) * P], xh[:, t, :], ident)
                ins.then_inc(xhat_turned, 1)

            def stacks(b, j):
                if j >= 1:
                    pe.wait_ge(stack_ready, 2 * G * b + max(j - 1, 1) + (j == 4))
                src = (wqs if j < G else wks)[:, (j % G) * P:(j % G + 1) * P]
                pe.matmul(proj[STACK_BANK[j]][:, :], src, xn_t[:, :], start=True, stop=True).then_inc(proj_ready, 1)

            def values(b):
                pe.wait_ge(stack_ready, 2 * G * b + 7)
                for w in range(4):
                    ins = pe.matmul(proj[1][:, w * P:(w + 1) * P], xn_t[:, WIN[w]:WIN[w] + P], wv[:, :],
                                    start=True, stop=True)
                ins.then_inc(v_ready, 1)
                pe.wait_ge(stack_ready, 2 * G * b + 8)
                pe.matmul(proj[0][:, 0:P], xn_t[:, WIN[4]:WIN[4] + P], wv[:, :], start=True,
                          stop=True).then_inc(v_ready, 1)

            def scores(win, w, par, g, first=False):
                if not first or g >= 2:
                    pe.wait_ge(max_done, G * win + g - 1)
                bank, rows, at = s_bank[g % 2], slice(32 * g, 32 * g + 32), slice(WIN[w], WIN[w] + P)
                pe.matmul(bank[:, :], ident_b, band4, start=True, stop=True)
                for t in range(4):
                    ins = pe.matmul(bank[:, t * P:(t + 1) * P], qst[rows, par, t, at], kst[rows, par, t, at],
                                    start=False, stop=True, skip_group_check=True)
                ins.then_inc(s_ready, 1)

            def scores_t(win, w, par, g):
                if g >= 2:
                    pe.wait_ge(exp_done, G * win + g - 1)
                rows, nq, lo = slice(32 * g, 32 * g + 32), NQ[w], QLO[w]
                bank = t_bank[g % 2][:, 0:4 * nq].rearrange("p (t q) -> p t q", t=4)
                band = band4.rearrange("p (t q) -> p t q", t=4)[:, :, lo - WIN[w]:lo - WIN[w] + nq]
                pe.matmul(bank, ident_b, band, start=True, stop=True)
                for t in range(4):
                    pe.matmul(bank[:, t, :], kst[rows, par, t, WIN[w]:WIN[w] + P], qst[rows, par, t, lo:lo + nq],
                              start=False, stop=False, skip_group_check=True)
                for t in range(4):
                    ins = pe.matmul(bank[:, t, :], sel[:, 4 * g + t, :], nm_t[:, lo - WIN[w]:lo - WIN[w] + nq],
                                    start=False, stop=True, skip_group_check=True)
                ins.then_inc(st_ready, 1)

            def weighted(win, w, par, g):
                if g == 0 and not (w == 0 and type(win) is int and win == 0):
                    pe.wait_ge(ao_ready, win)
                pe.wait_ge((low_even, low_odd)[g % 2], 2 * win + g // 2 + 1)
                for t in range(4):
                    hi, lo = (x[:, g, t * NQ[w]:t * NQ[w] + P] for x in (prob_hi, prob_lo))
                    v = v2[:, par, w, 4 * t + g, :]
                    pe.matmul(av[:, g, t, :], hi, v[:, 0:V1], start=True, stop=True)
                    pe.matmul(av[:, g, t, 0:HD], hi, v[:, V1:V1 + HD], start=False, stop=True, skip_group_check=True)
                    ins = pe.matmul(av[:, g, t, :], lo, v[:, 0:V1], start=False, stop=True, skip_group_check=True)
                if g == G - 1:
                    ins.then_inc(av_ready, 1)

            def turn_out(win):
                pe.wait_ge(ao_ready, win + 1)
                pe.transpose(ao_ps, ao[:, :], ident).then_inc(ao_turned, 1)

            def project_out(b):
                pe.wait_ge(ao_copied, NW * (b + 1))
                for t in range(T):
                    ins = pe.matmul(proj[0][:, t * P:(t + 1) * P], ao_t[:, t * P:(t + 1) * P], wo[:, :],
                                    start=True, stop=True)
                ins.then_inc(o_ready, 1)

            def body(b, i, par, prev, nxt, nxt2):
                for w in range(NW):
                    win = b * NW + w
                    before = w > 0 or prev
                    pe.wait_ge(max_done, G * (win + 1))
                    if not (type(b) is int and win < 2):
                        pe.wait_ge(ao_copied, win - 1)
                    pe.transpose(nm_ps, nm[:, :], ident).then_inc(nm_ready, 1)
                    after = lambda g: None
                    if w < NW - 1:
                        after = lambda g: scores(win + 1, w + 1, par, g)
                    elif nxt:
                        pe.wait_ge(stack_ready, 2 * G * (b + 2))
                        after = lambda g: scores(win + 1, 0, 1 - par, g)
                    after(0)
                    last_of = (win - 1, (w - 1) % NW, par if w > 0 else 1 - par)
                    if before:
                        weighted(*last_of, 2)
                    after(1)
                    if before:
                        weighted(*last_of, 3)
                    if prev and w == 3:
                        logits(0, b - 1, lg_ps)
                    if w == 0 and nxt:
                        pe.wait_ge(v_copied, 2 * (b + 1))
                        turn(b + 1)
                    if w == 1 and prev:
                        if nxt:
                            pe.wait_ge(xn_ready, b + 2)
                        project_out(b - 1)
                    if w in (2, 3) and nxt:
                        stacks(b + 1, 3 * w - 3)
                    pe.wait_ge(nm_split, win + 1)
                    scores_t(win, w, par, 0)
                    after(2)
                    scores_t(win, w, par, 1)
                    if before:
                        turn_out(win - 1)
                    after(3)
                    if w == 0 and nxt:
                        pe.wait_ge(xn_ready, b + 2)
                        if prev == 2:
                            pe.wait_ge(rank_used[0], b - 1)
                        stacks(b + 1, 0)
                    if w == 1 and nxt:
                        stacks(b + 1, 1)
                    if w == 2 and prev:
                        if nxt:
                            pe.wait_ge(stack_ready, 2 * G * (b + 1) + 3)
                        turn_x1(b, 1 - par, proj[0])
                    if w == 3 and nxt:
                        stacks(b + 1, 7)
                    scores_t(win, w, par, 2)
                    weighted(win, w, par, 0)
                    scores_t(win, w, par, 3)
                    weighted(win, w, par, 1)
                    if w == 1 and nxt:
                        if prev:
                            pe.wait_ge(y_ready, b)
                        stacks(b + 1, 2)
                    if w == 2 and nxt:
                        stacks(b + 1, 4)
                        if prev:
                            pe.wait_ge(x1_copied, b)
                        stacks(b + 1, 5)
                    if w == 3 and nxt:
                        values(b + 1)
                    if w == 4 and prev:
                        if nxt:
                            pe.wait_ge(v_copied, 2 * (b + 2))
                        ranks(0, b - 1, rk_ps)

            def turn_x1(count, par, bank):
                pe.wait_ge(x1_ready, count)
                for t in range(T):
                    ins = pe.transpose(bank[:, t * P:(t + 1) * P], x1w[:, par, t, :], ident)
                ins.then_inc(x1_turned, 1)

            def logits(n, b, dst):
                pe.wait_ge(x1_copied, B * n + b + 1)
                for t in range(T):
                    ins = pe.matmul(dst[:, t, 0:experts[n]], x1_t[:, t * P:(t + 1) * P], (g_route, wr_sb)[n][:, :],
                                    start=True, stop=True)
                ins.then_inc(lg_ready[n], 1)

            def ranks(n, b, dst):
                e_n = experts[n]
                pe.wait_ge(mask_ready[n], b + 1)
                if not (type(b) is int and b == 0):
                    pe.wait_ge(carry_ready[n], b)
                dst, mk = dst[:, :, 0:e_n], mask[:, :, 0:e_n]
                pe.matmul(dst, tri, mk, start=True, stop=True)
                for t in range(T - 1):
                    pe.matmul(dst[:, t + 1:T, :], ones_b, bc(mk[:, t, :], 1, T - 1 - t), start=False,
                              stop=True, skip_group_check=True)
                pe.matmul(dst, ones_b, bc(carry_b[n][:, :], 1, T), start=False, stop=True,
                          skip_group_check=True).then_inc(rank_ready[n], 1)

            def tile_table(n):
                pe.wait_ge(carry_ready[n], B)
                pe.wait_ge(rank_used[n], B)
                pe.matmul(xbank[:, 0:experts[n]], ones_b, carry_b[n][:, :], start=True, stop=True).then_inc(cnt_ready[n], 1)
                pe.wait_ge(table_ready[n], 1)
                for c in range(2):
                    pe.transpose(xbank[0:1, c * P:(c + 1) * P], tile_e[:, 4 + c:5 + c], ident)
                ins = pe.matmul(xbank[0:1, 2 * P:2 * P + 1], tile_e[:, 3:4], even, start=True, stop=True)
                ins.then_inc(table_turned[n], 1)
                pe.wait_ge(table_kept[n], 1)

            def expert_tiles(n):
                def turn_rows(j, par):
                    pe.wait_ge(xg_loaded[n][par], 8 * (j - par) + 16)
                    pe.wait_ge(xlo_done[n], j)
                    for k in range(S2):
                        ins = pe.transpose(xt_bank[:, k * P:(k + 1) * P], xg[:, par, k, :], ident)
                    ins.then_inc(g_turned[n], 1)

                def hidden_chunk(dst, w_at, e, c, par):
                    at = e * HID + (w_at + c * P)
                    w_h, w_l = w_hi[:, bass.ds(at, P)], w_lo[:, bass.ds(at, P)]
                    pe.matmul(dst, w_h, xt_hi[:, par, :], start=True, stop=False)
                    pe.matmul(dst, w_h, xt_lo[:, par, :], start=False, stop=False)
                    return pe.matmul(dst, w_l, xt_hi[:, par, :], start=False, stop=True)

                def outputs(j, par, e):
                    pe.wait_ge(y_done[n], j)
                    for half in range(2):
                        pe.wait_ge(split_done[n], 2 * j + half + 1)
                        for k in range(S2):
                            dst, rows = y_bank[par][:, k * D:(k + 1) * D], slice(k * P, (k + 1) * P)
                            for c in (2 * half, 2 * half + 1):
                                at = e * HID + ((W2_AT, WD_AT)[n] + c * D)
                                w_h, w_l = w_hi[:, bass.ds(at, D)], w_lo[:, bass.ds(at, D)]
                                for m, (x, w) in enumerate(((h_hi, w_h), (h_hi, w_l), (h_lo, w_h))):
                                    ins = pe.matmul(dst, x[:, par, c, rows], w, start=(c == 0 and m == 0 and k == 0),
                                                    stop=True, skip_group_check=True)
                    ins.then_inc(yp_ready[n], 1)

                def expert_of(j):
                    return pe.value_load(table[0:1, bass.ds(j, 1)], min_val=0, max_val=experts[n] - 1)

                def tile(j, par, first, last):
                    if not last:
                        turn_rows(j + 1, 1 - par)
                    e = expert_of(j)
                    pe.wait_ge(xlo_done[n], j + 1)
                    for c in range(NC_H):
                        if n == 0:
                            ins = hidden_chunk(h_bank[2 * par + c // 2][:, (c % 2) * TILE:(c % 2 + 1) * TILE], W1_AT, e, c, par)
                            if c % 2 == 1:
                                ins.then_inc(h_ready[n], 1)
                        else:
                            pe.wait_ge(split_done[n], 2 * j)
                            hidden_chunk(h_bank[c][:, 0:TILE], WG_AT, e, c, par)
                            hidden_chunk(h_bank[c][:, TILE:2 * TILE], WU_AT, e, c, par).then_inc(h_ready[n], 1)
                    if not first:
                        outputs(j - 1, 1 - par, expert_of(j - 1))

                turn_rows(0, 0)
                last_tile = over_tiles(pe, n, tile)
                outputs(last_tile, 1, expert_of(last_tile))

            def linear_body(b, i, par, nxt, nxt2):
                pe.wait_ge(x2_ready, b + 1)
                pe.wait_ge(rank_used[1], b)
                for t in range(T):
                    ins = pe.transpose(xbank[:, t * P:(t + 1) * P], x2w[:, t, :], ident)
                ins.then_inc(x2_turned, 1)
                pe.wait_ge(x2_copied, b + 1)
                for e in range(T):
                    if e == 2:
                        for t in range(T):
                            ins = pe.matmul(v_bank[:, t * D:(t + 1) * D], x2_t[:, 1 + t * P:1 + (t + 1) * P], wc[:, :],
                                            start=True, stop=True)
                        ins.then_inc(vv_ready, 1)
                    if e >= 2:
                        pe.wait_ge(decayed, T * b + e - 1)
                    pe.matmul(ws_bank[e % 2][:, 0:L - e * P], x2_t[:, e * P:(e + 1) * P], x2_t[:, 1 + e * P:1 + L],
                              start=True, stop=True).then_inc(ws_ready, 1)
                pe.wait_ge(vv_copied, b + 1)
                for c in range(T):
                    pe.wait_ge(decayed, T * b + c + 1)
                    for e in range(c + 1):
                        ins = pe.matmul(r_bank[:, c * P:(c + 1) * P], pm[:, e, (c - e) * P:(c - e + 1) * P],
                                        vv[:, e, :], start=e == 0, stop=e == c)
                ins.then_inc(reads_ready, 1)
                turn_x1(B + b + 1, par, xbank)
                logits(1, b, rt_lg)
                ranks(1, b, rank_ps)

            turn(0)
            pe.wait_ge(xn_ready, 1)
            for j in range(2 * G):
                stacks(0, j)
            values(0)
            for g in range(G):
                scores(0, 0, 0, g, first=True)
            over_attention(pe, body)
            last_of = (B * NW - 1, NW - 1, 1)
            weighted(*last_of, 2)
            weighted(*last_of, 3)
            turn_out(B * NW - 1)
            project_out(B - 1)
            turn_x1(B, 1, proj[0])
            logits(0, B - 1, lg_ps)
            ranks(0, B - 1, rk_ps)
            tile_table(0)
            expert_tiles(0)
            over_batches(pe, linear_body)
            tile_table(1)
            expert_tiles(1)


def constants():
    import numpy as np

    row = np.arange(P)
    cf = np.zeros((P, C_COLS), np.float32)
    cf[:, C_IDENT:C_IDENT + P] = np.eye(P)
    part = row % 32 // HD
    cf[:, C_NEG] = -1.0 * (part >= 2)
    cf[:, C_NEG + 1] = -1.0 * (part % 2)
    cf[:, C_IOTA:C_IOTA + E0] = np.arange(E0)
    cf[:, C_BASE:C_BASE + E0] = REGION * np.arange(E0)
    cf[:, C_NHALF:C_NHALF + T] = -0.5
    cf[:, C_ROW] = row
    lag = np.arange(L)[None, :] - 1 - row[:, None]
    cf[:, C_NMAT:C_NMAT + L] = -np.maximum(lag, 0)
    cf[:, C_CAUSAL:C_CAUSAL + L] = lag >= 0
    cf[:, C_EVEN] = (row % 2 == 0) & (row > 0)
    cf[:, C_STEP:C_STEP + E0] = TILE * np.arange(E0)
    cb = np.zeros((P, CB_COLS), np.float32)
    cb[:, CB_IDENT:CB_IDENT + P] = np.eye(P)
    cb[:, CB_TRI:CB_TRI + P] = row[:, None] < row[None, :]
    cb[:, CB_ONES:CB_ONES + P] = 1
    cb[:, CB_BAND:CB_BAND + 4 * P] = np.tile(np.where(abs(row[:, None] - row[None, :]) <= HALF, 0, NEG), 4)
    s = np.zeros((P, H, P), np.float32)
    for c in range(H):
        s[c, c] = s[32 + c, c] = 1
    cb[:, CB_SEL:] = s.reshape(P, H * P)
    return cf, cb.astype(mybir.dt.np(BF16))


def kernel(**inputs):
    import numpy as np
    import concourse.bacc as bacc
    from concourse.bass_utils import run_bass_kernel_spmd

    a = {k: np.asarray(v) for k, v in inputs.items()}
    wqkv = a["L0_attn_w_qkv"]

    def stacked(w):
        w = w.reshape(4, G, 1, HD, D)
        return np.broadcast_to(w, (4, G, 4, HD, D)).reshape(512, D).T

    w1 = a["L0_ffn_w1"].transpose(2, 0, 1).reshape(D, E0 * HID)
    w2 = a["L0_ffn_w2"].reshape(E0, D, NC_H, P).transpose(3, 0, 2, 1).reshape(P, E0 * HID)
    wg = a["L1_ffn_Wg"].transpose(1, 0, 2).reshape(D, E1 * HID)
    wu = a["L1_ffn_Wu"].transpose(1, 0, 2).reshape(D, E1 * HID)
    wd = a["L1_ffn_Wd"].reshape(E1, NC_H, P, D).transpose(2, 0, 1, 3).reshape(P, E1 * HID)
    cf, cb = constants()
    arrays = {
        "x_in": a["L0_attn_x"],
        "w_all": np.concatenate([w1, w2, wg, wu, wd], 1),
        "wq_s": stacked(wqkv[:D]),
        "wk_s": stacked(wqkv[D:2 * D]),
        "wv_t": wqkv[2 * D:].T,
        "wo_t": a["L0_attn_w_out"].T,
        "gamma": a["L0_attn_gamma"].reshape(D, 1),
        "beta": a["L0_attn_beta"].reshape(D, 1),
        "keys_t": a["L0_ffn_keys"].T,
        "rw_t": a["L0_ffn_rw"].T,
        "rb": a["L0_ffn_rb"].reshape(1, E0),
        "b1": a["L0_ffn_b1"].reshape(E0, NC_H, P).transpose(2, 0, 1).reshape(P, E0 * NC_H),
        "b2": a["L0_ffn_b2"].reshape(1, E0 * D),
        "w_write": a["L1_attn_W_write"],
        "w_read_t": a["L1_attn_W_read"].T,
        "decay": a["L1_attn_decay"].reshape(1, 1),
        "log_alpha": a["L1_attn_log_alpha"].reshape(1, 1),
        "wr": a["L1_ffn_Wr"],
        "const": cf,
        "const_b": cb,
    }
    arrays = {k: np.ascontiguousarray(v) for k, v in arrays.items()}
    nc = bacc.Bacc("TRN2", target_bir_lowering=False, num_devices=1)
    args = [nc.dram_tensor(k, v.shape, mybir.dt.from_np(v.dtype), kind="ExternalInput").ap()
            for k, v in arrays.items()]
    out = nc.dram_tensor("out", (B, L, D), F32, kind="ExternalOutput").ap()
    program(nc, *args, out)
    return run_bass_kernel_spmd(nc, [arrays], core_ids=[0]).results[0]["out"]
```

```python
from contextlib import ExitStack

import concourse.bass as bass
from concourse import mybir

F32 = mybir.dt.float32
BF16 = mybir.dt.bfloat16
U32 = mybir.dt.uint32
I32 = mybir.dt.int32
ALU = mybir.AluOpType
ACT = mybir.ActivationFunctionType
AX = mybir.AxisListType.X

P = 128
D = 128
B, L = 8, 512
T = L // P
NT = B * T
H, HD = 16, 8
HALF = 16
G = 4
WIN = [0, 96, 192, 288, 384]
QLO = [0, 112, 208, 304, 400, 512]
NW = len(WIN)
NQ = [QLO[w + 1] - QLO[w] for w in range(NW)]
V1 = HD + 1
EPS = 1e-5
NEG = -1.0e30
TILE = 256
S2 = TILE // P
HID = 512
NC_H = HID // P
CH = 512
E0, K0 = 16, 4
E1, K1 = 8, 2
REGION = B * L + TILE
W_COLS = 2 * E0 * HID + 3 * E1 * HID
CHUNKS = W_COLS // CH
CPB = CHUNKS // B
W1_AT, W2_AT = 0, E0 * HID
WG_AT = 2 * E0 * HID
WU_AT = WG_AT + E1 * HID
WD_AT = WU_AT + E1 * HID
SCALE = float(HD) ** -0.5
DEPTH_SCALE = 12.0 ** -0.5
DVE_STEPS = 26
STACK_BANK = [1, 1, 0, 1, 1, 0, 1, 0]
DVE_STEPS_1 = 21
DVE_STEPS_2 = 4


C_IDENT, C_NEG, C_IOTA, C_BASE, C_NHALF, C_ROW, C_STEP = 0, 128, 130, 146, 162, 166, 167
C_NMAT, C_CAUSAL = 183, 183 + L
C_EVEN = C_CAUSAL + L
C_COLS = C_EVEN + 1
CB_IDENT, CB_TRI, CB_ONES, CB_BAND, CB_SEL = 0, 128, 256, 384, 896
CB_COLS = CB_SEL + H * P


def max_tiles(experts, k):
    n = (B * L * k + experts * (TILE - 1)) // TILE
    return n + n % 2


PAIRS = max_tiles(E0, K0) // 2


class Chain:

    def __init__(self, eng, sem, base=0):
        self.eng, self.sem, self.base, self.n = eng, sem, base, 0

    def link(self, ins):
        ins.then_inc(self.sem, 1)
        self.n += 1
        self.eng.wait_ge(self.sem, self.base + self.n)
        return ins

    def mark(self, ins):
        ins.then_inc(self.sem, 1)
        self.n += 1
        return self.n

    def wait(self, n):
        self.eng.wait_ge(self.sem, self.base + n)


def bc(ap, axis, n):
    ap = ap.unsqueeze(axis)
    shape = list(ap.shape)
    shape[axis] = n
    return ap.to_broadcast(shape)



def program(nc, x_in, w_all, wq_s, wk_s, wv_t, wo_t, gamma, beta, keys_t, rw_t, rb, b1, b2,
            w_write, w_read_t, decay, log_alpha, wr, const, const_b, out):
    ctx = ExitStack()
    with ctx:
        scope = ctx

        def sb(name, shape, dt=F32):
            return scope.enter_context(nc.sbuf_tensor(name, shape, dt))

        def pb(name):
            return ctx.enter_context(nc.psum_tensor(name, [P, 512], F32))

        def sem(name):
            return ctx.enter_context(nc.semaphore(name))

        cf = sb("cf", [P, C_COLS])
        cb = sb("cb", [P, CB_COLS], BF16)
        ident = cf[:, C_IDENT:C_IDENT + P]
        neg_low = cf[:, C_NEG:C_NEG + 2]
        iota_e = cf[:, C_IOTA:C_IOTA + E0]
        base_e = cf[:, C_BASE:C_BASE + E0]
        nhalf = cf[:, C_NHALF:C_NHALF + T]
        ident_b = cb[:, CB_IDENT:CB_IDENT + P]
        tri = cb[:, CB_TRI:CB_TRI + P]
        ones_b = cb[:, CB_ONES:CB_ONES + P]
        band4 = cb[:, CB_BAND:CB_BAND + 4 * P]
        sel = cb[:, CB_SEL:CB_SEL + H * P].rearrange("p (c k) -> p c k", c=H)
        row_no = cf[:, C_ROW:C_ROW + 1]
        steps = cf[:, C_STEP:C_STEP + E0]
        nmat = cf[:, C_NMAT:C_NMAT + L]
        even = cf[:, C_EVEN:C_EVEN + 1]
        causal = cf[:, C_CAUSAL:C_CAUSAL + L]
        w_hi = sb("w_hi", [P, W_COLS], BF16)
        w_lo = sb("w_lo", [P, W_COLS], BF16)
        w_raw = sb("w_raw", [P, 2, CH])
        wqs = sb("wqs", [P, 512])
        wks = sb("wks", [P, 512])
        wv = sb("wv", [P, P])
        wo = sb("wo", [P, P])
        gb = sb("gb", [P, 2])
        keys_sb = sb("keys_sb", [P, 2, E0])
        keys2 = sb("keys2", [P, E0])
        ones_f = sb("ones_f", [P, P])
        g_route = sb("g_route", [P, E0])
        rb_sb = sb("rb_sb", [P, E0])
        c_route = sb("c_route", [P, E0])

        b1_sb = sb("b1_sb", [P, E0 * NC_H])
        wr_sb = sb("wr_sb", [P, E1])
        ww_sb = sb("ww_sb", [P, 2, D])
        dec = sb("dec", [P, 2])
        dexp = sb("dexp", [P, 1])
        dlog = sb("dlog", [P, 1])
        alpha = sb("alpha", [P, 1])
        wc = sb("wc", [P, D])
        zeros = sb("zeros", [P, S2 * D])

        xres = sb("xres", [P, NT, D])
        sres = [sb("sres0", [P, NT, K0]), sb("sres1", [P, NT, K1])]
        eres = [sb("eres0", [P, NT, K0]), sb("eres1", [P, NT, K1])]
        gres = [sb("gres0", [P, NT, K0], U32), sb("gres1", [P, NT, K1], U32)]
        wres = sb("wres", [P, NT, K0])
        carry = [sb("carry0", [P, E0]), sb("carry1", [P, E1])]
        carry_b = [sb("carry0_b", [P, E0], BF16), sb("carry1_b", [P, E1], BF16)]
        y = sb("y", [P, T, D])
        stat2 = sb("stat2", [P, T, 6])
        mv2 = sb("mv2", [P, T, 2])
        ve2 = sb("ve2", [P, T])
        rstd2 = sb("rstd2", [P, T])
        x1w = sb("x1w", [P, 2, T, D])
        x1_t = y[:, :, :].rearrange("p t d -> p (t d)")
        lg = sb("lg", [P, T, E0])
        mx8 = sb("mx8", [P, T, 8])
        ix8 = sb("ix8", [P, T, 8], U32)
        dtop = sb("dtop", [P, T, K0])
        etop = sb("etop", [P, T, K0])
        ssum = sb("ssum", [P, T])
        rsum = sb("rsum", [P, T])
        idf = sb("idf", [P, T, K0])
        oneh = sb("oneh", [P, T, K0, E0])
        mask = sb("mask", [P, T, E0], BF16)
        msum = sb("msum", [P, E0])
        r2 = sb("r2", [P, T, E0])
        pr = sb("pr", [P, T, K0, E0])
        slf = sb("slf", [P, T * K0])
        sidx = sb("sidx", [P, 2, T * K0], U32)
        cnt = sb("cnt", [P, E0])
        over = pr[:, :, :, :].rearrange("p t k e -> p (t k) e")
        ntile = sb("ntile", [P, E0])
        ntile_sum = sb("ntile_sum", [P, E0])
        past = sb("past", [P, E0])
        past_n = sb("past_n", [P, E0])
        tile_e = sb("tile_e", [P, 8])
        shift = sb("shift", [P, E0])
        table = sb("table", [1, 2 * PAIRS + 3], I32)
        quads = sb("quads", [1, PAIRS, 4], I32)
        tails = sb("tails", [1, E0], I32)

        scope = ExitStack()
        stat = sb("stat", [P, T, 6])
        mv = sb("mv", [P, T, 2])
        ve = sb("ve", [P, T])
        rstd = sb("rstd", [P, T])
        xh = sb("xh", [P, T, D])
        xn_t = sb("xn_t", [P, L])
        hi16 = sb("hi16", [P, 2, L], BF16)
        qst = sb("qst", [P, 2, G, L], BF16)
        kst = sb("kst", [P, 2, G, L], BF16)
        v2 = sb("v2", [P, 2, NW, H, V1 + HD], BF16)
        nm = sb("nm", [P, H])
        nm_t = sb("nm_t", [P, P], BF16)
        prob = sb("prob", [P, 2, 4 * P])
        prob_hi = sb("prob_hi", [P, G, 4 * P], BF16)
        prob_lo = sb("prob_lo", [P, G, 4 * P], BF16)
        rden = sb("rden", [P, G, 4])
        ao = sb("ao", [P, D])
        ao_t = sb("ao_t", [P, L])
        scope.close()

        scope = ExitStack()
        choice = sb("choice", [P, NT * K0, E0])
        xg = sb("xg", [P, 2, S2, D])
        xt_hi = sb("xt_hi", [P, 2, TILE], BF16)
        xt_lo = sb("xt_lo", [P, 2, TILE], BF16)
        act_out = sb("act_out", [P, NC_H, TILE])
        hid = sb("hid", [P, NC_H, TILE])
        h_hi = sb("h_hi", [P, 2, NC_H, TILE], BF16)
        h_lo = sb("h_lo", [P, 2, NC_H, TILE], BF16)
        ysb = sb("ysb", [P, 2, S2, D])
        b2_sb = sb("b2_sb", [P, E0, D])
        scope.close()

        scope = ExitStack()
        gat = sb("gat", [P, 2, T, K0, D])
        gidx = sb("gidx", [P, 2, T * K0], U32)
        wsel = sb("wsel", [P, T, K0])
        x2w = sb("x2w", [P, T, D])
        y3 = sb("y3", [P, T, D])
        stat3 = sb("stat3", [P, T, 6])
        mv3 = sb("mv3", [P, T, 2])
        ve3 = sb("ve3", [P, T])
        rstd3 = sb("rstd3", [P, T])
        x2_t = sb("x2_t", [P, L + 1])
        vv = sb("vv", [P, T, D])
        pm = sb("pm", [P, T, L])
        decay_m = sb("decay_m", [P, L])
        ow = sb("ow", [P, 2, T, D])
        scope.close()

        s_bank = [pb("s0"), pb("s1")]
        t_bank = [pb("t0"), pb("t1")]
        avbank = pb("avbank")
        proj = [pb("proj0"), pb("proj1")]
        xbank = pb("xbank")
        av = avbank[:, 0:H * V1].rearrange("p (i t v) -> p i t v", i=G, t=4)
        lg_ps = avbank[:, 192:192 + T * E0].rearrange("p (t e) -> p t e", t=T)
        rk_ps = avbank[:, 320:320 + T * E0].rearrange("p (t e) -> p t e", t=T)
        rt_lg = xbank[:, 64:64 + T * E0].rearrange("p (t e) -> p t e", t=T)
        nm_ps = xbank[0:H, 256:384]
        ao_ps = xbank[:, 384:512]
        rank_ps = xbank[:, 0:T * E0].rearrange("p (t e) -> p t e", t=T)

        xt_bank, h_bank, y_bank = xbank, s_bank + t_bank, [avbank, proj[0]]
        v_bank, ws_bank, r_bank = avbank, t_bank, proj[0]

        tiles = [max_tiles(E0, K0), max_tiles(E1, K1)]
        experts = [E0, E1]
        top = [K0, K1]
        xs = [nc.dram_tensor(f"xs{n}", [experts[n] * REGION, D], F32).ap() for n in range(2)]
        ys = [nc.dram_tensor(f"ys{n}", [(tiles[n] + 2) * TILE, D], F32).ap() for n in range(2)]

        (loaded, loaded_act, loaded_later, hi_done, lo_done, pool_step, dve_step, routes_ready, init_done, var_ready, rstd_ready, v_high, low_even, low_odd, gated, gated_high,
         xhat_ready, xhat_turned, xn_ready, proj_ready, half_ready, stack_ready, v_ready, v_copied,
         s_ready, max_done, nm_ready, nm_split, st_ready, exp_done, av_ready, ao_ready, ao_turned,
         ao_copied, o_ready, y_ready, var2_ready, rstd2_ready, x1_ready, x1_turned, x1_copied, x1_kept,
         stored, keys_ready, wc_ready, gamma_ready, decay_ready, expd_ready,
         y2_ready, var3_ready, rstd3_ready, x2_ready, x2_turned, x2_copied, vv_ready, vv_copied,
         ws_ready, decayed, reads_ready, y3_ready, comb_done, out_ready, yf_ready, dlog_ready) = [
            sem(n) for n in (
                "loaded loaded_act loaded_later hi_done lo_done pool_step dve_step routes_ready init_done var_ready rstd_ready v_high low_even low_odd gated gated_high "
                "xhat_ready xhat_turned xn_ready proj_ready half_ready stack_ready v_ready v_copied "
                "s_ready max_done nm_ready nm_split st_ready exp_done av_ready ao_ready ao_turned "
                "ao_copied o_ready y_ready var2_ready rstd2_ready x1_ready x1_turned x1_copied x1_kept "
                "stored keys_ready wc_ready gamma_ready decay_ready expd_ready "
                "y2_ready var3_ready rstd3_ready x2_ready x2_turned x2_copied vv_ready vv_copied "
                "ws_ready decayed reads_ready y3_ready comb_done out_ready yf_ready dlog_ready").split()]

        def pair_of(name):
            return [sem(name + "0"), sem(name + "1")]

        (lg_ready, d_ready, e_ready, mask_ready, rank_ready, rank_used, slots_ready, carry_ready, cnt_ready,
         table_ready, table_turned, table_kept, tails_ready, tails_stored, g_turned, xhi_done, xlo_done,
         h_ready, act_done, split_done, yp_ready, y_done, tile_step, rows_ready, slot_settled) = [
            pair_of(n) for n in (
                "lg_ready d_ready e_ready mask_ready rank_ready rank_used slots_ready carry_ready cnt_ready "
                "table_ready table_turned table_kept tails_ready tails_stored g_turned xhi_done xlo_done "
                "h_ready act_done split_done yp_ready y_done tile_step rows_ready slot_settled").split()]
        xg_loaded = [pair_of("xg_loaded0_"), pair_of("xg_loaded1_")]
        y_stored = [pair_of("y_stored0_"), pair_of("y_stored1_")]
        gathered = [pair_of("gathered0_"), pair_of("gathered1_")]
        scattered1 = pair_of("scattered1_")
        o_stored = pair_of("o_stored")
        raw_in = [sem("raw_in0"), sem("raw_in1")]
        scattered = [sem("scattered0"), sem("scattered1")]

        x_tiles = x_in.rearrange("b (t p) d -> p (b t) d", p=P)

        def tile_rounds(j, par):
            return 8 * (j - par)

        def more_pairs(eng, n):
            return eng.value_load(table[0:1, 2 * PAIRS + 2:2 * PAIRS + 3], min_val=B * L * top[n] // (2 * TILE) - 1,
                                  max_val=tiles[n] // 2 - 1)

        def experts_of(eng, n, p, count):
            which = {nc.tensor: mybir.EngineType.PE, nc.vector: mybir.EngineType.DVE,
                     nc.scalar: mybir.EngineType.Activation}[eng]
            _, values = nc.values_load_multi_w_load_instructions(
                quads[0:1, bass.ds(p, 1), 0:count], engines=(which,), min_val=0, max_val=experts[n] - 1,
                skip_runtime_bounds_check_because="the tile table names this layer's experts")
            return values

        def over_tiles(eng, n, tile, ch=None, steps=0, use=True):
            more = more_pairs(eng, n)
            last_tile = 2 * more + 1

            def one(j, par, first, last, e_before, e):
                if ch:
                    ch.base, ch.n = steps * j, 0
                tile(j, par, first, last, e_before, e)
                assert not ch or ch.n == steps, ch.n

            def load(p, count):
                return experts_of(eng, n, p, count) if use else (None,) * count
            one(0, 0, True, False, None, load(0, 1)[0])
            with eng.Fori(0, more) as p:
                e0, e1, e2 = load(p, 3)
                one(2 * p + 1, 1, False, False, e0, e1)
                one(2 * p + 2, 0, False, False, e1, e2)
            e0, e1 = load(more, 2)
            one(last_tile, 1, False, True, e0, e1)
            return last_tile, e1

        def over_batches(eng, body):
            with eng.Fori(0, B // 2 - 1) as i:
                body(2 * i, i, 0, True, True)
                body(2 * i + 1, i, 1, True, True)
            body(B - 2, B // 2 - 1, 0, True, False)
            body(B - 1, B // 2 - 1, 1, False, False)

        def over_attention(eng, body, ch=None, steps=0):
            body(0, 0, 0, 0, True, True)
            body(1, 0, 1, 1, True, True)
            start = ch.base + ch.n if ch else 0

            def one(b, i, par):
                if ch:
                    ch.base, ch.n = start + steps * (b - 2), 0
                body(b, i, par, 2, True, True)
                assert not ch or ch.n == steps, ch.n
            with eng.Fori(0, B // 2 - 2) as j:
                one(2 * j + 2, j + 1, 0)
                one(2 * j + 3, j + 1, 1)
            body(B - 2, B // 2 - 1, 0, 2, True, False)
            body(B - 1, B // 2 - 1, 1, 2, False, False)

        LOADS, LOADS_ACT, LOADS_LATER = 11, 4, 5

        def apart(eng):
            eng.nop(nofuse=True)

        block = ctx.enter_context(nc.Block())

        @block.sync
        def _(sp):
            for dst, src in [(xres[:, 0:T, :], x_tiles[:, 0:T, :]), (cf[:, 0:C_NMAT], const[:, 0:C_NMAT]),
                             (keys_sb[:, 0, :], keys_t), (keys_sb[:, 1, :], rw_t), (gb[:, 0:1], gamma),
                             (gb[:, 1:2], beta), (rb_sb[:, :], rb.to_broadcast([P, E0])),
                             (ww_sb[:, 0, :], w_write), (ww_sb[:, 1, :], w_read_t),
                             (dec[:, 0:1], decay.to_broadcast([P, 1])),
                             (dec[:, 1:2], log_alpha.to_broadcast([P, 1]))]:
                sp.dma_start(dst, src).then_inc(loaded, 16)
            for dst, src in [(xres[:, T:NT, :], x_tiles[:, T:NT, :]), (wo[:, :], wo_t), (b1_sb[:, :], b1),
                             (wr_sb[:, :], wr), (cf[:, C_NMAT:C_COLS], const[:, C_NMAT:C_COLS])]:
                sp.dma_start(dst, src).then_inc(loaded_later, 16)

            for k in range(2):
                sp.dma_start(w_raw[:, k, :], w_all[:, k * CH:(k + 1) * CH]).then_inc(raw_in[k], 16)
            with sp.Fori(1, CHUNKS // 2) as c:
                for k in range(2):
                    sp.wait_ge(lo_done, 2 * c + k - 1)
                    sp.dma_start(w_raw[:, k, :], w_all[:, bass.ds((2 * c + k) * CH, CH)]).then_inc(raw_in[k], 16)
            def fill_tails(n):
                sp.wait_ge(tails_ready[n], 1)
                for e in range(experts[n]):
                    row = sp.value_load(tails[0:1, e:e + 1], min_val=e * REGION, max_val=e * REGION + B * L)
                    sp.dma_start(xs[n][bass.ds(row, TILE), :].rearrange("(p s) d -> p (s d)", s=S2),
                                 zeros[:, :]).then_inc(tails_stored[n], 16)
                sp.wait_ge(tails_stored[n], 16 * experts[n])
                for par in range(2):
                    sp.wait_ge((scattered, scattered1)[n][par], 8 * B * T * top[n])

            def expert_tiles(n):
                def load(j, par):
                    row = sp.value_load(table[0:1, bass.ds(j, 1)], min_val=0, max_val=experts[n] * REGION - TILE)
                    sp.dma_start(xg[:, par, :, :].rearrange("p s d -> p (s d)"),
                                 xs[n][bass.ds(row, TILE), :].rearrange("(p s) d -> p (s d)", s=S2)
                                 ).then_inc(xg_loaded[n][par], 16)

                def tile(j, par, first, last, e_before, e):
                    if not last:
                        sp.wait_ge(g_turned[n], j + 1)
                        load(j + 2, par)

                sp.wait_ge(table_kept[n], 1)
                load(0, 0)
                load(1, 1)
                over_tiles(sp, n, tile, use=False)
                with sp.Fori(more_pairs(sp, n) + 1, tiles[n] // 2 + 1) as p:
                    for par in range(2):
                        sp.dma_start(ys[n][bass.ds((2 * p + par) * TILE, TILE), :].rearrange("(p s) d -> p (s d)", s=S2),
                                     zeros[:, :]).then_inc(slot_settled[n], 16)

            sp.wait_ge(x1_ready, B)
            sp.dma_start(b2_sb[:, :, :].rearrange("p e d -> p (e d)"), b2.to_broadcast([P, E0 * D])).then_inc(loaded, 16)
            fill_tails(0)
            expert_tiles(0)
            fill_tails(1)
            expert_tiles(1)
            for b in range(B):
                sp.wait_ge(out_ready, b + 1)
                sp.dma_start(out[b].rearrange("(t p) d -> p t d", p=P), ow[:, b % 2, :, :]).then_inc(o_stored[b % 2], 16)
            for par in range(2):
                sp.wait_ge(o_stored[par], 8 * B)

        @block.gpsimd
        def _(pool):
            pool.memset(nm_t[:, :], 0.0)
            pool.memset(prob_hi[:, :, :], 1.0)
            pool.memset(prob_lo[:, :, :], 0.0)
            for n in range(2):
                pool.memset(carry[n][:, :], 0.0)
                pool.memset(carry_b[n][:, :], 0.0)
            pool.memset(zeros[:, :], 0.0)
            pool.memset(ones_f[:, :], 1.0)
            pool.memset(v2[:, :, :, :, HD:V1], 1.0).then_inc(init_done, 1)
            pool.wait_ge(loaded, 16 * LOADS)

            def rstd_of(b):
                pool.wait_ge(var_ready, b + 1)
                pool.tensor_tensor(rstd[:, :], ve[:, :], nhalf, ALU.pow).then_inc(rstd_ready, 1)

            def low_of(win, w, g):
                pool.wait_ge(exp_done, G * win + g + 1)
                width = 4 * NQ[w]
                pool.tensor_tensor(prob_lo[:, g, 0:width], prob[:, g % 2, 0:width], prob_hi[:, g, 0:width],
                                   ALU.subtract).then_inc(low_odd, 1)

            def body(b, i, par, prev, nxt, nxt2):
                done = 0
                for w in range(NW):
                    low_of(b * NW + w, w, 1)
                    if prev == 2 and w > 0:
                        if w == 1:
                            pool.wait_ge(slots_ready[0], b - 1)
                            apart(pool)
                        scatter(0, par, w - 1, range(0, K0 // 2))
                    if w == 3 and nxt2:
                        rstd_of(b + 2)
                    low_of(b * NW + w, w, 3)
                    if prev == 2 and w > 0:
                        scatter(0, par, w - 1, range(K0 // 2, K0))
                    if w == 1 and prev:
                        rstd_of_y(b)
                    for k in range(done, done + (2 if w >= 2 * NW - CPB else 1)):
                        pool.wait_ge(hi_done, CPB * b + k + 1)
                        at = (b * CPB + k) * CH
                        pool.tensor_tensor(w_lo[:, bass.ds(at, CH)], w_raw[:, (par * CPB + k) % 2, :],
                                           w_hi[:, bass.ds(at, CH)], ALU.subtract).then_inc(lo_done, 1)
                        done = k + 1

            def rstd_of_y(count):
                pool.wait_ge(var2_ready, count)
                pool.tensor_tensor(rstd2[:, :], ve2[:, :], nhalf, ALU.pow).then_inc(rstd2_ready, 1)

            def scatter(n, par, t, ks):
                for k in ks:
                    at = t * top[n] + k
                    pool.indirect_dma_start(
                        out=xs[n][:, :], out_offset=bass.IndirectOffsetOnAxis(sidx[:, par, at:at + 1], 0),
                        in_=x1w[:, par, t, :], in_offset=None).then_inc((scattered, scattered1)[n][par], 16)

            def send(n, b, par):
                pool.wait_ge(slots_ready[n], b + 1)
                apart(pool)
                for t in range(T):
                    scatter(n, par, t, range(top[n]))

            def rstd_of_y3(b):
                pool.wait_ge(var3_ready, b + 1)
                pool.tensor_tensor(rstd3[:, :], ve3[:, :], nhalf, ALU.pow).then_inc(rstd3_ready, 1)

            def gather(n, b, par):
                gather_rows(n, b, par)
                fetch(n, par, 0, T * top[n])

            def gather_rows(n, b, par):
                k_n = top[n]
                apart(pool)
                pool.tensor_copy(gidx[:, par, 0:T * k_n].rearrange("p (t k) -> p t k", t=T),
                                 gres[n][:, bass.ds(b * T, T), :]).then_inc(pool_step, 1)
                pool.wait_ge(pool_step, B * n + b + 1)
                apart(pool)

            def fetch(n, par, lo, hi):
                k_n = top[n]
                for at in range(lo, hi):
                    pool.indirect_dma_start(
                        out=gat[:, par, at // k_n, at % k_n, :], out_offset=None, in_=ys[n][:, :],
                        in_offset=bass.IndirectOffsetOnAxis(gidx[:, par, at:at + 1], 0)).then_inc(gathered[n][par], 16)

            def linear_body(b, i, par, nxt, nxt2):
                if nxt2:
                    pool.wait_ge(comb_done, b + 1)
                    gather_rows(0, b + 2, par)
                    fetch(0, par, 0, 2)
                if nxt:
                    rstd_of_y(B + b + 2)
                if nxt2:
                    fetch(0, par, 2, 4)
                rstd_of_y3(b)
                if nxt2:
                    fetch(0, par, 4, T * K0)
                send(1, b, par)

            def final_body(b, i, par, nxt, nxt2):
                if nxt:
                    pool.wait_ge(comb_done, B + b)
                    gather(1, b + 1, 1 - par)
                rstd_of_y(2 * B + b + 1)

            def store_tiles(n):
                def rows(j):
                    return ys[n][bass.ds(j * TILE, TILE), :].rearrange("(p s) d -> p (s d)", s=S2)

                def tile(j, par, first, last, e_before, e):
                    pool.wait_ge(y_done[n], j + 1)
                    apart(pool)
                    pool.dma_start(rows(j), ysb[:, par, :, :].rearrange("p s d -> p (s d)")).then_inc(y_stored[n][par], 16)
                    pool.sem_inc(slot_settled[n], 16)

                pool.wait_ge(table_kept[n], 1)
                over_tiles(pool, n, tile, use=False)

            def outputs_stored(n):
                more = more_pairs(pool, n)
                for par in range(2):
                    pool.wait_ge(y_stored[n][par], 16 * more + 16)
                pool.wait_ge(slot_settled[n], 16 * (tiles[n] + 2))
                pool.wait_ge(xg_loaded[n][0], 16 * more + 32)
                pool.wait_ge(rows_ready[n], 1)

            rstd_of(0)
            rstd_of(1)
            over_attention(pool, body)
            rstd_of_y(B)
            send(0, B - 2, 0)
            send(0, B - 1, 1)
            store_tiles(0)
            outputs_stored(0)
            apart(pool)
            pool.memset(x2_t[:, 0:1], 0.0).then_inc(init_done, 1)
            gather(0, 0, 0)
            gather_rows(0, 1, 1)
            fetch(0, 1, 0, 8)
            rstd_of_y(B + 1)
            fetch(0, 1, 8, T * K0)
            over_batches(pool, linear_body)
            store_tiles(1)
            outputs_stored(1)
            gather(1, 0, 0)
            over_batches(pool, final_body)

        @block.vector
        def _(dve):
            ch = Chain(dve, dve_step)
            dve.wait_ge(loaded, 16 * LOADS)
            dve.wait_ge(init_done, 1)
            dve.tensor_tensor(keys2[:, :], keys_sb[:, 0, :], keys_sb[:, 0, :], ALU.mult).then_inc(keys_ready, 1)
            dve.scalar_tensor_tensor(out=g_route[:, :], in0=keys_sb[:, 0, :], scalar=2.0, in1=keys_sb[:, 1, :],
                                     op0=ALU.mult, op1=ALU.add)
            dve.wait_ge(routes_ready, 1)
            ch.link(dve.tensor_tensor(c_route[:, :], rb_sb[:, :], rt_lg[:, 0, :], ALU.subtract))

            def stats(src, st, m, v, ready):
                for t in range(T):
                    ins = dve.bn_stats(st[:, t, :], src(t))
                ch.link(ins)
                apart(dve)
                for t in range(T):
                    ins = dve.bn_aggr(m[:, t, :], st[:, t, :])
                ch.link(ins)
                dve.tensor_scalar(v[:, :], m[:, :, 1], EPS, None, ALU.add).then_inc(ready, 1)

            def prep_stats(b):
                stats(lambda t: xres[:, b * T + t, :], stat, mv, ve, var_ready)

            def prep_xhat(b):
                dve.wait_ge(rstd_ready, b + 1)
                dve.wait_ge(xhat_turned, b)
                for t in range(T):
                    ins = dve.tensor_scalar(xh[:, t, :], xres[:, b * T + t, :], mv[:, t, 0:1], rstd[:, t:t + 1],
                                            ALU.subtract, ALU.mult)
                ins.then_inc(xhat_ready, 1)

            def prep_stack(b, par, j):
                dve.wait_ge(half_ready, 2 * G * b + j + 1)
                dst = (qst if j < G else kst)[:, par, j % G, :]
                dve.scalar_tensor_tensor(out=dst, in0=hi16[:, j % 2, :], scalar=neg_low[:, j // G:j // G + 1],
                                         in1=proj[STACK_BANK[j]][:, :], op0=ALU.mult,
                                         op1=ALU.add).then_inc(stack_ready, 1)

            def value_low(b, par):
                for part, (bank, ws) in enumerate(((proj[1], range(0, 4)), (proj[0], range(4, 5)))):
                    dve.wait_ge(v_high, 2 * b + part + 1)
                    for w in ws:
                        at = (w % 4) * P
                        ins = dve.tensor_tensor(v2[:, par, w, :, V1:V1 + HD],
                                                bank[:, at:at + P].rearrange("p (h d) -> p h d", h=H),
                                                v2[:, par, w, :, 0:HD], ALU.subtract)
                    ins.then_inc(v_copied, 1)

            def max_of(win, i):
                dve.wait_ge(s_ready, G * win + i + 1)
                dve.tensor_reduce(nm[:, 4 * i:4 * i + 4], s_bank[i % 2][:, :].rearrange("p (t k) -> p t k", t=4),
                                  AX.X, ALU.max, negate=True).then_inc(max_done, 1)

            def prob_low(win, w, g):
                dve.wait_ge(exp_done, G * win + g + 1)
                width = 4 * NQ[w]
                dve.tensor_tensor(prob_lo[:, g, 0:width], prob[:, g % 2, 0:width], prob_hi[:, g, 0:width],
                                  ALU.subtract).then_inc(low_even, 1)

            def split_max(win):
                dve.wait_ge(nm_ready, win + 1)
                ch.link(dve.tensor_copy(nm_t[0:H, :], nm_ps))
                dve.tensor_tensor(nm_t[32:32 + H, :], nm_ps, nm_t[0:H, :], ALU.subtract).then_inc(nm_split, 1)

            def divide(win, beside=None):
                dve.wait_ge(av_ready, win + 1)
                if beside:
                    beside()
                ch.link(dve.reciprocal(rden[:, :, :], av[:, :, :, HD]))
                dve.wait_ge(ao_turned, win)
                dve.tensor_tensor(ao[:, :].rearrange("p (t i d) -> p i t d", t=4, i=G), av[:, :, :, 0:HD],
                                  bc(rden[:, :, :], 3, HD), ALU.mult).then_inc(ao_ready, 1)

            def take_logits(n, b):
                dve.wait_ge(lg_ready[n], b + 1)
                if n == 0:
                    ch.link(dve.tensor_tensor(lg[:, :, :], lg_ps, bc(c_route[:, :], 1, T), ALU.add))
                else:
                    ch.link(dve.tensor_copy(lg[:, :, 0:E1], rt_lg[:, :, 0:E1]))

            def choose(n):
                k_n = top[n]
                lgv = lg[:, :, 0:experts[n]]
                apart(dve)
                for t in range(T):
                    ins = dve.max(mx8[:, t, :], lgv[:, t, :])
                ch.link(ins)
                apart(dve)
                for t in range(T):
                    ins = dve.max_index(ix8[:, t, :], mx8[:, t, :], lgv[:, t, :])
                ch.link(ins)
                dve.tensor_tensor(dtop[:, :, 0:k_n], mx8[:, :, 0:k_n], mx8[:, :, 0:1].to_broadcast([P, T, k_n]),
                                  ALU.subtract).then_inc(d_ready[n], 1)
                ch.link(dve.tensor_copy(idf[:, :, 0:k_n], ix8[:, :, 0:k_n]))

            def mark(n):
                e_n, k_n = experts[n], top[n]
                mk, oh = mask[:, :, 0:e_n], oneh[:, :, 0:k_n, 0:e_n]
                for k in range(k_n):
                    ins = dve.tensor_tensor(oh[:, :, k, :], bc(iota_e[:, 0:e_n], 1, T),
                                            idf[:, :, k:k + 1].to_broadcast([P, T, e_n]), ALU.is_equal)
                ch.link(ins)
                with nc.allow_low_precision(reason="the sums are 0 or 1"):
                    dve.tensor_reduce(mk, oh.rearrange("p t k e -> p t e k"), AX.X, ALU.add).then_inc(mask_ready[n], 1)

            def take_ranks(n, b, ranks):
                e_n = experts[n]
                dve.wait_ge(rank_ready[n], b + 1)
                dve.tensor_tensor(r2[:, :, 0:e_n], ranks[:, :, 0:e_n], bc(base_e[:, 0:e_n], 1, T),
                                  ALU.add).then_inc(rank_used[n], 1)

            def weigh(n, b):
                e_n, k_n = experts[n], top[n]
                dve.wait_ge(mask_ready[n], b + 1)
                ch.link(dve.tensor_reduce(msum[:, 0:e_n], mask[:, :, 0:e_n].rearrange("p t e -> p e t"), AX.X, ALU.add))
                dve.wait_ge(e_ready[n], b + 1)
                ch.link(dve.tensor_reduce(ssum[:, :], etop[:, :, 0:k_n], AX.X, ALU.add))
                ch.link(dve.reciprocal(rsum[:, :], ssum[:, :]))
                if n == 1:
                    ch.link(dve.tensor_scalar(rsum[:, :], rsum[:, :], DEPTH_SCALE, None, ALU.mult))
                dve.tensor_tensor(wres[:, bass.ds(b * T, T), 0:k_n], etop[:, :, 0:k_n], bc(rsum[:, :], 2, k_n), ALU.mult)

            def place(n, b, par):
                e_n, k_n = experts[n], top[n]
                oh = oneh[:, :, 0:k_n, 0:e_n]
                dve.wait_ge(rank_used[n], b + 1)
                ch.link(dve.tensor_tensor(carry[n][:, :], carry[n][:, :], msum[:, 0:e_n], ALU.add))
                dve.tensor_copy(carry_b[n][:, :], carry[n][:, :]).then_inc(carry_ready[n], 1)
                for k in range(k_n):
                    ins = dve.tensor_tensor(pr[:, :, k, 0:e_n], oh[:, :, k, :], r2[:, :, 0:e_n], ALU.mult)
                ch.link(ins)
                ch.link(dve.tensor_reduce(slf[:, 0:T * k_n].rearrange("p (t k) -> p t k", t=T),
                                          pr[:, :, 0:k_n, 0:e_n], AX.X, ALU.add))
                dve.tensor_copy(sidx[:, par, 0:T * k_n], slf[:, 0:T * k_n]).then_inc(slots_ready[n], 1)
                dve.tensor_copy(eres[n][:, bass.ds(b * T, T), :], idf[:, :, 0:k_n])
                ch.link(dve.tensor_copy(sres[n][:, bass.ds(b * T, T), :],
                                        slf[:, 0:T * k_n].rearrange("p (t k) -> p t k", t=T)))

            def tile_table(n):
                e_n = experts[n]
                dve.wait_ge(cnt_ready[n], 1)
                ch.link(dve.tensor_copy(cnt[:, 0:e_n], xbank[:, 0:e_n]))
                dve.tensor_tensor(tails[0:1, 0:e_n], cnt[0:1, 0:e_n], base_e[0:1, 0:e_n], ALU.add).then_inc(tails_ready[n], 1)
                ch.link(dve.tensor_tensor(over[:, 0:e_n, :], cnt[:, 0:e_n].unsqueeze(2).to_broadcast([P, e_n, E0]),
                                          bc(steps, 1, e_n), ALU.is_gt))
                ch.link(dve.tensor_reduce(ntile[:, 0:e_n], over[:, 0:e_n, :], AX.X, ALU.add))
                ch.link(dve.tensor_tensor_scan(ntile_sum[:, 0:e_n], ones_f[:, 0:e_n], ntile[:, 0:e_n], 0.0, ALU.mult, ALU.add))
                ch.link(dve.tensor_scalar(past[:, 0:e_n], ntile_sum[:, 0:e_n], row_no, None, ALU.is_le))
                ch.link(dve.tensor_tensor(past_n[:, 0:e_n], past[:, 0:e_n], ntile[:, 0:e_n], ALU.mult))
                dve.tensor_reduce(tile_e[:, 0:1], past[:, 0:e_n], AX.X, ALU.add)
                ch.link(dve.tensor_reduce(tile_e[:, 1:2], past_n[:, 0:e_n], AX.X, ALU.add))
                dve.tensor_tensor(tile_e[:, 2:3], row_no, tile_e[:, 1:2], ALU.subtract)
                ch.link(dve.tensor_scalar(tile_e[:, 3:4], tile_e[:, 0:1], e_n - 0.5, None, ALU.is_lt))
                ch.link(dve.tensor_scalar(tile_e[:, 2:3], tile_e[:, 2:3], float(TILE), None, ALU.mult))
                ch.link(dve.scalar_tensor_tensor(out=tile_e[:, 2:3], in0=tile_e[:, 0:1], scalar=float(REGION),
                                                 in1=tile_e[:, 2:3], op0=ALU.mult, op1=ALU.add))
                dve.tensor_tensor(tile_e[:, 4:5], tile_e[:, 0:1], tile_e[:, 3:4], ALU.mult)
                dve.tensor_tensor(tile_e[:, 5:6], tile_e[:, 2:3], tile_e[:, 3:4], ALU.mult).then_inc(table_ready[n], 1)
                ch.link(dve.tensor_tensor(shift[:, 0:e_n], ntile_sum[:, 0:e_n], ntile[:, 0:e_n], ALU.subtract))
                ch.link(dve.tensor_scalar(shift[:, 0:e_n], shift[:, 0:e_n], float(TILE), None, ALU.mult))
                ch.link(dve.tensor_tensor(shift[:, 0:e_n], shift[:, 0:e_n], base_e[:, 0:e_n], ALU.subtract))
                dve.wait_ge(table_turned[n], 1)
                in_pairs = xbank[0:1, 0:P].rearrange("o (p two) -> o p two", two=2)
                dve.tensor_copy(quads[0:1, :, 0:2], in_pairs[:, 0:PAIRS, :])
                dve.tensor_copy(quads[0:1, :, 2:4], in_pairs[:, 1:PAIRS + 1, :])
                dve.tensor_copy(table[0:1, 0:2 * PAIRS + 2], xbank[0:1, P:P + 2 * PAIRS + 2])
                dve.tensor_copy(table[0:1, 2 * PAIRS + 2:2 * PAIRS + 3], xbank[0:1, 2 * P:2 * P + 1]).then_inc(table_kept[n], 1)

            def expert_tiles(n):
                ch = Chain(dve, tile_step[n])

                def lo_of(j, par):
                    dve.wait_ge(xhi_done[n], j + 1)
                    dve.tensor_tensor(xt_lo[:, par, :], xt_bank[:, 0:TILE], xt_hi[:, par, :],
                                      ALU.subtract).then_inc(xlo_done[n], 1)

                def split(j, par, half, src):
                    c = slice(2 * half, 2 * half + 2)
                    ch.link(dve.tensor_copy(h_hi[:, par, c, :], src[:, c, :]))
                    dve.tensor_tensor(h_lo[:, par, c, :], src[:, c, :], h_hi[:, par, c, :],
                                      ALU.subtract).then_inc(split_done[n], 1)

                def take_out(j, par, e):
                    dve.wait_ge(yp_ready[n], j + 1)
                    dve.wait_ge(y_stored[n][par], tile_rounds(j, par))
                    src = y_bank[par][:, 0:S2 * D].rearrange("p (s d) -> p s d", s=S2)
                    dve.tensor_tensor(ysb[:, par, :, :], src, b2_sb[:, bass.ds(e, 1), :].to_broadcast([P, S2, D]),
                                      ALU.add).then_inc(y_done[n], 1)

                def tile(j, par, first, last, e_before, e):
                    if not last:
                        lo_of(j + 1, 1 - par)
                    if n == 0:
                        for half in range(2):
                            dve.wait_ge(act_done[n], 2 * j + half + 1)
                            split(j, par, half, act_out)
                    else:
                        dve.wait_ge(split_done[n], 2 * j)
                        for c in range(NC_H):
                            dve.wait_ge(act_done[n], NC_H * j + c + 1)
                            dve.tensor_tensor(hid[:, c, :], act_out[:, c, :], h_bank[c][:, TILE:2 * TILE],
                                              ALU.mult).then_inc(gated, 1)
                        for half in range(2):
                            c = slice(2 * half, 2 * half + 2)
                            dve.wait_ge(gated_high, 2 * j + half + 1)
                            dve.tensor_tensor(h_lo[:, par, c, :], hid[:, c, :], h_hi[:, par, c, :],
                                              ALU.subtract).then_inc(split_done[n], 1)
                    if n == 0 and not first:
                        take_out(j - 1, 1 - par, e_before)

                dve.wait_ge(table_kept[n], 1)
                lo_of(0, 0)
                last_tile, e = over_tiles(dve, n, tile, ch, 2 if n == 0 else 0, use=n == 0)
                if n == 0:
                    take_out(last_tile, 1, e)
                else:
                    dve.wait_ge(split_done[n], 2 * last_tile + 2)
                    apart(dve)

            def output_rows(n):
                e_n, m = experts[n], NT * top[n]
                sel_e = choice[:, 0:m, 0:e_n]
                ch.link(dve.tensor_tensor(sel_e, bc(iota_e[:, 0:e_n], 1, m),
                                          bc(eres[n][:, :, :].rearrange("p t k -> p (t k)"), 2, e_n), ALU.is_equal))
                ch.link(dve.tensor_tensor(sel_e, sel_e, bc(shift[:, 0:e_n], 1, m), ALU.mult))
                rows = eres[n][:, :, :].rearrange("p t k -> p (t k)")
                ch.link(dve.tensor_reduce(rows, sel_e, AX.X, ALU.add))
                ch.link(dve.tensor_tensor(rows, rows, sres[n][:, :, :].rearrange("p t k -> p (t k)"), ALU.add))
                dve.tensor_copy(gres[n][:, :, :].rearrange("p t k -> p (t k)"), rows).then_inc(rows_ready[n], 1)

            def combine(n, b, count, par, ks):
                k_n = top[n]
                if 0 in ks:
                    ch.link(dve.tensor_copy(wsel[:, :, 0:k_n], wres[:, bass.ds(b * T, T), 0:k_n]))
                    dve.wait_ge(gathered[n][par], 16 * T * k_n * count)
                for k in ks:
                    for t in range(T):
                        before = xres[:, b * T + t, :] if k == 0 else y[:, t, :]
                        ins = dve.scalar_tensor_tensor(out=y[:, t, :], in0=gat[:, par, t, k, :],
                                                       scalar=wsel[:, t, k:k + 1], in1=before,
                                                       op0=ALU.mult, op1=ALU.add)
                    if k < k_n - 1:
                        ch.link(ins)
                    else:
                        ins.then_inc(comb_done, 1)
                        dve.wait_ge(comb_done, B * n + b + 1)

            def y_stats():
                stats(lambda t: y[:, t, :], stat2, mv2, ve2, var2_ready)

            def norm_apply(count, dst, ready):
                dve.wait_ge(rstd2_ready, count)
                for t in range(T):
                    ins = dve.tensor_scalar(dst(t), y[:, t, :], mv2[:, t, 0:1], rstd2[:, t:t + 1],
                                            ALU.subtract, ALU.mult)
                ins.then_inc(ready, 1)

            def norm(count, dst, ready):
                y_stats()
                norm_apply(count, dst, ready)

            def x2_apply(b):
                norm_apply(B + b + 1, lambda t: x2w[:, t, :], x2_ready)

            def linear_body(b, i, par, nxt, nxt2):
                def more(ks):
                    if nxt:
                        combine(0, b + 1, i + par + 1, 1 - par, ks)
                for e in range(T):
                    if e == 2:
                        more((0, 1))
                    dve.wait_ge(ws_ready, T * b + e + 1)
                    dve.tensor_tensor(pm[:, e, 0:L - e * P], ws_bank[e % 2][:, 0:L - e * P],
                                      decay_m[:, 0:L - e * P], ALU.mult).then_inc(decayed, 1)
                more((2, 3))
                if nxt:
                    y_stats()
                dve.wait_ge(reads_ready, b + 1)
                dve.scalar_tensor_tensor(out=y3[:, :, :].rearrange("p t d -> p (t d)"),
                                         in0=x2w[:, :, :].rearrange("p t d -> p (t d)"), scalar=2.0,
                                         in1=r_bank[:, :], op0=ALU.mult, op1=ALU.add).then_inc(y3_ready, 1)
                dve.wait_ge(y3_ready, b + 1)
                stats(lambda t: y3[:, t, :], stat3, mv3, ve3, var3_ready)
                if nxt:
                    x2_apply(b + 1)
                dve.wait_ge(scattered1[par], 16 * T * K1 * i)
                dve.wait_ge(rstd3_ready, b + 1)
                for t in range(T):
                    ins = dve.tensor_scalar(x1w[:, par, t, :], y3[:, t, :], mv3[:, t, 0:1], rstd3[:, t:t + 1],
                                            ALU.subtract, ALU.mult)
                ins.then_inc(x1_ready, 1)
                take_logits(1, b)
                choose(1)
                mark(1)
                weigh(1, b)
                take_ranks(1, b, rank_ps)
                place(1, b, par)

            def final_body(b, i, par, nxt, nxt2):
                combine(1, b, i + 1, par, range(K1))
                dve.wait_ge(o_stored[par], 16 * i)
                norm(2 * B + b + 1, lambda t: ow[:, par, t, :], out_ready)

            def residual(b):
                dve.wait_ge(o_ready, b + 1)
                dve.scalar_tensor_tensor(out=y[:, :, :].rearrange("p t d -> p (t d)"),
                                         in0=xres[:, bass.ds(b * T, T), :].rearrange("p t d -> p (t d)"), scalar=2.0,
                                         in1=proj[0][:, :], op0=ALU.mult, op1=ALU.add).then_inc(y_ready, 1)

            def residual_stats(b):
                dve.wait_ge(y_ready, b + 1)
                y_stats()

            def normalise(b, i, par, kept=True):
                if kept:
                    dve.wait_ge(x1_kept, b - 1)
                dve.wait_ge(scattered[par], 16 * T * K0 * i)
                norm_apply(b + 1, lambda t: x1w[:, par, t, :], x1_ready)

            def body(b, i, par, prev, nxt, nxt2):
                for w in range(NW):
                    win = b * NW + w
                    before, after = w > 0 or prev, w < NW - 1 or nxt
                    split_max(win)
                    if after:
                        max_of(win + 1, 0)
                    if after:
                        max_of(win + 1, 1)
                    if w in (2, 3) and nxt:
                        prep_stack(b + 1, 1 - par, 3 * w - 3)
                    if before:
                        beside = None
                        if w == 3 and prev:
                            beside = lambda: take_logits(0, b - 1)
                        if w == 0 and prev == 2:
                            beside = lambda: take_ranks(0, b - 2, rk_ps)
                        divide(win - 1, beside)
                    if w == 2 and prev:
                        normalise(b - 1, i - 1 + par, 1 - par, prev == 2)
                    if w == 1 and prev:
                        residual(b - 1)
                    if w == 4 and prev:
                        choose(0)
                    if w == 0 and prev == 2:
                        weigh(0, b - 2)
                        place(0, b - 2, par)
                    if after:
                        max_of(win + 1, 2)
                    prob_low(win, w, 0)
                    if after:
                        max_of(win + 1, 3)
                    if w in (0, 1, 3) and nxt:
                        prep_stack(b + 1, 1 - par, (0, 1, None, 7)[w])
                    prob_low(win, w, 2)
                    if w == 1 and prev:
                        residual_stats(b - 1)
                    if w == 1 and nxt:
                        prep_stack(b + 1, 1 - par, 2)
                    if w == 2:
                        if nxt:
                            prep_stack(b + 1, 1 - par, 4)
                            prep_stack(b + 1, 1 - par, 5)
                        if nxt2:
                            prep_stats(b + 2)
                    if w == 3:
                        if nxt:
                            value_low(b + 1, 1 - par)
                    if w == 4:
                        if nxt2:
                            prep_xhat(b + 2)
                        if prev:
                            mark(0)

            prep_stats(0)
            prep_xhat(0)
            for j in range(2 * G):
                prep_stack(0, 0, j)
                if j == 1:
                    dve.wait_ge(loaded_later, 16 * LOADS_LATER)
                    prep_stats(1)
                if j == 5:
                    prep_xhat(1)
            max_of(0, 0)
            max_of(0, 1)
            value_low(0, 0)
            max_of(0, 2)
            max_of(0, 3)

            def counted(body, steps):
                start = ch.base + ch.n

                def one(b, i, par, nxt, nxt2):
                    if nxt:
                        ch.base, ch.n = start + steps * b, 0
                    body(b, i, par, nxt, nxt2)
                    assert not nxt2 or ch.n == steps, ch.n
                return one

            over_attention(dve, body, ch, DVE_STEPS)
            divide(B * NW - 1, lambda: take_ranks(0, B - 2, rk_ps))
            weigh(0, B - 2)
            place(0, B - 2, 0)
            residual(B - 1)
            residual_stats(B - 1)
            normalise(B - 1, B // 2 - 1, 1)
            take_logits(0, B - 1)
            choose(0)
            mark(0)
            weigh(0, B - 1)
            take_ranks(0, B - 1, rk_ps)
            place(0, B - 1, 1)
            tile_table(0)
            output_rows(0)
            expert_tiles(0)
            dve.wait_ge(expd_ready, 1)
            dve.tensor_tensor(decay_m[:, :], decay_m[:, :], causal, ALU.mult).then_inc(decay_ready, 1)
            dve.wait_ge(decay_ready, 1)
            dve.wait_ge(x1_kept, B)
            combine(0, 0, 1, 0, range(K0))
            y_stats()
            x2_apply(0)
            over_batches(dve, counted(linear_body, DVE_STEPS_1))
            tile_table(1)
            output_rows(1)
            expert_tiles(1)
            dve.wait_ge(x1_kept, 2 * B)
            over_batches(dve, counted(final_body, DVE_STEPS_2))

        @block.scalar
        def _(act):
            for dst, src in [(wqs[:, :], wq_s), (wks[:, :], wk_s), (cb[:, :], const_b), (wv[:, :], wv_t)]:
                act.dma_start(dst, src).then_inc(loaded_act, 16)
            act.wait_ge(loaded, 16 * LOADS)

            def prep(b):
                act.wait_ge(xhat_turned, b + 1)
                nc.scalar.activation(xn_t[:, :], proj[0][:, :], ACT.Identity, bias=gb[:, 1:2],
                                     scale=gb[:, 0:1]).then_inc(xn_ready, 1)

            def half(b, j):
                act.wait_ge(proj_ready, 2 * G * b + j + 1)
                nc.scalar.copy(hi16[:, j % 2, :], proj[STACK_BANK[j]][:, :]).then_inc(half_ready, 1)

            def values(b, par):
                act.wait_ge(v_ready, 2 * b + 1)
                for w in range(4):
                    ins = nc.scalar.copy(v2[:, par, w, :, 0:HD],
                                         proj[1][:, w * P:w * P + P].rearrange("p (h d) -> p h d", h=H))
                ins.then_inc(v_high, 1)
                act.wait_ge(v_ready, 2 * b + 2)
                nc.scalar.copy(v2[:, par, 4, :, 0:HD],
                               proj[0][:, 0:P].rearrange("p (h d) -> p h d", h=H)).then_inc(v_high, 1)

            def keep_turned(win, w):
                lo, hi = QLO[w], QLO[w + 1]
                act.wait_ge(ao_turned, win + 1)
                nc.scalar.copy(ao_t[:, lo:hi], ao_ps[:, 0:NQ[w]]).then_inc(ao_copied, 1)

            def probs(win, w, g):
                act.wait_ge(st_ready, G * win + g + 1)
                if g >= 2:
                    act.wait_ge((low_even, low_odd)[g % 2], 2 * win + 1)
                width = 4 * NQ[w]
                nc.scalar.activation(prob[:, g % 2, 0:width], t_bank[g % 2][:, 0:width], ACT.Exp, scale=SCALE)
                nc.scalar.activation(prob_hi[:, g, 0:width], t_bank[g % 2][:, 0:width], ACT.Exp,
                                     scale=SCALE).then_inc(exp_done, 1)

            def keep(b, par):
                nc.scalar.copy(xres[:, bass.ds(b * T, T), :],
                               x1w[:, par, :, :]).then_inc(x1_kept, 1)

            def copy_x1(b):
                act.wait_ge(x1_turned, b + 1)
                nc.scalar.copy(x1_t, proj[0][:, :]).then_inc(x1_copied, 1)

            def body(b, i, par, prev, nxt, nxt2):
                done = 0
                for w in range(NW):
                    win = b * NW + w
                    if w == 0 and nxt:
                        prep(b + 1)
                    if w in (2, 3) and nxt:
                        half(b + 1, 3 * w - 3)
                    probs(win, w, 0)
                    probs(win, w, 1)
                    if w > 0 or prev:
                        keep_turned(win - 1, (w - 1) % NW)
                    if w in (0, 1, 3) and nxt:
                        half(b + 1, (0, 1, None, 7)[w])
                    if w == 2 and prev:
                        copy_x1(b - 1)
                    probs(win, w, 2)
                    probs(win, w, 3)
                    if w == 4 and prev:
                        route(0, b - 1)
                        keep(b - 1, 1 - par)
                    if w == 1 and nxt:
                        half(b + 1, 2)
                    if w == 2 and nxt:
                        half(b + 1, 4)
                        half(b + 1, 5)
                    if w == 3 and nxt:
                        values(b + 1, 1 - par)
                    for k in range(done, done + (2 if w >= 2 * NW - CPB else 1)):
                        act.wait_ge(raw_in[(par * CPB + k) % 2], 16 * (CPB * i + (par * CPB + k) // 2 + 1))
                        nc.scalar.copy(w_hi[:, bass.ds((b * CPB + k) * CH, CH)],
                                       w_raw[:, (par * CPB + k) % 2, :]).then_inc(hi_done, 1)
                        done = k + 1

            def route(n, b):
                act.wait_ge(d_ready[n], b + 1)
                nc.scalar.activation(etop[:, :, 0:top[n]], dtop[:, :, 0:top[n]], ACT.Exp).then_inc(e_ready[n], 1)

            def expert_tiles(n):
                def hi_of(j, par):
                    act.wait_ge(g_turned[n], j + 1)
                    nc.scalar.copy(xt_hi[:, par, :], xt_bank[:, 0:TILE]).then_inc(xhi_done[n], 1)

                def tile(j, par, first, last, e_before, e):
                    if not last:
                        hi_of(j + 1, 1 - par)
                    if n == 0:
                        act.wait_ge(split_done[n], 2 * j)
                    else:
                        act.wait_ge(gated, NC_H * j)
                    for c in range(NC_H):
                        if n == 0:
                            if c % 2 == 0:
                                act.wait_ge(h_ready[n], 2 * j + c // 2 + 1)
                            ins = nc.scalar.activation(
                                act_out[:, c, :], h_bank[2 * par + c // 2][:, (c % 2) * TILE:(c % 2 + 1) * TILE],
                                ACT.Gelu, bias=b1_sb[:, bass.ds(e * NC_H + c, 1)])
                            if c % 2 == 1:
                                ins.then_inc(act_done[n], 1)
                        else:
                            act.wait_ge(h_ready[n], NC_H * j + c + 1)
                            nc.scalar.activation(act_out[:, c, :], h_bank[c][:, 0:TILE],
                                                 ACT.Silu).then_inc(act_done[n], 1)
                    if n == 1:
                        for half in range(2):
                            c = slice(2 * half, 2 * half + 2)
                            act.wait_ge(gated, NC_H * j + 2 * half + 2)
                            nc.scalar.copy(h_hi[:, par, c, :], hid[:, c, :]).then_inc(gated_high, 1)
                        if not first:
                            take_out(j - 1, 1 - par)

                def take_out(j, par):
                    act.wait_ge(yp_ready[n], j + 1)
                    act.wait_ge(y_stored[n][par], tile_rounds(j, par))
                    nc.scalar.copy(ysb[:, par, :, :], y_bank[par][:, 0:S2 * D].rearrange("p (s d) -> p s d", s=S2)
                                   ).then_inc(y_done[n], 1)

                act.wait_ge(table_kept[n], 1)
                hi_of(0, 0)
                last_tile, _ = over_tiles(act, n, tile, use=n == 0)
                if n == 1:
                    take_out(last_tile, 1)

            def keep_x2_turned(b):
                act.wait_ge(x2_turned, b + 1)
                nc.scalar.copy(x2_t[:, 1:L + 1], proj[1][:, :]).then_inc(x2_copied, 1)

            def linear_body(b, i, par, nxt, nxt2):
                act.wait_ge(vv_ready, b + 1)
                nc.scalar.copy(vv[:, :, :].rearrange("p t d -> p (t d)"), v_bank[:, :]).then_inc(vv_copied, 1)
                if nxt:
                    keep_x2_turned(b + 1)
                act.wait_ge(x1_turned, B + b + 1)
                nc.scalar.copy(x1_t, xbank[:, :]).then_inc(x1_copied, 1)
                keep(b, par)
                route(1, b)

            nc.scalar.activation(dexp[:, :], dec[:, 0:1], ACT.Exp, scale=-1.0).then_inc(gamma_ready, 1)
            nc.scalar.activation(alpha[:, :], dec[:, 1:2], ACT.Exp).then_inc(gamma_ready, 1)
            act.wait_ge(gamma_ready, 2)
            nc.scalar.activation(dlog[:, :], dexp[:, :], ACT.Ln, bias=1.0).then_inc(dlog_ready, 1)
            act.wait_ge(wc_ready, 1)
            nc.scalar.activation(wc[:, :], avbank[:, 0:D], ACT.Identity, scale=alpha[:, 0:1])
            act.wait_ge(init_done, 1)
            prep(0)
            for j in range(2 * G):
                half(0, j)
            values(0, 0)
            over_attention(act, body)
            keep_turned(B * NW - 1, NW - 1)
            copy_x1(B - 1)
            route(0, B - 1)
            keep(B - 1, 1)
            expert_tiles(0)
            act.wait_ge(dlog_ready, 1)
            act.wait_ge(init_done, 2)
            act.wait_ge(loaded_later, 16 * LOADS_LATER)
            nc.scalar.activation(decay_m[:, :], nmat, ACT.Exp, scale=dlog[:, 0:1]).then_inc(expd_ready, 1)
            keep_x2_turned(0)
            over_batches(act, linear_body)
            expert_tiles(1)

        @block.tensor
        def _(pe):
            pe.wait_ge(loaded, 16 * LOADS)
            pe.wait_ge(keys_ready, 1)
            pe.wait_ge(init_done, 1)
            pe.matmul(rt_lg[:, 0, :], ones_f[:, :], keys2[:, :], start=True, stop=True).then_inc(routes_ready, 1)
            pe.matmul(avbank[:, 0:D], ww_sb[:, 0, :], ww_sb[:, 1, :], start=True, stop=True).then_inc(wc_ready, 1)

            def turn(b):
                pe.wait_ge(xhat_ready, b + 1)
                for t in range(T):
                    ins = pe.transpose(proj[0][:, t * P:(t + 1) * P], xh[:, t, :], ident)
                ins.then_inc(xhat_turned, 1)

            def stacks(b, j):
                if j >= 1:
                    pe.wait_ge(stack_ready, 2 * G * b + max(j - 1, 1) + (j == 4))
                src = (wqs if j < G else wks)[:, (j % G) * P:(j % G + 1) * P]
                pe.matmul(proj[STACK_BANK[j]][:, :], src, xn_t[:, :], start=True, stop=True).then_inc(proj_ready, 1)

            def values(b):
                pe.wait_ge(stack_ready, 2 * G * b + 7)
                for w in range(4):
                    ins = pe.matmul(proj[1][:, w * P:(w + 1) * P], xn_t[:, WIN[w]:WIN[w] + P], wv[:, :],
                                    start=True, stop=True)
                ins.then_inc(v_ready, 1)
                pe.wait_ge(stack_ready, 2 * G * b + 8)
                pe.matmul(proj[0][:, 0:P], xn_t[:, WIN[4]:WIN[4] + P], wv[:, :], start=True,
                          stop=True).then_inc(v_ready, 1)

            def scores(win, w, par, g, first=False):
                if not first or g >= 2:
                    pe.wait_ge(max_done, G * win + g - 1)
                bank, rows, at = s_bank[g % 2], slice(32 * g, 32 * g + 32), slice(WIN[w], WIN[w] + P)
                pe.matmul(bank[:, :], ident_b, band4, start=True, stop=True)
                for t in range(4):
                    ins = pe.matmul(bank[:, t * P:(t + 1) * P], qst[rows, par, t, at], kst[rows, par, t, at],
                                    start=False, stop=True, skip_group_check=True)
                ins.then_inc(s_ready, 1)

            def scores_t(win, w, par, g):
                if g >= 2:
                    pe.wait_ge(exp_done, G * win + g - 1)
                rows, nq, lo = slice(32 * g, 32 * g + 32), NQ[w], QLO[w]
                bank = t_bank[g % 2][:, 0:4 * nq].rearrange("p (t q) -> p t q", t=4)
                band = band4.rearrange("p (t q) -> p t q", t=4)[:, :, lo - WIN[w]:lo - WIN[w] + nq]
                pe.matmul(bank, ident_b, band, start=True, stop=True)
                for t in range(4):
                    pe.matmul(bank[:, t, :], kst[rows, par, t, WIN[w]:WIN[w] + P], qst[rows, par, t, lo:lo + nq],
                              start=False, stop=False, skip_group_check=True)
                for t in range(4):
                    ins = pe.matmul(bank[:, t, :], sel[:, 4 * g + t, :], nm_t[:, lo - WIN[w]:lo - WIN[w] + nq],
                                    start=False, stop=True, skip_group_check=True)
                ins.then_inc(st_ready, 1)

            def weighted(win, w, par, g):
                if g == 0 and not (w == 0 and type(win) is int and win == 0):
                    pe.wait_ge(ao_ready, win)
                pe.wait_ge((low_even, low_odd)[g % 2], 2 * win + g // 2 + 1)
                for t in range(4):
                    hi, lo = (x[:, g, t * NQ[w]:t * NQ[w] + P] for x in (prob_hi, prob_lo))
                    v = v2[:, par, w, 4 * t + g, :]
                    pe.matmul(av[:, g, t, :], hi, v[:, 0:V1], start=True, stop=True)
                    pe.matmul(av[:, g, t, 0:HD], hi, v[:, V1:V1 + HD], start=False, stop=True, skip_group_check=True)
                    ins = pe.matmul(av[:, g, t, :], lo, v[:, 0:V1], start=False, stop=True, skip_group_check=True)
                if g == G - 1:
                    ins.then_inc(av_ready, 1)

            def turn_out(win):
                pe.wait_ge(ao_ready, win + 1)
                pe.transpose(ao_ps, ao[:, :], ident).then_inc(ao_turned, 1)

            def project_out(b):
                pe.wait_ge(ao_copied, NW * (b + 1))
                for t in range(T):
                    ins = pe.matmul(proj[0][:, t * P:(t + 1) * P], ao_t[:, t * P:(t + 1) * P], wo[:, :],
                                    start=True, stop=True)
                ins.then_inc(o_ready, 1)

            def body(b, i, par, prev, nxt, nxt2):
                for w in range(NW):
                    win = b * NW + w
                    before = w > 0 or prev
                    pe.wait_ge(max_done, G * (win + 1))
                    if not (type(b) is int and win < 2):
                        pe.wait_ge(ao_copied, win - 1)
                    pe.transpose(nm_ps, nm[:, :], ident).then_inc(nm_ready, 1)
                    after = lambda g: None
                    if w < NW - 1:
                        after = lambda g: scores(win + 1, w + 1, par, g)
                    elif nxt:
                        pe.wait_ge(stack_ready, 2 * G * (b + 2))
                        after = lambda g: scores(win + 1, 0, 1 - par, g)
                    after(0)
                    last_of = (win - 1, (w - 1) % NW, par if w > 0 else 1 - par)
                    if before:
                        weighted(*last_of, 2)
                    after(1)
                    if before:
                        weighted(*last_of, 3)
                    if prev and w == 3:
                        logits(0, b - 1, lg_ps)
                    if prev == 2 and w == 0:
                        ranks(0, b - 2, rk_ps)
                    if w == 0 and nxt:
                        pe.wait_ge(v_copied, 2 * (b + 1))
                        turn(b + 1)
                    if w == 1 and prev:
                        if nxt:
                            pe.wait_ge(xn_ready, b + 2)
                        project_out(b - 1)
                    if w in (2, 3) and nxt:
                        stacks(b + 1, 3 * w - 3)
                    pe.wait_ge(nm_split, win + 1)
                    scores_t(win, w, par, 0)
                    after(2)
                    scores_t(win, w, par, 1)
                    after(3)
                    if before:
                        turn_out(win - 1)
                    if w == 0 and nxt:
                        pe.wait_ge(xn_ready, b + 2)
                        stacks(b + 1, 0)
                    if w == 1 and nxt:
                        stacks(b + 1, 1)
                    if w == 2 and prev:
                        if nxt:
                            pe.wait_ge(stack_ready, 2 * G * (b + 1) + 3)
                        turn_x1(b, 1 - par, proj[0])
                    if w == 3 and nxt:
                        stacks(b + 1, 7)
                    scores_t(win, w, par, 2)
                    weighted(win, w, par, 0)
                    scores_t(win, w, par, 3)
                    weighted(win, w, par, 1)
                    if w == 1 and nxt:
                        if prev:
                            pe.wait_ge(y_ready, b)
                        stacks(b + 1, 2)
                    if w == 2 and nxt:
                        stacks(b + 1, 4)
                        if prev:
                            pe.wait_ge(x1_copied, b)
                        stacks(b + 1, 5)
                    if w == 3 and nxt:
                        values(b + 1)

            def turn_x1(count, par, bank):
                pe.wait_ge(x1_ready, count)
                for t in range(T):
                    ins = pe.transpose(bank[:, t * P:(t + 1) * P], x1w[:, par, t, :], ident)
                ins.then_inc(x1_turned, 1)

            def logits(n, b, dst):
                pe.wait_ge(x1_copied, B * n + b + 1)
                for t in range(T):
                    ins = pe.matmul(dst[:, t, 0:experts[n]], x1_t[:, t * P:(t + 1) * P], (g_route, wr_sb)[n][:, :],
                                    start=True, stop=True)
                ins.then_inc(lg_ready[n], 1)

            def ranks(n, b, dst):
                e_n = experts[n]
                pe.wait_ge(mask_ready[n], b + 1)
                if not (type(b) is int and b == 0):
                    pe.wait_ge(carry_ready[n], b)
                dst, mk = dst[:, :, 0:e_n], mask[:, :, 0:e_n]
                pe.matmul(dst, tri, mk, start=True, stop=True)
                for t in range(T - 1):
                    pe.matmul(dst[:, t + 1:T, :], ones_b, bc(mk[:, t, :], 1, T - 1 - t), start=False,
                              stop=True, skip_group_check=True)
                pe.matmul(dst, ones_b, bc(carry_b[n][:, :], 1, T), start=False, stop=True,
                          skip_group_check=True).then_inc(rank_ready[n], 1)

            def tile_table(n):
                pe.wait_ge(carry_ready[n], B)
                pe.wait_ge(rank_used[n], B)
                pe.matmul(xbank[:, 0:experts[n]], ones_b, carry_b[n][:, :], start=True, stop=True).then_inc(cnt_ready[n], 1)
                pe.wait_ge(table_ready[n], 1)
                for c in range(2):
                    pe.transpose(xbank[0:1, c * P:(c + 1) * P], tile_e[:, 4 + c:5 + c], ident)
                ins = pe.matmul(xbank[0:1, 2 * P:2 * P + 1], tile_e[:, 3:4], even, start=True, stop=True)
                ins.then_inc(table_turned[n], 1)
                pe.wait_ge(table_kept[n], 1)

            def expert_tiles(n):
                def turn_rows(j, par):
                    pe.wait_ge(xg_loaded[n][par], 8 * (j - par) + 16)
                    pe.wait_ge(xlo_done[n], j)
                    for k in range(S2):
                        ins = pe.transpose(xt_bank[:, k * P:(k + 1) * P], xg[:, par, k, :], ident)
                    ins.then_inc(g_turned[n], 1)

                def hidden_chunk(dst, w_at, e, c, par):
                    at = e * HID + (w_at + c * P)
                    w_h, w_l = w_hi[:, bass.ds(at, P)], w_lo[:, bass.ds(at, P)]
                    pe.matmul(dst, w_h, xt_hi[:, par, :], start=True, stop=False)
                    pe.matmul(dst, w_h, xt_lo[:, par, :], start=False, stop=False)
                    return pe.matmul(dst, w_l, xt_hi[:, par, :], start=False, stop=True)

                def outputs(j, par, e):
                    pe.wait_ge(y_done[n], j)
                    for half in range(2):
                        pe.wait_ge(split_done[n], 2 * j + half + 1)
                        for k in range(S2):
                            dst, rows = y_bank[par][:, k * D:(k + 1) * D], slice(k * P, (k + 1) * P)
                            for c in (2 * half, 2 * half + 1):
                                at = e * HID + ((W2_AT, WD_AT)[n] + c * D)
                                w_h, w_l = w_hi[:, bass.ds(at, D)], w_lo[:, bass.ds(at, D)]
                                for m, (x, w) in enumerate(((h_hi, w_h), (h_hi, w_l), (h_lo, w_h))):
                                    ins = pe.matmul(dst, x[:, par, c, rows], w, start=(c == 0 and m == 0 and k == 0),
                                                    stop=True, skip_group_check=True)
                    ins.then_inc(yp_ready[n], 1)

                def hidden(j, par, e):
                    pe.wait_ge(xlo_done[n], j + 1)
                    for c in range(NC_H):
                        if n == 0:
                            ins = hidden_chunk(h_bank[2 * par + c // 2][:, (c % 2) * TILE:(c % 2 + 1) * TILE], W1_AT, e, c, par)
                            if c % 2 == 1:
                                ins.then_inc(h_ready[n], 1)
                        else:
                            if not (type(j) is int and j == 0):
                                pe.wait_ge(gated, NC_H * j - NC_H + c + 1)
                            hidden_chunk(h_bank[c][:, 0:TILE], WG_AT, e, c, par)
                            hidden_chunk(h_bank[c][:, TILE:2 * TILE], WU_AT, e, c, par).then_inc(h_ready[n], 1)

                more = more_pairs(pe, n)
                e0, e1 = experts_of(pe, n, 0, 2)
                turn_rows(0, 0)
                turn_rows(1, 1)
                hidden(0, 0, e0)
                turn_rows(2, 0)
                hidden(1, 1, e1)
                with pe.Fori(0, more) as p:
                    e0, e1, e2, e3 = experts_of(pe, n, p, 4)
                    outputs(2 * p, 0, e0)
                    turn_rows(2 * p + 3, 1)
                    hidden(2 * p + 2, 0, e2)
                    outputs(2 * p + 1, 1, e1)
                    turn_rows(2 * p + 4, 0)
                    hidden(2 * p + 3, 1, e3)
                e0, e1 = experts_of(pe, n, more, 2)
                outputs(2 * more, 0, e0)
                outputs(2 * more + 1, 1, e1)

            def turn_x2(b):
                pe.wait_ge(x2_ready, b + 1)
                for t in range(T):
                    ins = pe.transpose(proj[1][:, t * P:(t + 1) * P], x2w[:, t, :], ident)
                ins.then_inc(x2_turned, 1)

            def linear_body(b, i, par, nxt, nxt2):
                pe.wait_ge(x2_copied, b + 1)
                for e in range(T):
                    if e == 2:
                        for t in range(T):
                            ins = pe.matmul(v_bank[:, t * D:(t + 1) * D], x2_t[:, 1 + t * P:1 + (t + 1) * P], wc[:, :],
                                            start=True, stop=True)
                        ins.then_inc(vv_ready, 1)
                    if e >= 2:
                        pe.wait_ge(decayed, T * b + e - 1)
                    pe.matmul(ws_bank[e % 2][:, 0:L - e * P], x2_t[:, e * P:(e + 1) * P], x2_t[:, 1 + e * P:1 + L],
                              start=True, stop=True).then_inc(ws_ready, 1)
                pe.wait_ge(vv_copied, b + 1)
                for c in range(T):
                    pe.wait_ge(decayed, T * b + c + 1)
                    for e in range(c + 1):
                        ins = pe.matmul(r_bank[:, c * P:(c + 1) * P], pm[:, e, (c - e) * P:(c - e + 1) * P],
                                        vv[:, e, :], start=e == 0, stop=e == c)
                ins.then_inc(reads_ready, 1)
                if nxt:
                    turn_x2(b + 1)
                pe.wait_ge(rank_used[1], b)
                turn_x1(B + b + 1, par, xbank)
                logits(1, b, rt_lg)
                ranks(1, b, rank_ps)

            turn(0)
            pe.wait_ge(xn_ready, 1)
            pe.wait_ge(loaded_act, 16 * LOADS_ACT)
            for j in range(2 * G):
                stacks(0, j)
            values(0)
            for g in range(G):
                scores(0, 0, 0, g, first=True)
            pe.wait_ge(loaded_later, 16 * LOADS_LATER)
            over_attention(pe, body)
            last_of = (B * NW - 1, NW - 1, 1)
            weighted(*last_of, 2)
            weighted(*last_of, 3)
            ranks(0, B - 2, rk_ps)
            turn_out(B * NW - 1)
            project_out(B - 1)
            turn_x1(B, 1, proj[0])
            logits(0, B - 1, lg_ps)
            ranks(0, B - 1, rk_ps)
            tile_table(0)
            expert_tiles(0)
            turn_x2(0)
            over_batches(pe, linear_body)
            tile_table(1)
            expert_tiles(1)


def constants():
    import numpy as np

    row = np.arange(P)
    cf = np.zeros((P, C_COLS), np.float32)
    cf[:, C_IDENT:C_IDENT + P] = np.eye(P)
    part = row % 32 // HD
    cf[:, C_NEG] = -1.0 * (part >= 2)
    cf[:, C_NEG + 1] = -1.0 * (part % 2)
    cf[:, C_IOTA:C_IOTA + E0] = np.arange(E0)
    cf[:, C_BASE:C_BASE + E0] = REGION * np.arange(E0)
    cf[:, C_NHALF:C_NHALF + T] = -0.5
    cf[:, C_ROW] = row
    lag = np.arange(L)[None, :] - 1 - row[:, None]
    cf[:, C_NMAT:C_NMAT + L] = -np.maximum(lag, 0)
    cf[:, C_CAUSAL:C_CAUSAL + L] = lag >= 0
    cf[:, C_EVEN] = (row % 2 == 0) & (row > 0)
    cf[:, C_STEP:C_STEP + E0] = TILE * np.arange(E0)
    cb = np.zeros((P, CB_COLS), np.float32)
    cb[:, CB_IDENT:CB_IDENT + P] = np.eye(P)
    cb[:, CB_TRI:CB_TRI + P] = row[:, None] < row[None, :]
    cb[:, CB_ONES:CB_ONES + P] = 1
    cb[:, CB_BAND:CB_BAND + 4 * P] = np.tile(np.where(abs(row[:, None] - row[None, :]) <= HALF, 0, NEG), 4)
    s = np.zeros((P, H, P), np.float32)
    for c in range(H):
        s[c, c] = s[32 + c, c] = 1
    cb[:, CB_SEL:] = s.reshape(P, H * P)
    return cf, cb.astype(mybir.dt.np(BF16))


def kernel(**inputs):
    import numpy as np
    import concourse.bacc as bacc
    from concourse.bass_utils import run_bass_kernel_spmd

    a = {k: np.asarray(v) for k, v in inputs.items()}
    wqkv = a["L0_attn_w_qkv"]

    def stacked(w):
        w = w.reshape(4, G, 1, HD, D)
        return np.broadcast_to(w, (4, G, 4, HD, D)).reshape(512, D).T

    w1 = a["L0_ffn_w1"].transpose(2, 0, 1).reshape(D, E0 * HID)
    w2 = a["L0_ffn_w2"].reshape(E0, D, NC_H, P).transpose(3, 0, 2, 1).reshape(P, E0 * HID)
    wg = a["L1_ffn_Wg"].transpose(1, 0, 2).reshape(D, E1 * HID)
    wu = a["L1_ffn_Wu"].transpose(1, 0, 2).reshape(D, E1 * HID)
    wd = a["L1_ffn_Wd"].reshape(E1, NC_H, P, D).transpose(2, 0, 1, 3).reshape(P, E1 * HID)
    cf, cb = constants()
    arrays = {
        "x_in": a["L0_attn_x"],
        "w_all": np.concatenate([w1, w2, wg, wu, wd], 1),
        "wq_s": stacked(wqkv[:D]),
        "wk_s": stacked(wqkv[D:2 * D]),
        "wv_t": wqkv[2 * D:].T,
        "wo_t": a["L0_attn_w_out"].T,
        "gamma": a["L0_attn_gamma"].reshape(D, 1),
        "beta": a["L0_attn_beta"].reshape(D, 1),
        "keys_t": a["L0_ffn_keys"].T,
        "rw_t": a["L0_ffn_rw"].T,
        "rb": a["L0_ffn_rb"].reshape(1, E0),
        "b1": a["L0_ffn_b1"].reshape(E0, NC_H, P).transpose(2, 0, 1).reshape(P, E0 * NC_H),
        "b2": a["L0_ffn_b2"].reshape(1, E0 * D),
        "w_write": a["L1_attn_W_write"],
        "w_read_t": a["L1_attn_W_read"].T,
        "decay": a["L1_attn_decay"].reshape(1, 1),
        "log_alpha": a["L1_attn_log_alpha"].reshape(1, 1),
        "wr": a["L1_ffn_Wr"],
        "const": cf,
        "const_b": cb,
    }
    arrays = {k: np.ascontiguousarray(v) for k, v in arrays.items()}
    nc = bacc.Bacc("TRN2", target_bir_lowering=False, num_devices=1)
    args = [nc.dram_tensor(k, v.shape, mybir.dt.from_np(v.dtype), kind="ExternalInput").ap()
            for k, v in arrays.items()]
    out = nc.dram_tensor("out", (B, L, D), F32, kind="ExternalOutput").ap()
    program(nc, *args, out)
    return run_bass_kernel_spmd(nc, [arrays], core_ids=[0]).results[0]["out"]
```
